# Optimizing a Trainium2 kernel written in Bass

```python
import numpy as np
import jax
import jax.numpy as jnp

def _softmax(x, axis=-1):
    return jax.nn.softmax(x, axis=axis)

def _gelu(x):
    return jax.nn.gelu(x, approximate=True)

def _silu(x):
    return jax.nn.silu(x)

def _sigmoid(x):
    return jax.nn.sigmoid(x)

def _layernorm(x, axis=-1, eps=1e-05):
    m = jnp.mean(x, axis=axis, keepdims=True)
    v = jnp.var(x, axis=axis, keepdims=True)
    return (x - m) / jnp.sqrt(v + eps)

def _scatter_add(tgt, idx, src, axis=0):
    return tgt.at[idx].add(src)

def _segment_sum(src, seg, n):
    return jax.ops.segment_sum(src, seg, n)
kernel_name = 'mk_lm_tower_d1_tok_ids512_r4_189e75'

def setup_inputs(seed: int=0):
    np.random.seed(seed)
    _w = jnp.asarray

    def _rec_inputs():
        import jax
        import jax.numpy as jnp
        _rk = jax.random.key(seed)
        x = jax.random.randint(jax.random.fold_in(_rk, 1), (128, 128), 0, 12500, jnp.int32)
        return x
    x = _rec_inputs()

    def _L0_tok_setup():
        import jax, jax.numpy as jnp
        import numpy as np
        VOCAB = 12500
        DIM = 128
        NUM_NUM = 250
        key = jax.random.key(seed)
        k1, k2 = jax.random.split(key)
        x = jax.random.randint(k1, (8, 1024), 0, VOCAB, dtype=jnp.int32)
        weight = jax.random.normal(k2, (VOCAB, DIM), dtype=jnp.float32) * 0.1
        ids = jnp.arange(VOCAB)
        is_num = ids < NUM_NUM
        num_value = jnp.where(is_num, ids, 0).astype(jnp.int32)
        return {'x': x, 'weight': weight, 'num_value': num_value, 'is_num': is_num}
    _L0_tok_all = _L0_tok_setup()
    _L0_tok_in = {k: v for k, v in _L0_tok_all.items() if k in ('weight', 'num_value', 'is_num')}
    del _L0_tok_all

    def _L0_attn_setup():
        import jax, jax.numpy as jnp
        import numpy as np
        B, N, DIM = (16, 256, 128)
        H, DH = (8, 64)
        MASK_VAL = -1e-09
        key = jax.random.key(seed)
        ks = jax.random.split(key, 8)
        w = 0.02
        x = jax.random.normal(ks[0], (B, N, DIM), dtype=jnp.float32)
        Wq = jax.random.normal(ks[1], (DIM, H * DH), dtype=jnp.float32) * w
        Wkv = jax.random.normal(ks[2], (DIM, 2 * H * DH), dtype=jnp.float32) * w
        scale = jnp.full((H,), DH ** (-0.5), dtype=jnp.float32)
        mix_pre = jax.random.normal(ks[3], (H, H), dtype=jnp.float32) * w
        mix_post = jax.random.normal(ks[4], (H, H), dtype=jnp.float32) * w
        Wout = jax.random.normal(ks[5], (H * DH, DIM), dtype=jnp.float32) * w
        bout = jnp.zeros((DIM,), dtype=jnp.float32)
        return {'x': x, 'Wq': Wq, 'Wkv': Wkv, 'scale': scale, 'mix_pre': mix_pre, 'mix_post': mix_post, 'Wout': Wout, 'bout': bout}
    _L0_attn_all = _L0_attn_setup()
    _L0_attn_in = {k: v for k, v in _L0_attn_all.items() if k in ('Wq', 'Wkv', 'scale', 'mix_pre', 'mix_post', 'Wout', 'bout')}
    del _L0_attn_all

    def _L0_ffn_setup():
        import math
        import jax, jax.numpy as jnp
        import numpy as np
        B, T, D, FF, E = (32, 256, 128, 512, 8)
        CAPACITY_FACTOR = 1.25
        CAP = int(math.ceil(CAPACITY_FACTOR * B * T / E))

        def _bank_residual(x2, Wr, br, W1, b1, W2, b2):
            N, d = x2.shape
            e = Wr.shape[1]
            logits = x2 @ Wr + br
            probs = jax.nn.softmax(logits, axis=-1)
            expert = jnp.argmax(probs, axis=-1)
            gate = jnp.take_along_axis(probs, expert[:, None], axis=-1)[:, 0]
            oneh = jax.nn.one_hot(expert, e, dtype=x2.dtype)
            pos = (jnp.cumsum(oneh, axis=0) * oneh).sum(-1).astype(jnp.int32) - 1
            keep = pos < CAP
            slot = expert.astype(jnp.int32) * CAP + jnp.minimum(pos, CAP - 1)
            xd = jnp.where(keep[:, None], x2, 0.0)
            buf = jnp.zeros((e * CAP, d), x2.dtype).at[slot].add(xd)
            buf = buf.reshape(e, CAP, d)
            h = jax.nn.gelu(jnp.einsum('ecd,edf->ecf', buf, W1) + b1[:, None, :], approximate=False)
            out = jnp.einsum('ecf,efd->ecd', h, W2) + b2[:, None, :]
            y = out.reshape(e * CAP, d)[slot]
            return y * (gate * keep.astype(x2.dtype))[:, None]
        key = jax.random.key(seed)
        ks = jax.random.split(key, 18)
        s = 0.02
        inp = {'x': jax.random.normal(ks[0], (B, T, D), dtype=jnp.float32), 'Wr_sp': jax.random.normal(ks[1], (D, E)) * s, 'br_sp': jnp.zeros((E,), jnp.float32), 'Wr_fq': jax.random.normal(ks[2], (D, E)) * s, 'br_fq': jnp.zeros((E,), jnp.float32), 'Ws1': jax.random.normal(ks[3], (D, FF)) * s, 'bs1': jnp.zeros((FF,), jnp.float32), 'Ws2': jax.random.normal(ks[4], (FF, D)) * s, 'bs2': jnp.zeros((D,), jnp.float32), 'W1_sp': jax.random.normal(ks[5], (E, D, FF)) * s, 'b1_sp': jnp.zeros((E, FF), jnp.float32), 'W2_sp': jax.random.normal(ks[6], (E, FF, D)) * s, 'b2_sp': jnp.zeros((E, D), jnp.float32), 'W1_fq': jax.random.normal(ks[7], (E, D, FF)) * s, 'b1_fq': jnp.zeros((E, FF), jnp.float32), 'W2_fq': jax.random.normal(ks[8], (E, FF, D)) * s, 'b2_fq': jnp.zeros((E, D), jnp.float32)}
        return inp
    _L0_ffn_all = _L0_ffn_setup()
    _L0_ffn_in = {k: v for k, v in _L0_ffn_all.items() if k in ('Wr_sp', 'br_sp', 'Wr_fq', 'br_fq', 'Ws1', 'bs1', 'Ws2', 'bs2', 'W1_sp', 'b1_sp', 'W2_sp', 'b2_sp', 'W1_fq', 'b1_fq', 'W2_fq', 'b2_fq')}
    del _L0_ffn_all
    return {'x': x, 'L0_tok_weight': _L0_tok_in['weight'], 'L0_tok_num_value': _L0_tok_in['num_value'], 'L0_tok_is_num': _L0_tok_in['is_num'], 'L0_attn_Wq': _L0_attn_in['Wq'], 'L0_attn_Wkv': _L0_attn_in['Wkv'], 'L0_attn_scale': _L0_attn_in['scale'], 'L0_attn_mix_pre': _L0_attn_in['mix_pre'], 'L0_attn_mix_post': _L0_attn_in['mix_post'], 'L0_attn_Wout': _L0_attn_in['Wout'], 'L0_attn_bout': _L0_attn_in['bout'], 'L0_ffn_Wr_sp': _L0_ffn_in['Wr_sp'], 'L0_ffn_br_sp': _L0_ffn_in['br_sp'], 'L0_ffn_Wr_fq': _L0_ffn_in['Wr_fq'], 'L0_ffn_br_fq': _L0_ffn_in['br_fq'], 'L0_ffn_Ws1': _L0_ffn_in['Ws1'], 'L0_ffn_bs1': _L0_ffn_in['bs1'], 'L0_ffn_Ws2': _L0_ffn_in['Ws2'], 'L0_ffn_bs2': _L0_ffn_in['bs2'], 'L0_ffn_W1_sp': _L0_ffn_in['W1_sp'], 'L0_ffn_b1_sp': _L0_ffn_in['b1_sp'], 'L0_ffn_W2_sp': _L0_ffn_in['W2_sp'], 'L0_ffn_b2_sp': _L0_ffn_in['b2_sp'], 'L0_ffn_W1_fq': _L0_ffn_in['W1_fq'], 'L0_ffn_b1_fq': _L0_ffn_in['b1_fq'], 'L0_ffn_W2_fq': _L0_ffn_in['W2_fq'], 'L0_ffn_b2_fq': _L0_ffn_in['b2_fq']}

def reference(x, L0_tok_weight, L0_tok_num_value, L0_tok_is_num, L0_attn_Wq, L0_attn_Wkv, L0_attn_scale, L0_attn_mix_pre, L0_attn_mix_post, L0_attn_Wout, L0_attn_bout, L0_ffn_Wr_sp, L0_ffn_br_sp, L0_ffn_Wr_fq, L0_ffn_br_fq, L0_ffn_Ws1, L0_ffn_bs1, L0_ffn_Ws2, L0_ffn_bs2, L0_ffn_W1_sp, L0_ffn_b1_sp, L0_ffn_W2_sp, L0_ffn_b2_sp, L0_ffn_W1_fq, L0_ffn_b1_fq, L0_ffn_W2_fq, L0_ffn_b2_fq):
    import jax
    import jax.numpy as jnp

    def _L0_tok_ref(x, weight, num_value, is_num):
        import jax, jax.numpy as jnp
        import numpy as np
        VOCAB = 12500
        DIM = 128
        NUM_NUM = 250
        dim = weight.shape[1]
        freqs = jnp.arange(1, dim + 1, dtype=jnp.float32)
        scaled = num_value.astype(jnp.float32) / 1000.0
        sin_table = jnp.sin(scaled[:, None] * freqs[None, :])
        table = jnp.where(is_num[:, None], sin_table, weight)
        return table[x]

    def _L0_attn_ref(x, Wq, Wkv, scale, mix_pre, mix_post, Wout, bout):
        import jax, jax.numpy as jnp
        import numpy as np
        B, N, DIM = (16, 256, 128)
        H, DH = (8, 64)
        MASK_VAL = -1e-09
        b, n, _ = x.shape
        q = (x @ Wq).reshape(b, n, H, DH).transpose(0, 2, 1, 3)
        kv = (x @ Wkv).reshape(b, n, 2, H, DH)
        k = kv[:, :, 0].transpose(0, 2, 1, 3)
        v = kv[:, :, 1].transpose(0, 2, 1, 3)
        dots = jnp.einsum('bhid,bhjd->bhij', q, k) * scale[None, :, None, None]
        eye = jnp.eye(n, dtype=bool)
        dots = jnp.where(eye, jnp.float32(MASK_VAL), dots)
        dots = jnp.einsum('bhij,hg->bgij', dots, mix_pre)
        attn = jax.nn.softmax(dots, axis=-1)
        attn = jnp.einsum('bhij,hg->bgij', attn, mix_post)
        out = jnp.einsum('bhij,bhjd->bhid', attn, v)
        out = out.transpose(0, 2, 1, 3).reshape(b, n, H * DH)
        return out @ Wout + bout

    def _L0_ffn_ref(x, Wr_sp, br_sp, Wr_fq, br_fq, Ws1, bs1, Ws2, bs2, W1_sp, b1_sp, W2_sp, b2_sp, W1_fq, b1_fq, W2_fq, b2_fq):
        import math
        import jax, jax.numpy as jnp
        import numpy as np
        B, T, D, FF, E = (32, 256, 128, 512, 8)
        CAPACITY_FACTOR = 1.25
        CAP = int(math.ceil(CAPACITY_FACTOR * B * T / E))

        def _bank_residual(x2, Wr, br, W1, b1, W2, b2):
            N, d = x2.shape
            e = Wr.shape[1]
            logits = x2 @ Wr + br
            probs = jax.nn.softmax(logits, axis=-1)
            expert = jnp.argmax(probs, axis=-1)
            gate = jnp.take_along_axis(probs, expert[:, None], axis=-1)[:, 0]
            oneh = jax.nn.one_hot(expert, e, dtype=x2.dtype)
            pos = (jnp.cumsum(oneh, axis=0) * oneh).sum(-1).astype(jnp.int32) - 1
            keep = pos < CAP
            slot = expert.astype(jnp.int32) * CAP + jnp.minimum(pos, CAP - 1)
            xd = jnp.where(keep[:, None], x2, 0.0)
            buf = jnp.zeros((e * CAP, d), x2.dtype).at[slot].add(xd)
            buf = buf.reshape(e, CAP, d)
            h = jax.nn.gelu(jnp.einsum('ecd,edf->ecf', buf, W1) + b1[:, None, :], approximate=False)
            out = jnp.einsum('ecf,efd->ecd', h, W2) + b2[:, None, :]
            y = out.reshape(e * CAP, d)[slot]
            return y * (gate * keep.astype(x2.dtype))[:, None]
        b, t, d = x.shape
        x2 = x.reshape(b * t, d)
        shared = jax.nn.gelu(x2 @ Ws1 + bs1, approximate=False) @ Ws2 + bs2
        y = shared
        y = y + _bank_residual(x2, Wr_sp, br_sp, W1_sp, b1_sp, W2_sp, b2_sp)
        y = y + _bank_residual(x2, Wr_fq, br_fq, W1_fq, b1_fq, W2_fq, b2_fq)
        return y.reshape(b, t, d)
    h = _L0_tok_ref(x, L0_tok_weight, L0_tok_num_value, L0_tok_is_num)
    h = h + _L0_attn_ref(_layernorm(h, axis=-1), L0_attn_Wq, L0_attn_Wkv, L0_attn_scale, L0_attn_mix_pre, L0_attn_mix_post, L0_attn_Wout, L0_attn_bout)
    h = h + _L0_ffn_ref(_layernorm(h, axis=-1), L0_ffn_Wr_sp, L0_ffn_br_sp, L0_ffn_Wr_fq, L0_ffn_br_fq, L0_ffn_Ws1, L0_ffn_bs1, L0_ffn_Ws2, L0_ffn_bs2, L0_ffn_W1_sp, L0_ffn_b1_sp, L0_ffn_W2_sp, L0_ffn_b2_sp, L0_ffn_W1_fq, L0_ffn_b1_fq, L0_ffn_W2_fq, L0_ffn_b2_fq)
    return h

_drawn_inputs = setup_inputs


def setup_inputs(seed=0):
    import zlib

    import numpy as np

    out = dict(_drawn_inputs(seed))
    spreads = {'L0_attn_scale': (0.125, 0.6),
     'L0_attn_bout': (0.0, 0.1),
     'L0_ffn_br_sp': (0.0, 0.283),
     'L0_ffn_br_fq': (0.0, 0.359),
     'L0_ffn_bs1': (0.0, 0.293),
     'L0_ffn_bs2': (0.0, 0.1),
     'L0_ffn_b1_sp': (0.0, 2.0),
     'L0_ffn_b2_sp': (0.0, 0.579),
     'L0_ffn_b1_fq': (0.0, 2.0),
     'L0_ffn_b2_fq': (0.0, 0.568)}
    factors = {'L0_attn_Wq': 8.0,
     'L0_attn_Wkv': 8.0,
     'L0_attn_mix_pre': 8.0,
     'L0_attn_mix_post': 6.934,
     'L0_attn_Wout': 7.85,
     'L0_ffn_W1_sp': 6.315,
     'L0_ffn_W1_fq': 6.499}
    for name, (base, spread) in spreads.items():
        noise = np.random.default_rng([zlib.crc32(name.encode()), seed]).standard_normal(out[name].shape)
        drawn = base * np.exp(spread * noise) if base else spread * noise
        out[name] = jnp.asarray(drawn.astype(out[name].dtype))
    for name, factor in factors.items():
        out[name] = (out[name] * factor).astype(out[name].dtype)
    return out
```

```python
from contextlib import ExitStack

import concourse.bass as bass
from concourse import mybir

F32 = mybir.dt.float32
F32R = mybir.dt.float32r
BF16 = mybir.dt.bfloat16
I32 = mybir.dt.int32
U8 = mybir.dt.uint8
ALU = mybir.AluOpType
ACT = mybir.ActivationFunctionType
X_AXIS = mybir.AxisListType.X

P = 128
VOCAB, D = 12500, 128
B, N = 128, 128
TILES = B * N // P
H, DH = 8, 64
HD = H * DH
HC = HD // P
E, FF = 8, 512
FC = FF // P
CAP = 1280
ROWS = E * CAP
BANKS = 2
RE = BANKS * E
EPS = 1e-5
MASK_VAL = -1e-9
TWO_PI_HI = 6.28125
TWO_PI_LO = 0.0019353071795864769
INV_TWO_PI = 0.15915494309189535
ROUND = 12582912.0
PI_BELOW = 3.1415925
DROPPED = 1 << 20

VP = 125
VR = VOCAB // VP
VC = 10


def need(eng, sem, count, most=None):
    if isinstance(count, int):
        if most is not None:
            count = min(count, most)
        if count <= 0:
            return
    eng.wait_ge(sem, count)


def need_apart(eng, sem, count):
    need(eng, sem, count)
    if not isinstance(count, int):
        eng.nop(nofuse=True)


class Chain:

    def __init__(self, eng, sem):
        self.eng, self.sem, self.n, self.at = eng, sem, 0, None

    def inc(self, ins):
        self.n += 1
        ins.then_inc(self.sem, 1)

    def wait(self):
        if self.at is None:
            self.eng.wait_ge(self.sem, self.n)
        else:
            i, first, per, before = self.at
            self.eng.wait_ge(self.sem, i * per + (self.n - first * per))

    def __call__(self, ins, apart=False):
        self.inc(ins)
        self.wait()
        if apart and self.at is not None:
            self.eng.nop(nofuse=True)

    def enter(self, i, first, per):
        self.at = (i, first, per, self.n)

    def leave(self, rounds):
        _, _, per, before = self.at
        assert self.n - before == per, (self.n - before, per)
        self.n = before + per * rounds
        self.at = None


def pipelined(eng, step, body, first, last, lead, end, chain=None, per=0):
    for t in range(-lead, first * body):
        step(0, t)
    with eng.Fori(first, last) as i:
        if chain:
            chain.enter(i, first, per)
        for k in range(body):
            step(i, k)
        if chain:
            chain.leave(last - first)
    for t in range(last * body, end):
        step(0, t)


def build(nc, x, weight, num_value, is_num, Wq, Wkv, scale, mix_pre, mix_post, Wout, bout,
          Wr_sp, br_sp, Wr_fq, br_fq, Ws1, bs1, Ws2, bs2,
          W1_sp, b1_sp, W2_sp, b2_sp, W1_fq, b1_fq, W2_fq, b2_fq, out):
    table = nc.dram_tensor("table", (VOCAB, D), F32).ap()
    sent = [nc.dram_tensor(f"sent_{b}", (ROWS, D), F32).ap() for b in ("sp", "fq")]
    answered = [nc.dram_tensor(f"answered_{b}", (ROWS, D), F32).ap() for b in ("sp", "fq")]
    with ExitStack() as whole:
        def keep(name, shape, dt=F32):
            return whole.enter_context(nc.sbuf_tensor(name, shape, dt))

        ident = keep("ident", [P, P])
        h_sb = keep("h_sb", [P, TILES * D])
        ids = keep("ids", [P, B], I32)
        slots = keep("slots", [P, TILES * BANKS], I32)
        gates = keep("gates", [P, TILES * BANKS])
        norm2 = keep("norm2", [P, TILES * 2])
        with ExitStack() as s:
            mats = {n: s.enter_context(nc.sbuf_tensor(n, [P, H * D], F32R))
                    for n in ("M_hi", "M_lo", "N_hi", "N_lo")}
            masked = [s.enter_context(nc.sbuf_tensor(f"masked{k}", [P, H * N], F32)) for k in range(2)]
            off_diag = s.enter_context(nc.sbuf_tensor("off_diag", [P, N], I32))
            setup(nc, x, weight, num_value, is_num, Wq, Wkv, scale, mix_pre, mix_post, Wout,
                  table, sent, ident, ids, mats, masked, off_diag)
            attention(nc, bout, Wr_sp, br_sp, Wr_fq, br_fq, table, sent, ident, h_sb, ids, slots,
                      gates, norm2, mats, masked, off_diag)
        acc = keep("acc", [P, TILES * D])
        for which, weights in enumerate(((W1_sp, b1_sp, W2_sp, b2_sp), (W1_fq, b1_fq, W2_fq, b2_fq), (Ws1, bs1, Ws2, bs2))):
            feed_forward(nc, which, *weights, bs2, sent, answered, ident, h_sb, slots, gates, norm2, acc,
                         out.rearrange("b n d -> (b n) d"))


def setup(nc, x, weight, num_value, is_num, Wq, Wkv, scale, mix_pre, mix_post, Wout,
          table, sent, ident, ids, mats, masked, off_diag):
    CH = VC * D
    ZR = 40
    chunks = VR // VC
    with ExitStack() as s:
        def sb(name, shape, dt=F32):
            return s.enter_context(nc.sbuf_tensor(name, shape, dt))

        def sem(name):
            return s.enter_context(nc.semaphore(name))

        zeros = sb("zeros", [P, ZR * D])
        freq_i = sb("freq_i", [P, D], I32)
        freq = sb("freq", [P, D])
        num_i = sb("num_i", [VP, VR], I32)
        num_f = sb("num_f", [VP, VR])
        isn = sb("isn", [VP, VR], U8)
        rows = [sb(f"rows{k}", [VP, CH]) for k in range(2)]
        angle = [sb(f"angle{k}", [VP, CH]) for k in range(2)]
        turns = sb("turns", [VP, CH])
        sines = [sb(f"sines{k}", [VP, CH]) for k in range(2)]
        mask_c = [sb(f"mask_c{k}", [VP, VC], I32) for k in range(2)]
        num_c = sb("num_c", [VP, VC])
        wq = sb("wq", [P, HD])
        wkv = sb("wkv", [P, 2 * HD])
        wo = sb("wo", [P, HC, D])
        wqT = sb("wqT", [P, HC, P])
        wkT = sb("wkT", [P, HC, P])
        wvT = sb("wvT", [P, HC, P])
        pre = sb("pre", [H, H])
        spre = sb("spre", [H, H])
        sc = sb("sc", [H, 1])
        postT = sb("postT", [H, H])
        head_of = sb("head_of", [H, HD])
        minus = sb("minus", [H, P])
        cpre = sb("cpre", [P, HC, H])
        cpost = sb("cpost", [P, HC, H])
        diag = sb("diag", [P, H])
        mixed = [sb(f"mixed{k}", [P, H, D]) for k in range(2 * HC)]
        idx_i = sb("idx_i", [P, N], I32)
        idx_f = sb("idx_f", [P, N])
        ps_t = [s.enter_context(nc.psum_tensor(f"ps_t{k}", [P, 512], F32)) for k in range(3)]
        ps_m = s.enter_context(nc.psum_tensor("ps_m", [P, H * D], F32))
        ps_n = s.enter_context(nc.psum_tensor("ps_n", [P, H * D], F32))
        ps_c = s.enter_context(nc.psum_tensor("ps_c", [P, 512], F32))
        s_num, s_small, s_zero, s_zeroed = sem("s_num"), sem("s_small"), sem("s_zero"), sem("s_zeroed")
        s_row = [sem(f"s_row{k}") for k in range(2)]
        s_put = [sem(f"s_put{k}") for k in range(2)]
        s_const, s_angle, s_sine, s_done = sem("s_const"), sem("s_angle"), sem("s_sine"), sem("s_done")
        s_turn, s_mixed, s_M, s_hi = sem("s_turn"), sem("s_mixed"), sem("s_M"), sem("s_hi")
        s_coef, s_coefd, s_v = sem("s_coef"), sem("s_coefd"), sem("s_v")
        w_t = weight.rearrange("(p r) d -> p (r d)", p=VP)
        t_t = table.rearrange("(p r) d -> p (r d)", p=VP)
        fills = []
        for b in range(BANKS):
            z_t = sent[b].rearrange("(p n r) d -> n p (r d)", p=P, r=ZR)
            fills += [z_t[n] for n in range(ROWS // P // ZR)]
        block = s.enter_context(nc.Block())

        @block.sync
        def _(sp):
            sp.dma_start(num_i[:, :], num_value.rearrange("(p r) -> p r", p=VP)).then_inc(s_num, 16)
            sp.dma_start(isn[:, :], is_num.rearrange("(p r) -> p r", p=VP)).then_inc(s_num, 16)
            for dst, src in ((idx_i[:, :], x), (wq[:, :], Wq), (wkv[:, :], Wkv),
                             (wo[:, :, :], Wout.rearrange("(c p) n -> p c n", p=P)),
                             (pre[:, :], mix_pre), (postT[:, :], mix_post.rearrange("h g -> g h")),
                             (sc[:, :], scale.rearrange("(h o) -> h o", o=1))):
                sp.dma_start(dst, src, allow_slow_non_contiguous=True).then_inc(s_small, 16)
            for k in range(2):
                sp.dma_start(rows[k][:, :], w_t[:, k * CH:(k + 1) * CH]).then_inc(s_row[k], 16)
            with sp.Fori(1, chunks // 2) as i:
                for k in range(2):
                    sp.wait_ge(s_put[k], 16 * i)
                    sp.dma_start(rows[k][:, :], w_t[:, bass.ds(i * (2 * CH) + k * CH, CH)]).then_inc(s_row[k], 16)
            sp.wait_ge(s_zero, 1)
            for fill in fills:
                sp.dma_start(fill, zeros[:, :]).then_inc(s_zeroed, 16)
            sp.wait_ge(s_zeroed, 16 * len(fills))

        @block.gpsimd
        def _(pool):
            nc.gpsimd.memset(ident[:, :], 0.0).then_inc(s_const, 1)
            nc.gpsimd.memset(off_diag[:, :], 1).then_inc(s_const, 1)
            nc.gpsimd.memset(head_of[:, :], 1.0).then_inc(s_const, 1)
            nc.gpsimd.iota(freq_i[:, :], [[1, D]], base=1, channel_multiplier=0).then_inc(s_const, 1)
            nc.gpsimd.memset(minus[:, :], MASK_VAL).then_inc(s_const, 1)
            pool.wait_ge(s_const, 5)
            nc.gpsimd.affine_select(out=ident[:, :], in_=ident[:, :], compare_op=ALU.not_equal, fill=1.0,
                                    base=0, pattern=[[-1, P]], channel_multiplier=1).then_inc(s_const, 1)
            nc.gpsimd.affine_select(out=off_diag[:, :], in_=off_diag[:, :], compare_op=ALU.not_equal, fill=0,
                                    base=0, pattern=[[-1, P]], channel_multiplier=1).then_inc(s_const, 1)
            nc.gpsimd.affine_select(out=head_of[:, :], in_=head_of[:, :], compare_op=ALU.is_ge, fill=0.0,
                                    base=0, pattern=[[1, HD]], channel_multiplier=-DH).then_inc(s_const, 1)
            pool.wait_ge(s_const, 8)
            nc.gpsimd.affine_select(out=head_of[:, :], in_=head_of[:, :], compare_op=ALU.is_ge, fill=0.0,
                                    base=DH - 1, pattern=[[-1, HD]], channel_multiplier=DH).then_inc(s_const, 1)
            nc.gpsimd.memset(zeros[:, :], 0.0).then_inc(s_zero, 1)

        @block.scalar
        def _(act):
            for n, (ps, hi) in enumerate(((ps_m, "M_hi"), (ps_n, "N_hi"))):
                act.wait_ge(s_M, n + 1)
                nc.scalar.activation(mats[hi][:, :], ps[:, :], ACT.Copy).then_inc(s_hi, 1)
            with act.Fori(0, chunks // 2) as i:
                for k in range(2):
                    act.wait_ge(s_angle, 2 * i + (k + 1))
                    nc.scalar.activation(sines[k][:, :], angle[k][:, :], ACT.Sin).then_inc(s_sine, 1)
                    act.wait_ge(s_done, 2 * i + (k + 1))
                    act.dma_start(t_t[:, bass.ds(i * (2 * CH) + k * CH, CH)], rows[k][:, :]).then_inc(s_put[k], 16)
            for k in range(2):
                act.wait_ge(s_put[k], 16 * (chunks // 2))

        @block.tensor
        def _(pe):
            pe.wait_ge(s_const, 9)
            pe.wait_ge(s_small, 112)
            for c in range(HC):
                nc.tensor.transpose(ps_t[0][:, c * P:(c + 1) * P], wq[:, c * P:(c + 1) * P], ident[:, :])
                nc.tensor.transpose(ps_t[1][:, c * P:(c + 1) * P], wkv[:, c * P:(c + 1) * P], ident[:, :])
                last = nc.tensor.transpose(ps_t[2][:, c * P:(c + 1) * P], wkv[:, HD + c * P:HD + (c + 1) * P], ident[:, :])
            last.then_inc(s_turn, 1)
            pe.wait_ge(s_coef, 1)
            for c in range(HC):
                nc.tensor.matmul(ps_c[:, c * H:(c + 1) * H], head_of[:, c * P:(c + 1) * P], spre[:, :], start=True, stop=True)
                nc.tensor.matmul(ps_c[:, 64 + c * H:64 + (c + 1) * H], head_of[:, c * P:(c + 1) * P], postT[:, :], start=True, stop=True)
            nc.tensor.matmul(ps_c[:, 128:128 + H], minus[:, :], pre[:, :], start=True, stop=True)
            nc.tensor.transpose(ps_c[:, 256:384], idx_f[:, :], ident[:, :]).then_inc(s_coefd, 1)
            for w, (lhs, ps) in enumerate(((wkT, ps_m), (wvT, ps_n))):
                for c in range(HC):
                    pe.wait_ge(s_mixed, w * HC + c + 1)
                    m = mixed[w * HC + c][:, :, :].rearrange("p g d -> p (g d)")
                    for half in range(2):
                        last = nc.tensor.matmul(ps[:, half * 512:(half + 1) * 512], lhs[:, c, :],
                                                m[:, half * 512:(half + 1) * 512], start=(c == 0), stop=(c == HC - 1))
                last.then_inc(s_M, 1)

        @block.vector
        def _(dve):
            link = Chain(dve, s_v)
            dve.wait_ge(s_small, 112)
            link.inc(nc.vector.tensor_copy(idx_f[:, :], idx_i[:, :]))
            nc.vector.tensor_scalar(spre[:, :], pre[:, :], sc[:, 0:1], None, ALU.mult).then_inc(s_coef, 1)
            dve.wait_ge(s_turn, 1)
            for n, dst in enumerate((wqT, wkT, wvT)):
                link.inc(nc.vector.tensor_copy(dst[:, :, :].rearrange("p c n -> p (c n)"), ps_t[n][:, :]))
            dve.wait_ge(s_coefd, 1)
            link.inc(nc.vector.tensor_copy(cpre[:, :, :].rearrange("p c h -> p (c h)"), ps_c[:, 0:HC * H]))
            link.inc(nc.vector.tensor_copy(cpost[:, :, :].rearrange("p c h -> p (c h)"), ps_c[:, 64:64 + HC * H]))
            link.inc(nc.vector.tensor_copy(diag[:, :], ps_c[:, 128:128 + H]))
            link(nc.vector.tensor_copy(ids[:, :], ps_c[:, 256:384]))
            for w, (src, co) in enumerate(((wqT, cpre), (wo, cpost))):
                for c in range(HC):
                    nc.vector.tensor_tensor(mixed[w * HC + c][:, :, :], src[:, c, :].unsqueeze(1).to_broadcast([P, H, D]),
                                            co[:, c, :].unsqueeze(2).to_broadcast([P, H, D]), ALU.mult).then_inc(s_mixed, 1)
            for k in range(2):
                link.inc(nc.vector.tensor_copy(masked[k][:, :].rearrange("p (g j) -> p g j", g=H),
                                               diag[:, :].unsqueeze(2).to_broadcast([P, H, N])))
            for n, (ps, m) in enumerate(((ps_m, "M"), (ps_n, "N"))):
                dve.wait_ge(s_hi, n + 1)
                link.inc(nc.vector.tensor_tensor(mats[m + "_lo"][:, :], ps[:, :], mats[m + "_hi"][:, :].bitcast(F32), ALU.subtract))
            dve.wait_ge(s_const, 4)
            dve.wait_ge(s_num, 32)
            link.inc(nc.vector.tensor_copy(freq[:, :], freq_i[:, :]))
            link(nc.vector.tensor_scalar(num_f[:, :], num_i[:, :], 0.001, None, ALU.mult))
            per = 14
            with dve.Fori(0, chunks // 2) as i:
                link.enter(i, 0, per)
                for k in range(2):
                    a = angle[k][:, :]
                    link.inc(nc.vector.tensor_copy(mask_c[k][:, :], isn[:, bass.ds(i * (2 * VC) + k * VC, VC)]))
                    link(nc.vector.tensor_copy(num_c[:, :], num_f[:, bass.ds(i * (2 * VC) + k * VC, VC)]))
                    link(nc.vector.tensor_tensor(a.rearrange("p (r d) -> p r d", r=VC),
                                                 freq[0:VP, :].unsqueeze(1).to_broadcast([VP, VC, D]),
                                                 num_c[:, :].unsqueeze(2).to_broadcast([VP, VC, D]), ALU.mult))
                    link(nc.vector.tensor_scalar(turns[:, :], a, INV_TWO_PI, ROUND, ALU.mult, ALU.add))
                    link(nc.vector.tensor_scalar(turns[:, :], turns[:, :], ROUND, None, ALU.subtract))
                    link(nc.vector.scalar_tensor_tensor(a, turns[:, :], -TWO_PI_HI, a, ALU.mult, ALU.add))
                    link(nc.vector.scalar_tensor_tensor(a, turns[:, :], -TWO_PI_LO, a, ALU.mult, ALU.add))
                    nc.vector.tensor_scalar(a, a, PI_BELOW, -PI_BELOW, ALU.min, ALU.max).then_inc(s_angle, 1)
                    dve.wait_ge(s_row[k], 16 * i + 16)
                    need_apart(dve, s_sine, 2 * i + (k + 1))
                    nc.vector.copy_predicated(rows[k][:, :].rearrange("p (r d) -> p r d", r=VC),
                                              mask_c[k][:, :].unsqueeze(2).to_broadcast([VP, VC, D]),
                                              sines[k][:, :].rearrange("p (r d) -> p r d", r=VC)).then_inc(s_done, 1)
                link.leave(chunks // 2)


def attention(nc, bout, Wr_sp, br_sp, Wr_fq, br_fq, table, sent, ident, h_sb, ids, slots, gates, norm2,
              mats, masked, off_diag):
    BODY, FIRST, LAST, LEAD, END = 8, 3, 14, 12, TILES + 18
    GROUPS, QUADS = TILES // 2, TILES // 4
    with ExitStack() as s:
        def sb(name, shape, dt=F32):
            return s.enter_context(nc.sbuf_tensor(name, shape, dt))

        def pb(name, cols):
            return s.enter_context(nc.psum_tensor(name, [P, cols], F32))

        def sem(name):
            return s.enter_context(nc.semaphore(name))

        got = [sb(f"got{k}", [P, D]) for k in range(8)]
        gi = [sb(f"gi{k}", [P, 4], I32) for k in range(2)]
        x1 = [sb(f"x1_{k}", [P, 2 * D]) for k in range(2)]
        xT_hi = sb("xT_hi", [P, 4, 2 * N], F32R)
        xT_lo = sb("xT_lo", [P, 4, 2 * N], F32R)
        w_hi = [sb(f"w_hi{k}", [P, 2, H, N], F32R) for k in range(2)]
        w_lo = [sb(f"w_lo{k}", [P, 2, H, N], F32R) for k in range(2)]
        nmax = [sb(f"nmax{k}", [P, H]) for k in range(2)]
        expd = [sb(f"expd{k}", [P, H * N]) for k in range(2)]
        total = [sb(f"total{k}", [P, H]) for k in range(4)]
        rtotal = [sb(f"rtotal{k}", [P, H]) for k in range(2)]
        prob = [sb(f"prob{k}", [P, H * N]) for k in range(2)]
        probT = [sb(f"probT{k}", [P, H * N]) for k in range(2)]
        u = [sb(f"u{k}", [P, H * D]) for k in range(2)]
        bout_b = sb("bout_b", [P, D])
        x2 = [sb(f"x2_{k}", [P, D]) for k in range(8)]
        x2T = sb("x2T", [P, 4 * N])
        stat = [sb(f"stat{k}", [P, 6]) for k in range(8)]
        mv1 = [sb(f"mv1_{k}", [P, 4, 2]) for k in range(2)]
        mv2 = [sb(f"mv2_{k}", [P, 4, 2]) for k in range(2)]
        var = sb("var", [P, 8])
        rstd = [sb(f"rstd{k}", [P, 8]) for k in range(2)]
        power = sb("power", [P, 8])
        wr = sb("wr", [P, RE])
        br_b = sb("br_b", [P, RE])
        tri = sb("tri", [P, P], BF16)
        ones = sb("ones", [P, P], BF16)
        rank = sb("rank", [P, E])
        rank_i = sb("rank_i", [P, E], I32)
        logits = sb("logits", [P, 4 * RE])
        work = sb("work", [P, 4 * RE])
        work2 = sb("work2", [P, 4 * RE])
        expo = sb("expo", [P, 4 * RE])
        chosen = sb("chosen", [P, 4 * RE], BF16)
        counts = sb("counts", [P, 8 * RE])
        before = sb("before", [P, 5 * RE])
        top = sb("top", [P, 8])
        gate = sb("gate", [P, 8])
        key = sb("key", [P, 8])
        place = sb("place", [P, 8])
        slot = sb("slot", [P, 8])
        over = sb("over", [P, 8])
        kept = sb("kept", [P, 8])
        to_row = [sb(f"to_row{k}", [P, 8], I32) for k in range(2)]
        ps_s = pb("ps_s", H * N)
        ps_ut = pb("ps_ut", H * D)
        ps_w = [pb(f"ps_w{k}", 512) for k in range(2)]
        ps_x = pb("ps_x", 512)
        ps_o = pb("ps_o", 512)
        names = ("scored", "copied", "maxed", "expd", "rtot", "normed", "turned", "turn_out", "u_made", "u_out",
                 "pv", "h1", "w_made", "w_hi", "w_lo", "x_made", "x_turned", "xhi", "xlo", "stat1", "stat2",
                 "rstd", "x2", "x2_turned", "x2T", "logit", "logit_out", "chosen", "cum", "cum_out", "routed",
                 "gate_in", "gate_exp", "resid", "const", "cload", "chain", "pchain")
        S = {n: sem("a_" + n) for n in names}
        s_got = [sem(f"a_got{k}") for k in range(8)]
        s_sent = [sem(f"a_sent{k}") for k in range(8)]
        block = s.enter_context(nc.Block())

        def live(i, k):
            return not isinstance(i, int) or 0 <= BODY * i + k < TILES

        def tile(i, k):
            return i * BODY + k

        def group(i, k):
            return i * (BODY // 2) + k // 2

        def quad(i, k):
            return i * (BODY // 4) + k // 4

        @block.sync
        def _(sp):
            sp.dma_start(wr[:, 0:E], Wr_sp).then_inc(S["cload"], 16)
            sp.dma_start(wr[:, E:RE], Wr_fq).then_inc(S["cload"], 16)
            sp.dma_start(br_b[:, 0:E], br_sp.rearrange("(o e) -> o e", o=1).to_broadcast([P, E])).then_inc(S["cload"], 16)
            sp.dma_start(br_b[:, E:RE], br_fq.rearrange("(o e) -> o e", o=1).to_broadcast([P, E])).then_inc(S["cload"], 16)
            sp.dma_start(bout_b[:, :], bout.rearrange("(o e) -> o e", o=1).to_broadcast([P, D])).then_inc(S["cload"], 16)

        @block.gpsimd
        def _(pool):
            link = Chain(pool, S["pchain"])
            link.inc(nc.gpsimd.memset(power[:, :], -0.5))
            link.inc(nc.gpsimd.memset(ones[:, :], 1.0))
            link.inc(nc.gpsimd.memset(tri[:, :], 1.0))
            link.inc(nc.gpsimd.iota(rank_i[:, :], [[-1, E]], base=E, channel_multiplier=0))
            link.inc(nc.gpsimd.memset(before[:, :], 0.0))
            for m in (*mv1, *mv2):
                link.inc(nc.gpsimd.memset(m[:, :, :], 1.0))
            link.wait()
            link(nc.gpsimd.affine_select(out=tri[:, :], in_=tri[:, :], compare_op=ALU.is_ge, fill=0.0,
                                         base=0, pattern=[[1, P]], channel_multiplier=-1))
            pool.wait_ge(S["cload"], 80)
            nc.gpsimd.memset(var[:, :], 1.0).then_inc(S["const"], 1)
            pool.wait_ge(S["const"], 1)

            def step(i, k):
                j = k % 4
                if live(i, k + 10):
                    if (k + 10) % 4 == 0:
                        q = quad(i, k + 10)
                        if (not isinstance(i, int)) or q >= 2:
                            for b in range(4):
                                pool.wait_ge(s_got[(k + 10 + b) % 8], (i + (k + 10 + b) // 8) * 16)
                        link(nc.gpsimd.tensor_copy(gi[((k + 10) // 4) % 2][:, :], ids[:, bass.ds(tile(i, k + 10), 4)]))
                    need(pool, S["x_made"], group(i, k + 2) + 1)
                    need_apart(pool, S["resid"], tile(i, k + 3))
                    nc.gpsimd.indirect_dma_start(
                        got[(k + 10) % 8][:, :], None, table,
                        bass.IndirectOffsetOnAxis(ap=gi[((k + 10) // 4) % 2][:, (k + 10) % 4:(k + 10) % 4 + 1], axis=0),
                    ).then_inc(s_got[(k + 10) % 8], 16)
                if live(i, k - 2):
                    need(pool, S["rtot"], tile(i, k - 1))
                    need(pool, S["turned"], tile(i, k - 3))
                    nc.gpsimd.tensor_tensor(prob[k % 2][:, :].rearrange("p (g j) -> p g j", g=H),
                                            expd[k % 2][:, :].rearrange("p (g j) -> p g j", g=H),
                                            rtotal[k % 2][:, :].unsqueeze(2).to_broadcast([P, H, N]),
                                            ALU.mult).then_inc(S["normed"], 1)
                if live(i, k + 7):
                    pool.wait_ge(s_got[(k + 7) % 8], (i + ((k + 7) // 8 + 1)) * 16)
                    nc.gpsimd.tensor_tensor(h_sb[:, bass.ds(tile(i, k + 7) * D, D)], got[(k + 7) % 8][:, :],
                                            bout_b[:, :], ALU.add).then_inc(S["resid"], 1)
                if j == 0 and (live(i, k + 4) or live(i, k - 8)):
                    if live(i, k + 4):
                        need(pool, S["stat1"], quad(i, k + 4) + 1)
                    if live(i, k - 8):
                        need(pool, S["stat2"], quad(i, k - 8) + 1)
                    need(pool, S["x_made"], group(i, k), GROUPS)
                    need(pool, S["x2"], group(i, k - 12), GROUPS)
                    if not isinstance(i, int):
                        pool.nop(nofuse=True)
                    m1, m2 = mv1[(k // 4 + 1) % 2], mv2[(k // 4) % 2]
                    link.inc(nc.gpsimd.tensor_scalar(var[:, 0:4], m1[:, :, 1], 1.0, EPS, ALU.mult, ALU.add))
                    link(nc.gpsimd.tensor_scalar(var[:, 4:8], m2[:, :, 1], 1.0, EPS, ALU.mult, ALU.add))
                    nc.gpsimd.tensor_tensor(rstd[(k // 4) % 2][:, :], var[:, :], power[:, :], ALU.pow).then_inc(S["rstd"], 1)
                if live(i, k - 14):
                    need_apart(pool, S["routed"], quad(i, k - 14) + 1)
                    for b in range(BANKS):
                        c = ((k - 14) % 4) * BANKS + b
                        nc.gpsimd.indirect_dma_start(
                            sent[b], bass.IndirectOffsetOnAxis(ap=to_row[((k - 14) // 4) % 2][:, c:c + 1], axis=0),
                            x2[(k - 14) % 8][:, :], None, bounds_check=ROWS - 1, oob_is_err=False,
                        ).then_inc(s_sent[(k - 14) % 8], 16)

            pipelined(pool, step, BODY, FIRST, LAST, LEAD, END, link, PCHAIN)
            for k in range(8):
                pool.wait_ge(s_sent[k], TILES // 8 * 32)

        @block.tensor
        def _(pe):
            pe.wait_ge(S["const"], 1)

            def step(i, k):
                j = k % 4
                if j == 0 and live(i, k - 12):
                    q = quad(i, k - 12)
                    need(pe, S["x2T"], q + 1)
                    need(pe, S["h1"], tile(i, k - 4), TILES)
                    for b in range(4):
                        mm = nc.tensor.matmul(ps_o[:, 128 + b * RE:128 + (b + 1) * RE], x2T[:, b * N:(b + 1) * N],
                                              wr[:, :], start=True, stop=True)
                    mm.then_inc(S["logit"], 1)
                if j == 1 and live(i, k - 13):
                    q = quad(i, k - 13)
                    need(pe, S["chosen"], q + 1)
                    need(pe, S["h1"], tile(i, k - 4), TILES)
                    nc.tensor.matmul(ps_o[:, 192:192 + 4 * RE], tri[:, :], chosen[:, :], start=True, stop=True)
                    nc.tensor.matmul(ps_o[:, 256:256 + 4 * RE], ones[:, :], chosen[:, :], start=True, stop=True).then_inc(S["cum"], 1)
                if live(i, k):
                    m, b = k // 2, k % 2
                    need(pe, S["copied"], tile(i, k))
                    need(pe, S["w_lo"], group(i, k) * 4 + 4)
                    cols = slice(b * N, (b + 1) * N)
                    hi, lo = xT_hi[:, m % 4, cols], xT_lo[:, m % 4, cols]
                    for n, (lhs, rhs) in enumerate(((hi, w_hi), (hi, w_lo), (lo, w_hi))):
                        r = rhs[m % 2][:, b, :, :].rearrange("p g j -> p (g j)")
                        for half in range(2):
                            mm = nc.tensor.matmul(ps_s[:, half * 512:(half + 1) * 512], lhs,
                                                  r[:, half * 512:(half + 1) * 512], start=(n == 0), stop=(n == 2))
                    mm.then_inc(S["scored"], 1)
                if live(i, k - 3):
                    need(pe, S["normed"], tile(i, k - 2))
                    need(pe, S["u_out"], tile(i, k - 3))
                    for g in range(H):
                        mm = nc.tensor.transpose(ps_ut[:, g * N:(g + 1) * N], prob[(k - 3) % 2][:, g * N:(g + 1) * N], ident[:, :])
                    mm.then_inc(S["turned"], 1)
                if live(i, 2 * (k // 2 + 1)):
                    m = k // 2 + 1
                    need(pe, S["xlo"], group(i, 2 * m) + 1)
                    for q in (2 * (k % 2), 2 * (k % 2) + 1):
                        need(pe, S["w_lo"], group(i, 2 * m) * 4 + q - 1)
                        for g in (2 * q, 2 * q + 1):
                            o = ps_w[q % 2][:, (g % 2) * 256:(g % 2 + 1) * 256]
                            M_hi, M_lo = (mats[n][:, g * D:(g + 1) * D] for n in ("M_hi", "M_lo"))
                            nc.tensor.matmul(o, M_hi, xT_hi[:, m % 4, :], start=True, stop=False)
                            nc.tensor.matmul(o, M_lo, xT_hi[:, m % 4, :], start=False, stop=False)
                            mm = nc.tensor.matmul(o, M_hi, xT_lo[:, m % 4, :], start=False, stop=True)
                        mm.then_inc(S["w_made"], 1)
                if live(i, k - 4):
                    need(pe, S["turn_out"], tile(i, k - 3))
                    need(pe, S["u_out"], tile(i, k - 3))
                    need(pe, S["h1"], tile(i, k - 4))
                    if j == 0 and live(i, k - 12):
                        need(pe, S["logit_out"], quad(i, k - 12) + 1)
                    if j == 1 and live(i, k - 13):
                        need(pe, S["cum_out"], quad(i, k - 13) + 1)
                    for g in range(H):
                        mm = nc.tensor.matmul(ps_o[:, 0:D], probT[k % 2][:, g * N:(g + 1) * N],
                                              u[k % 2][:, g * D:(g + 1) * D], start=(g == 0), stop=(g == H - 1))
                    mm.then_inc(S["pv"], 1)
                if live(i, k - 3):
                    m, b = (k - 3) // 2, (k - 3) % 2
                    need(pe, S["turn_out"], tile(i, k - 2))
                    cols = slice(b * N, (b + 1) * N)
                    hi, lo = xT_hi[:, m % 4, cols], xT_lo[:, m % 4, cols]
                    for n, (lhs, rhs) in enumerate(((hi, "N_hi"), (hi, "N_lo"), (lo, "N_hi"))):
                        for half in range(2):
                            mm = nc.tensor.matmul(ps_ut[:, half * 512:(half + 1) * 512], lhs,
                                                  mats[rhs][:, half * 512:(half + 1) * 512], start=(n == 0), stop=(n == 2))
                    mm.then_inc(S["u_made"], 1)
                if k % 2 and live(i, k + 3):
                    m = group(i, k + 3)
                    need(pe, S["x_made"], m + 1)
                    need(pe, S["xlo"], m)
                    need(pe, S["x2T"], quad(i, k - 11) + 1, QUADS)
                    for b in range(2):
                        mm = nc.tensor.transpose(ps_x[:, b * N:(b + 1) * N], x1[((k + 3) // 2) % 2][:, b * D:(b + 1) * D], ident[:, :])
                    mm.then_inc(S["x_turned"], 1)
                if j == 2 and live(i, k - 10):
                    need(pe, S["x2"], group(i, k - 10) + 2)
                    need(pe, S["xlo"], group(i, k + 2) + 1, GROUPS)
                    for b in range(4):
                        mm = nc.tensor.transpose(ps_x[:, b * N:(b + 1) * N], x2[(k - 10 + b) % 8][:, :], ident[:, :])
                    mm.then_inc(S["x2_turned"], 1)

            pipelined(pe, step, BODY, FIRST, LAST, LEAD, END)

        @block.scalar
        def _(act):
            def step(i, k):
                j = k % 4

                def exps(heads):
                    for g in heads:
                        ins = nc.scalar.activation(expd[(k - 1) % 2][:, g * N:(g + 1) * N],
                                                   masked[(k - 1) % 2][:, g * N:(g + 1) * N], ACT.Exp,
                                                   bias=nmax[(k - 1) % 2][:, g:g + 1],
                                                   accum_out=total[(k - 1) % 4][:, g:g + 1])
                    return ins

                if j == 3 and live(i, k - 11):
                    q = quad(i, k - 11)
                    need(act, S["x2_turned"], q + 1)
                    need(act, S["logit"], q)
                    nc.scalar.activation(x2T[:, :], ps_x[:, :], ACT.Copy).then_inc(S["x2T"], 1)
                if k % 2 == 0 and live(i, k + 2):
                    m = group(i, k + 2)
                    need(act, S["x_turned"], m + 1)
                    need(act, S["u_made"], tile(i, k + 2) - 6)
                    nc.scalar.activation(xT_hi[:, (k // 2 + 1) % 4, :], ps_x[:, 0:2 * N], ACT.Copy).then_inc(S["xhi"], 1)
                if live(i, k - 4):
                    need(act, S["u_made"], tile(i, k - 3))
                    need(act, S["pv"], tile(i, k - 5))
                    nc.scalar.activation(u[k % 2][:, :], ps_ut[:, :], ACT.Copy).then_inc(S["u_out"], 1)
                if live(i, k - 1):
                    need(act, S["maxed"], tile(i, k))
                    need(act, S["normed"], tile(i, k - 2))
                    exps(range(0, 3))
                if live(i, k - 3):
                    need(act, S["turned"], tile(i, k - 2))
                    need(act, S["pv"], tile(i, k - 4))
                    nc.scalar.activation(probT[(k - 3) % 2][:, :], ps_ut[:, :], ACT.Copy).then_inc(S["turn_out"], 1)
                if live(i, 2 * (k // 2 + 1)):
                    m = k // 2 + 1
                    for q in (2 * (k % 2), 2 * (k % 2) + 1):
                        need(act, S["w_made"], group(i, 2 * m) * 4 + q + 1)
                        need(act, S["scored"], tile(i, 2 * m) - 2)
                        nc.scalar.activation(w_hi[m % 2][:, :, 2 * q:2 * q + 2, :].rearrange("p b g j -> p g b j"),
                                             ps_w[q % 2][:, :].rearrange("p (g b j) -> p g b j", g=2, b=2),
                                             ACT.Copy).then_inc(S["w_hi"], 1)
                if live(i, k - 1):
                    exps(range(3, 8)).then_inc(S["expd"], 1)
                if j == 0 and live(i, k - 12):
                    need(act, S["gate_in"], quad(i, k - 12) + 1)
                    nc.scalar.activation(expo[:, :], work[:, :], ACT.Exp).then_inc(S["gate_exp"], 1)

            pipelined(act, step, BODY, FIRST, LAST, LEAD, END)

        @block.vector
        def _(dve):
            link = Chain(dve, S["chain"])
            dve.wait_ge(S["const"], 1)
            link(nc.vector.tensor_copy(rank[:, :], rank_i[:, :]))

            def by_expert(t):
                return t[:, :].rearrange("p (n e) -> p n e", e=E)

            def over_experts(t):
                return t[:, :].unsqueeze(2).to_broadcast([P, 4 * BANKS, E])

            def step(i, k):
                j = k % 4
                if live(i, k - 2):
                    need(dve, S["expd"], tile(i, k - 1))
                    need(dve, S["normed"], tile(i, k - 3))
                    nc.vector.reciprocal(rtotal[k % 2][:, :], total[(k - 2) % 4][:, :]).then_inc(S["rtot"], 1)
                routing = j == 0 and live(i, k - 12)
                if routing:
                    need(dve, S["logit"], quad(i, k - 12) + 1)
                    nc.vector.tensor_tensor(logits[:, :].rearrange("p (t e) -> p t e", t=4),
                                            ps_o[:, 128:128 + 4 * RE].rearrange("p (t e) -> p t e", t=4),
                                            br_b[:, :].unsqueeze(1).to_broadcast([P, 4, RE]), ALU.add).then_inc(S["logit_out"], 1)
                placing = j == 1 and live(i, k - 13)
                if placing:
                    need(dve, S["cum"], quad(i, k - 13) + 1)
                    nc.vector.tensor_copy(counts[:, :], ps_o[:, 192:192 + 8 * RE]).then_inc(S["cum_out"], 1)
                if k % 2 == 0 and live(i, k + 2):
                    m = group(i, k + 2)
                    need(dve, S["xhi"], m + 1)
                    c = (k // 2 + 1) % 4
                    nc.vector.tensor_tensor(xT_lo[:, c, :], ps_x[:, 0:2 * N], xT_hi[:, c, :].bitcast(F32), ALU.subtract).then_inc(S["xlo"], 1)
                if live(i, k):
                    need(dve, S["scored"], tile(i, k + 1))
                    need_apart(dve, S["expd"], tile(i, k - 1))
                    nc.vector.copy_predicated(masked[k % 2][:, :].rearrange("p (g j) -> p g j", g=H),
                                              off_diag[:, :].unsqueeze(1).to_broadcast([P, H, N]),
                                              ps_s[:, :].rearrange("p (g j) -> p g j", g=H)).then_inc(S["copied"], 1)
                    need(dve, S["copied"], tile(i, k + 1))
                    nc.vector.tensor_reduce(nmax[k % 2][:, :], masked[k % 2][:, :].rearrange("p (g j) -> p g j", g=H),
                                            X_AXIS, ALU.max, negate=True).then_inc(S["maxed"], 1)
                if routing:
                    need(dve, S["logit_out"], quad(i, k - 12) + 1)
                    link(nc.vector.tensor_reduce(top[:, :], by_expert(logits), X_AXIS, ALU.max))
                    link.inc(nc.vector.tensor_tensor(by_expert(work2), by_expert(logits), over_experts(top), ALU.is_equal))
                    nc.vector.tensor_tensor(by_expert(work), by_expert(logits), over_experts(top), ALU.subtract).then_inc(S["gate_in"], 1)
                    link.wait()
                    link(nc.vector.tensor_tensor(by_expert(work2), by_expert(work2),
                                                 rank[:, :].unsqueeze(1).to_broadcast([P, 4 * BANKS, E]), ALU.mult))
                    link(nc.vector.tensor_reduce(key[:, :], by_expert(work2), X_AXIS, ALU.max))
                    nc.vector.tensor_tensor(by_expert(chosen), rank[:, :].unsqueeze(1).to_broadcast([P, 4 * BANKS, E]),
                                            over_experts(key), ALU.is_equal).then_inc(S["chosen"], 1)
                if placing:
                    need(dve, S["cum_out"], quad(i, k - 13) + 1)
                    need(dve, S["gate_exp"], quad(i, k - 13) + 1)
                    link(nc.vector.tensor_reduce(gate[:, :], by_expert(expo), X_AXIS, ALU.add))
                    link.inc(nc.vector.reciprocal(gate[:, :], gate[:, :]))
                    for t in range(4):
                        link(nc.vector.tensor_tensor(before[:, (t + 1) * RE:(t + 2) * RE], before[:, t * RE:(t + 1) * RE],
                                                     counts[:, (4 + t) * RE:(5 + t) * RE], ALU.add))
                    link(nc.vector.tensor_tensor(counts[:, 0:4 * RE], counts[:, 0:4 * RE], before[:, 0:4 * RE], ALU.add))
                    link.inc(nc.vector.tensor_copy(before[:, 0:RE], before[:, 4 * RE:5 * RE]))
                    link(nc.vector.tensor_tensor(work2[:, :], counts[:, 0:4 * RE], chosen[:, :], ALU.mult))
                    link(nc.vector.tensor_reduce(place[:, :], by_expert(work2), X_AXIS, ALU.add))
                    link.inc(nc.vector.tensor_scalar(key[:, :], key[:, :], -float(CAP), float(ROWS - 1), ALU.mult, ALU.add))
                    link.inc(nc.vector.tensor_scalar(over[:, :], place[:, :], CAP + 0.5, float(DROPPED), ALU.is_gt, ALU.mult))
                    link.inc(nc.vector.tensor_scalar(kept[:, :], place[:, :], CAP + 0.5, None, ALU.is_lt))
                    link(nc.vector.tensor_scalar(slot[:, :], place[:, :], float(CAP), None, ALU.min))
                    link(nc.vector.tensor_tensor(slot[:, :], slot[:, :], key[:, :], ALU.add))
                    c = tile(i, k - 13) * BANKS
                    link.inc(nc.vector.tensor_copy(slots[:, bass.ds(c, 8)], slot[:, :]))
                    link.inc(nc.vector.tensor_tensor(gates[:, bass.ds(c, 8)], kept[:, :], gate[:, :], ALU.mult))
                    q = quad(i, k - 13)
                    if (not isinstance(i, int)) or q >= 2:
                        for b in range(4):
                            dve.wait_ge(s_sent[(k - 13 + b) % 8], (i + (k - 13) // 8) * 32)
                    nc.vector.tensor_tensor(to_row[((k - 13) // 4) % 2][:, :], slot[:, :], over[:, :], ALU.add).then_inc(S["routed"], 1)
                if live(i, 2 * (k // 2 + 1)):
                    m = k // 2 + 1
                    for q in (2 * (k % 2), 2 * (k % 2) + 1):
                        need(dve, S["w_hi"], group(i, 2 * m) * 4 + q + 1)
                        dst, hi = (w[m % 2][:, :, 2 * q:2 * q + 2, :].rearrange("p b g j -> p g b j") for w in (w_lo, w_hi))
                        nc.vector.tensor_tensor(dst, ps_w[q % 2][:, :].rearrange("p (g b j) -> p g b j", g=2, b=2),
                                                hi.bitcast(F32), ALU.subtract).then_inc(S["w_lo"], 1)
                if j in (1, 2) and live(i, k - 8 - (j == 1)):
                    t0 = k - 8 - (j == 1)
                    if j == 1:
                        need(dve, S["rstd"], quad(i, k) + 2)
                    for b in range(2):
                        t = t0 + b
                        if (not isinstance(i, int)) or tile(i, t) >= 8:
                            dve.wait_ge(s_sent[t % 8], (i + t // 8) * 32)
                        a = ((t // 4) % 2, t % 4)
                        mean, rs = mv2[a[0]][:, a[1], 0:1], rstd[a[0]][:, 4 + a[1]:5 + a[1]]
                        ins = nc.vector.tensor_scalar(x2[t % 8][:, :], h_sb[:, bass.ds(tile(i, t) * D, D)], mean, rs,
                                                      ALU.subtract, ALU.mult)
                    ins.then_inc(S["x2"], 1)
                    if j == 2:
                        n2 = norm2[:, bass.ds(tile(i, k - 10) * 2, 8)].rearrange("p (t c) -> p t c", c=2)
                        a = ((k - 10) // 4) % 2
                        link.inc(nc.vector.tensor_copy(n2[:, :, 0], mv2[a][:, :, 0]))
                        link.inc(nc.vector.tensor_copy(n2[:, :, 1], rstd[a][:, 4:8]))
                if k % 2 and live(i, k + 3):
                    need(dve, S["rstd"], quad(i, k) + 2)
                    need(dve, S["x_turned"], group(i, k + 1))
                    for b in range(2):
                        t = k + 3 + b
                        a = ((t // 4) % 2, t % 4)
                        mean, rs = mv1[a[0]][:, a[1], 0:1], rstd[(t // 4 - 1) % 2][:, a[1]:a[1] + 1]
                        ins = nc.vector.tensor_scalar(x1[((k + 3) // 2) % 2][:, b * D:(b + 1) * D], got[t % 8][:, :], mean, rs,
                                                      ALU.subtract, ALU.mult)
                    ins.then_inc(S["x_made"], 1)
                if live(i, k + 8):
                    dve.wait_ge(s_got[k % 8], (i + (k // 8 + 2)) * 16)
                    link(nc.vector.bn_stats(stat[j][:, :], got[k % 8][:, :]), apart=True)
                    ins = nc.vector.bn_aggr(mv1[((k + 8) // 4) % 2][:, k % 4, :], stat[j][:, :])
                    if j == 3:
                        ins.then_inc(S["stat1"], 1)
                    else:
                        link.inc(ins)
                if live(i, k - 4):
                    hk = h_sb[:, bass.ds(tile(i, k - 4) * D, D)]
                    need(dve, S["pv"], tile(i, k - 3))
                    need(dve, S["resid"], tile(i, k - 3))
                    nc.vector.tensor_tensor(hk, ps_o[:, 0:D], hk, ALU.add).then_inc(S["h1"], 1)
                    need_apart(dve, S["h1"], tile(i, k - 3))
                    link(nc.vector.bn_stats(stat[4 + j][:, :], hk), apart=True)
                    ins = nc.vector.bn_aggr(mv2[((k - 4) // 4) % 2][:, k % 4, :], stat[4 + j][:, :])
                    if j == 3:
                        ins.then_inc(S["stat2"], 1)
                    else:
                        link.inc(ins)

            pipelined(dve, step, BODY, FIRST, LAST, LEAD, END, link, VCHAIN)
            link.wait()



def feed_forward(nc, which, W1, b1, W2, b2, bs2, sent, answered, ident, h_sb, slots, gates, norm2, acc, out):
    routed = which < 2
    name = ("sp", "fq", "sh")[which]
    G = 2 * P
    EACH = ROWS // E // G if routed else B * N // G
    GROUPS = EACH * E if routed else EACH
    BODY, FIRST, LAST = (2 * EACH, 1, GROUPS // (2 * EACH) - 1) if routed else (4, 1, GROUPS // 4 - 1)
    RING = EACH if routed else 2
    LOADS = 64
    with ExitStack() as s:
        def sb(n, shape, dt=F32):
            return s.enter_context(nc.sbuf_tensor(f"{name}_{n}", shape, dt))

        def sem(n):
            return s.enter_context(nc.semaphore(f"{name}_{n}"))

        w1 = [sb(f"w1_{k}", [P, FF]) for k in range(2)]
        w1_hi = [sb(f"w1_hi{k}", [P, FF], F32R) for k in range(2)]
        w1_lo = [sb(f"w1_lo{k}", [P, FF], F32R) for k in range(2)]
        w2 = [sb(f"w2_{k}", [P, FC, D]) for k in range(2)]
        b1_c = [sb(f"b1_{k}", [P, FC]) for k in range(2)]
        b2_b = [sb(f"b2_{k}", [P, D]) for k in range(2)]
        rows = [sb(f"rows{k}", [P, 2, D]) for k in range(RING)]
        xT_hi = [sb(f"xT_hi{k}", [P, G], F32R) for k in range(2)]
        xT_lo = [sb(f"xT_lo{k}", [P, G], F32R) for k in range(2)]
        hid = [sb(f"hid{k}", [P, FC, G]) for k in range(2)]
        res = [sb(f"res{k}", [P, 2, D]) for k in range(2)]
        back = [sb(f"back{k}", [P, D]) for k in range(8)] if which else []
        back_i = [sb(f"back_i{k}", [P, 8], I32) for k in range(4)]
        part = [sb(f"part{k}", [P, 2, D]) for k in range(2)]
        ps_x = [s.enter_context(nc.psum_tensor(f"{name}_ps_x{k}", [P, 512], F32)) for k in range(2)]
        ps_h = [s.enter_context(nc.psum_tensor(f"{name}_ps_h{k}", [P, FC, G], F32)) for k in range(2)]
        ps_o = [s.enter_context(nc.psum_tensor(f"{name}_ps_o{k}", [P, 512], F32)) for k in range(2)]
        S = {n: sem(n) for n in ("w_hi", "w_lo", "rows", "turned", "xhi", "xlo", "up", "gelu", "down", "part",
                                 "out", "added", "index")}
        s_w = [sem(f"w{k}") for k in range(2)]
        s_in = [sem(f"in{k}") for k in range(RING)] if routed else []
        s_put = [sem(f"put{k}") for k in range(2)]
        s_back = [sem(f"back{k}") for k in range(8)] if which else []
        block = s.enter_context(nc.Block())

        def live(i, k):
            return not isinstance(i, int) or 0 <= BODY * i + k < GROUPS

        def group(i, k):
            return i * BODY + k

        def expert(i, k):
            return i * 2 + k // EACH if routed else 0

        def opens(k):
            return k % EACH == 0

        def side(w):
            return (w // EACH) % 2 if routed else 0

        def gathered(k):
            per = BODY * 2 if which == 2 else BODY * TILES // GROUPS
            return range(k * per // BODY, (k + 1) * per // BODY)

        def tile(i, t):
            return i * (BODY * TILES // GROUPS) + t

        def round_of(i, t, ring):
            return i * (BODY * TILES // GROUPS // ring) + t // ring

        def dram_rows(t, i, k):
            return t[bass.ds(group(i, k) * G, G), :].rearrange("(s p) d -> p s d", p=P)

        @block.sync
        def _(sp):
            if which == 0:
                sp.dma_start(part[0][:, 0, :], bs2.rearrange("(o d) -> o d", o=1).to_broadcast([P, D])).then_inc(S["index"], 16)

            def step(i, k):
                a = k + 4
                if opens(a) and live(i, a):
                    e, c = expert(i, a), side(a)
                    need(sp, S["w_lo"], e - 1)
                    need_apart(sp, S["down"], group(i, a) - EACH)
                    need_apart(sp, S["out"], group(i, a) - EACH)
                    src = [t[bass.ds(e, 1)] for t in (W1, b1, W2, b2)] if routed else [W1, b1, W2, b2]
                    if routed:
                        src = [src[0].rearrange("o d f -> (o d) f"), src[1].rearrange("o (c p) -> p (o c)", p=P),
                               src[2].rearrange("o (c p) d -> p (o c) d", p=P), src[3].to_broadcast([P, D])]
                    else:
                        src = [src[0], src[1].rearrange("(c p) -> p c", p=P), src[2].rearrange("(c p) d -> p c d", p=P),
                               src[3].rearrange("(o d) -> o d", o=1).to_broadcast([P, D])]
                    for dst, one in zip((w1[c][:, :], b1_c[c][:, :], w2[c][:, :, :], b2_b[c][:, :]), src):
                        sp.dma_start(dst, one, allow_slow_non_contiguous=True).then_inc(s_w[c], 16)
                if routed and live(i, k + 4):
                    need(sp, S["turned"], group(i, k + 4) - RING + 1)
                    sp.dma_start(rows[(k + 4) % RING][:, :, :],
                                 dram_rows(sent[which], i, k + 4)).then_inc(s_in[(k + 4) % RING], 16)
                if live(i, k - 1):
                    need(sp, S["out"], group(i, k))
                    dst = dram_rows(answered[which], i, k - 1) if routed else dram_rows(out, i, k - 1)
                    sp.dma_start(dst, res[(k - 1) % 2][:, :, :]).then_inc(s_put[(k - 1) % 2], 16)

            pipelined(sp, step, BODY, FIRST, LAST, 4, GROUPS + 2)
            for k in range(2):
                sp.wait_ge(s_put[k], 16 * GROUPS // 2)

        @block.tensor
        def _(pe):
            def step(i, k):
                if live(i, k + 1):
                    c = (k + 1) % 2
                    if routed:
                        pe.wait_ge(s_in[(k + 1) % RING], (i * (BODY // RING) + (k + 1) // RING + 1) * 16)
                    else:
                        need(pe, S["rows"], group(i, k + 1) + 1)
                    need(pe, S["xlo"], group(i, k))
                    for b in range(2):
                        mm = nc.tensor.transpose(ps_x[c][:, b * P:(b + 1) * P], rows[(k + 1) % RING][:, b, :], ident[:, :])
                    mm.then_inc(S["turned"], 1)
                if live(i, k):
                    c, w = k % 2, side(k)
                    need(pe, S["xlo"], group(i, k) + 1)
                    need(pe, S["w_lo"], expert(i, k) + 1)
                    need(pe, S["gelu"], group(i, k) - 1)
                    for f in range(FC):
                        hi, lo = w1_hi[w][:, f * P:(f + 1) * P], w1_lo[w][:, f * P:(f + 1) * P]
                        nc.tensor.matmul(ps_h[c][:, f, :], hi, xT_hi[c][:, :], start=True, stop=False)
                        nc.tensor.matmul(ps_h[c][:, f, :], lo, xT_hi[c][:, :], start=False, stop=False)
                        mm = nc.tensor.matmul(ps_h[c][:, f, :], hi, xT_lo[c][:, :], start=False, stop=True)
                    mm.then_inc(S["up"], 1)
                if live(i, k - 1):
                    c, w = (k - 1) % 2, side(k - 1)
                    need(pe, S["gelu"], group(i, k))
                    need(pe, S["out"], group(i, k) - 2)
                    for b in range(2):
                        for f in range(FC):
                            mm = nc.tensor.matmul(ps_o[c][:, b * D:(b + 1) * D], hid[c][:, f, b * P:(b + 1) * P],
                                                  w2[w][:, f, :], start=(f == 0), stop=(f == FC - 1))
                    mm.then_inc(S["down"], 1)

            pipelined(pe, step, BODY, FIRST, LAST, 4, GROUPS + 2)

        @block.scalar
        def _(act):
            def step(i, k):
                if live(i, k + 1):
                    c = (k + 1) % 2
                    need(act, S["turned"], group(i, k) + 2)
                    need(act, S["up"], group(i, k))
                    nc.scalar.activation(xT_hi[c][:, :], ps_x[c][:, 0:G], ACT.Copy).then_inc(S["xhi"], 1)
                if live(i, k):
                    c = k % 2
                    need(act, S["up"], group(i, k) + 1)
                    need(act, S["down"], group(i, k) - 1)
                    for f in range(FC):
                        ins = nc.scalar.activation(hid[c][:, f, :], ps_h[c][:, f, :], ACT.Gelu, bias=b1_c[side(k)][:, f:f + 1])
                    ins.then_inc(S["gelu"], 1)

            pipelined(act, step, BODY, FIRST, LAST, 4, GROUPS + 2)

        @block.vector
        def _(dve):
            def step(i, k):
                a = k + 2
                if opens(a) and live(i, a):
                    c = side(a)
                    e = expert(i, a)
                    dve.wait_ge(s_w[c], (i + a // EACH // 2 + 1) * LOADS if routed else LOADS)
                    need(dve, S["up"], group(i, a) - EACH)
                    nc.vector.tensor_copy(w1_hi[c][:, :], w1[c][:, :]).then_inc(S["w_hi"], 1)
                    dve.wait_ge(S["w_hi"], e + 1)
                    nc.vector.tensor_tensor(w1_lo[c][:, :], w1[c][:, :], w1_hi[c][:, :].bitcast(F32), ALU.subtract).then_inc(S["w_lo"], 1)
                if not routed and live(i, k + 2):
                    need(dve, S["turned"], group(i, k) + 1)
                    for b in range(2):
                        t = tile(i, 2 * (k + 2) + b)
                        ins = nc.vector.tensor_scalar(rows[k % 2][:, b, :], h_sb[:, bass.ds(t * D, D)],
                                                      norm2[:, bass.ds(t * 2, 1)], norm2[:, bass.ds(t * 2 + 1, 1)],
                                                      ALU.subtract, ALU.mult)
                    ins.then_inc(S["rows"], 1)
                if live(i, k + 1):
                    c = (k + 1) % 2
                    need(dve, S["xhi"], group(i, k) + 2)
                    nc.vector.tensor_tensor(xT_lo[c][:, :], ps_x[c][:, 0:G], xT_hi[c][:, :].bitcast(F32), ALU.subtract).then_inc(S["xlo"], 1)
                if which == 1 and live(i, k - 1):
                    for t in gathered(k - 1):
                        n = tile(i, t)
                        dve.wait_ge(s_back[t % 8], (round_of(i, t, 8) + 1) * 16)
                        a = acc[:, bass.ds(n * D, D)]
                        nc.vector.scalar_tensor_tensor(a, back[t % 8][:, :], gates[:, bass.ds(n * 2, 1)], a,
                                                       ALU.mult, ALU.add).then_inc(S["added"], 1)
                if live(i, k - 1):
                    c = (k - 1) % 2
                    if which == 2:
                        need(dve, S["out"], group(i, k) - 2)
                        for b in range(2):
                            t = 2 * (k - 1) + b
                            n = tile(i, t)
                            dve.wait_ge(s_back[t % 8], (round_of(i, t, 8) + 1) * 16)
                            ins = nc.vector.scalar_tensor_tensor(part[c][:, b, :], back[t % 8][:, :], gates[:, bass.ds(n * 2 + 1, 1)],
                                                                 acc[:, bass.ds(n * D, D)], ALU.mult, ALU.add)
                        ins.then_inc(S["part"], 1)
                    need(dve, S["down"], group(i, k))
                    need(dve, s_put[c], (i * (BODY // 2) + (k - 1) // 2) * 16)
                    if which == 2:
                        need(dve, S["part"], group(i, k))
                        plus = part[c][:, :, :]
                    else:
                        plus = b2_b[side(k - 1)][:, :].unsqueeze(1).to_broadcast([P, 2, D])
                    nc.vector.tensor_tensor(res[c][:, :, :], ps_o[c][:, 0:G].rearrange("p (b d) -> p b d", b=2), plus,
                                            ALU.add).then_inc(S["out"], 1)

            pipelined(dve, step, BODY, FIRST, LAST, 4, GROUPS + 2)

        @block.gpsimd
        def _(pool):
            if which == 0:
                pool.wait_ge(S["index"], 16)
                per = TILES // 16
                with pool.Fori(0, 16) as i:
                    at = bass.ds(i * (per * D), per * D)
                    nc.gpsimd.tensor_tensor(acc[:, at].rearrange("p (t d) -> p t d", t=per),
                                            h_sb[:, at].rearrange("p (t d) -> p t d", t=per),
                                            part[0][:, 0, :].unsqueeze(1).to_broadcast([P, per, D]), ALU.add).then_inc(S["added"], 1)
                pool.wait_ge(S["added"], 16)
                return
            bank = which - 1

            def step(i, k):
                a = k + (2 if which == 2 else 0)
                if not live(i, a):
                    return
                ts = gathered(a)
                c = a % (4 if which == 2 else 2)
                if which == 2:
                    need(pool, S["part"], group(i, a) - 3)
                else:
                    need(pool, S["added"], tile(i, gathered(k - 1)[0]))
                nc.gpsimd.tensor_copy(back_i[c][:, 0:2 * len(ts)], slots[:, bass.ds(tile(i, ts[0]) * 2, 2 * len(ts))]).then_inc(S["index"], 1)
                need_apart(pool, S["index"], group(i, a) + 1)
                for n, t in enumerate(ts):
                    if which == 1:
                        need_apart(pool, S["added"], tile(i, t) - 7)
                    nc.gpsimd.indirect_dma_start(back[t % 8][:, :], None, answered[bank],
                                                 bass.IndirectOffsetOnAxis(ap=back_i[c][:, 2 * n + bank:2 * n + bank + 1], axis=0)
                                                 ).then_inc(s_back[t % 8], 16)

            pipelined(pool, step, BODY, FIRST, LAST, 4, GROUPS + 2)



PCHAIN = 6
VCHAIN = 74

_INS = ["x", "L0_tok_weight", "L0_tok_num_value", "L0_tok_is_num", "L0_attn_Wq", "L0_attn_Wkv", "L0_attn_scale",
        "L0_attn_mix_pre", "L0_attn_mix_post", "L0_attn_Wout", "L0_attn_bout", "L0_ffn_Wr_sp", "L0_ffn_br_sp",
        "L0_ffn_Wr_fq", "L0_ffn_br_fq", "L0_ffn_Ws1", "L0_ffn_bs1", "L0_ffn_Ws2", "L0_ffn_bs2", "L0_ffn_W1_sp",
        "L0_ffn_b1_sp", "L0_ffn_W2_sp", "L0_ffn_b2_sp", "L0_ffn_W1_fq", "L0_ffn_b1_fq", "L0_ffn_W2_fq", "L0_ffn_b2_fq"]


def kernel(**inputs):
    import numpy as np
    import concourse.bacc as bacc
    from concourse.bass_utils import run_bass_kernel_spmd

    nc = bacc.Bacc("TRN2", target_bir_lowering=False, num_devices=1)
    arrays, args = {}, []
    for name in _INS:
        a = np.ascontiguousarray(inputs[name])
        arrays[f"in_{name}"] = a
        args.append(nc.dram_tensor(f"in_{name}", a.shape, mybir.dt.from_np(a.dtype), kind="ExternalInput").ap())
    out = nc.dram_tensor("out_0", (B, N, D), F32, kind="ExternalOutput").ap()
    build(nc, *args, out)
    r = run_bass_kernel_spmd(nc, [arrays], core_ids=[0])
    return r.results[0]["out_0"]
```

```python
from contextlib import ExitStack

import concourse.bass as bass
from concourse import mybir

F32 = mybir.dt.float32
F32R = mybir.dt.float32r
BF16 = mybir.dt.bfloat16
I32 = mybir.dt.int32
U8 = mybir.dt.uint8
ALU = mybir.AluOpType
ACT = mybir.ActivationFunctionType
X_AXIS = mybir.AxisListType.X

P = 128
VOCAB, D = 12500, 128
B, N = 128, 128
TILES = B * N // P
H, DH = 8, 64
HD = H * DH
HC = HD // P
E, FF = 8, 512
FC = FF // P
CAP = 1280
ROWS = E * CAP
BANKS = 2
RE = BANKS * E
EPS = 1e-5
MASK_VAL = -1e-9
TWO_PI_HI = 6.28125
TWO_PI_LO = 0.0019353071795864769
INV_TWO_PI = 0.15915494309189535
ROUND = 12582912.0
PI_BELOW = 3.1415925
DROPPED = 1 << 20

VP = 125
VR = VOCAB // VP
VC = 10


def need(eng, sem, count, most=None):
    if isinstance(count, int):
        if most is not None:
            count = min(count, most)
        if count <= 0:
            return
    eng.wait_ge(sem, count)


def need_apart(eng, sem, count):
    need(eng, sem, count)
    if not isinstance(count, int):
        eng.nop(nofuse=True)


class Chain:

    def __init__(self, eng, sem):
        self.eng, self.sem, self.n, self.at = eng, sem, 0, None

    def inc(self, ins):
        self.n += 1
        ins.then_inc(self.sem, 1)

    def wait(self, apart=False):
        if self.at is None:
            self.eng.wait_ge(self.sem, self.n)
        else:
            i, first, per, before = self.at
            self.eng.wait_ge(self.sem, i * per + (self.n - first * per))
            if apart:
                self.eng.nop(nofuse=True)

    def __call__(self, ins):
        self.inc(ins)
        self.wait()

    def enter(self, i, first, per):
        self.at = (i, first, per, self.n)

    def leave(self, rounds):
        _, _, per, before = self.at
        assert self.n - before == per, (self.n - before, per)
        self.n = before + per * rounds
        self.at = None


def pipelined(eng, step, body, first, last, lead, end, chain=None, per=0):
    for t in range(-lead, first * body):
        step(0, t)
    with eng.Fori(first, last) as i:
        if chain:
            chain.enter(i, first, per)
        for k in range(body):
            step(i, k)
        if chain:
            chain.leave(last - first)
    for t in range(last * body, end):
        step(0, t)


def build(nc, x, weight, num_value, is_num, Wq, Wkv, scale, mix_pre, mix_post, Wout, bout,
          Wr_sp, br_sp, Wr_fq, br_fq, Ws1, bs1, Ws2, bs2,
          W1_sp, b1_sp, W2_sp, b2_sp, W1_fq, b1_fq, W2_fq, b2_fq, out):
    table = nc.dram_tensor("table", (VOCAB, D), F32).ap()
    sent = [nc.dram_tensor(f"sent_{b}", (ROWS, D), F32).ap() for b in ("sp", "fq")]
    answered = [nc.dram_tensor(f"answered_{b}", (ROWS, D), F32).ap() for b in ("sp", "fq")]
    with ExitStack() as whole:
        def keep(name, shape, dt=F32):
            return whole.enter_context(nc.sbuf_tensor(name, shape, dt))

        ident = keep("ident", [P, P])
        h_sb = keep("h_sb", [P, TILES * D])
        ids = keep("ids", [P, B], I32)
        slots = keep("slots", [P, TILES * BANKS], I32)
        gates = keep("gates", [P, TILES * BANKS])
        norm2 = keep("norm2", [P, TILES * 2])
        with ExitStack() as s:
            mats = {n: s.enter_context(nc.sbuf_tensor(n, [P, H * D], F32R))
                    for n in ("M_hi", "M_lo", "N_hi", "N_lo")}
            masked = [s.enter_context(nc.sbuf_tensor(f"masked{k}", [P, H * N], F32)) for k in range(2)]
            off_diag = s.enter_context(nc.sbuf_tensor("off_diag", [P, N], I32))
            setup(nc, x, weight, num_value, is_num, Wq, Wkv, scale, mix_pre, mix_post, Wout,
                  table, sent, ident, ids, mats, masked, off_diag)
            attention(nc, bout, Wr_sp, br_sp, Wr_fq, br_fq, table, sent, ident, h_sb, ids, slots,
                      gates, norm2, mats, masked, off_diag)
        acc = keep("acc", [P, TILES * D])
        for which, weights in enumerate(((W1_sp, b1_sp, W2_sp, b2_sp), (W1_fq, b1_fq, W2_fq, b2_fq), (Ws1, bs1, Ws2, bs2))):
            feed_forward(nc, which, *weights, bs2, sent, answered, ident, h_sb, slots, gates, norm2, acc,
                         out.rearrange("b n d -> (b n) d"))


def setup(nc, x, weight, num_value, is_num, Wq, Wkv, scale, mix_pre, mix_post, Wout,
          table, sent, ident, ids, mats, masked, off_diag):
    CH = VC * D
    ZR = 40
    chunks = VR // VC
    with ExitStack() as s:
        def sb(name, shape, dt=F32):
            return s.enter_context(nc.sbuf_tensor(name, shape, dt))

        def sem(name):
            return s.enter_context(nc.semaphore(name))

        zeros = sb("zeros", [P, ZR * D])
        freq_i = sb("freq_i", [P, D], I32)
        freq = sb("freq", [P, D])
        num_i = sb("num_i", [VP, VR], I32)
        num_f = sb("num_f", [VP, VR])
        isn = sb("isn", [VP, VR], U8)
        rows = [sb(f"rows{k}", [VP, CH]) for k in range(2)]
        angle = [sb(f"angle{k}", [VP, CH]) for k in range(2)]
        turns = sb("turns", [VP, CH])
        sines = [sb(f"sines{k}", [VP, CH]) for k in range(2)]
        mask_c = [sb(f"mask_c{k}", [VP, VC], I32) for k in range(2)]
        num_c = sb("num_c", [VP, VC])
        wq = sb("wq", [P, HD])
        wkv = sb("wkv", [P, 2 * HD])
        wo = sb("wo", [P, HC, D])
        wqT = sb("wqT", [P, HC, P])
        wkT = sb("wkT", [P, HC, P])
        wvT = sb("wvT", [P, HC, P])
        pre = sb("pre", [H, H])
        spre = sb("spre", [H, H])
        sc = sb("sc", [H, 1])
        postT = sb("postT", [H, H])
        head_of = sb("head_of", [H, HD])
        minus = sb("minus", [H, P])
        cpre = sb("cpre", [P, HC, H])
        cpost = sb("cpost", [P, HC, H])
        diag = sb("diag", [P, H])
        mixed = [sb(f"mixed{k}", [P, H, D]) for k in range(2 * HC)]
        idx_i = sb("idx_i", [P, N], I32)
        idx_f = sb("idx_f", [P, N])
        ps_t = [s.enter_context(nc.psum_tensor(f"ps_t{k}", [P, 512], F32)) for k in range(3)]
        ps_m = s.enter_context(nc.psum_tensor("ps_m", [P, H * D], F32))
        ps_n = s.enter_context(nc.psum_tensor("ps_n", [P, H * D], F32))
        ps_c = s.enter_context(nc.psum_tensor("ps_c", [P, 512], F32))
        s_num, s_small, s_zero, s_zeroed = sem("s_num"), sem("s_small"), sem("s_zero"), sem("s_zeroed")
        s_row = [sem(f"s_row{k}") for k in range(2)]
        s_put = [sem(f"s_put{k}") for k in range(2)]
        s_const, s_angle, s_sine, s_done = sem("s_const"), sem("s_angle"), sem("s_sine"), sem("s_done")
        s_turn, s_mixed, s_M, s_hi = sem("s_turn"), sem("s_mixed"), sem("s_M"), sem("s_hi")
        s_coef, s_coefd, s_v = sem("s_coef"), sem("s_coefd"), sem("s_v")
        w_t = weight.rearrange("(p r) d -> p (r d)", p=VP)
        t_t = table.rearrange("(p r) d -> p (r d)", p=VP)
        fills = []
        for b in range(BANKS):
            z_t = sent[b].rearrange("(p n r) d -> n p (r d)", p=P, r=ZR)
            fills += [z_t[n] for n in range(ROWS // P // ZR)]
        block = s.enter_context(nc.Block())

        @block.sync
        def _(sp):
            sp.dma_start(num_i[:, :], num_value.rearrange("(p r) -> p r", p=VP)).then_inc(s_num, 16)
            sp.dma_start(isn[:, :], is_num.rearrange("(p r) -> p r", p=VP)).then_inc(s_num, 16)
            for dst, src in ((idx_i[:, :], x), (wq[:, :], Wq), (wkv[:, :], Wkv),
                             (wo[:, :, :], Wout.rearrange("(c p) n -> p c n", p=P)),
                             (pre[:, :], mix_pre), (postT[:, :], mix_post.rearrange("h g -> g h")),
                             (sc[:, :], scale.rearrange("(h o) -> h o", o=1))):
                sp.dma_start(dst, src, allow_slow_non_contiguous=True).then_inc(s_small, 16)
            for k in range(2):
                sp.dma_start(rows[k][:, :], w_t[:, k * CH:(k + 1) * CH]).then_inc(s_row[k], 16)
            with sp.Fori(1, chunks // 2) as i:
                for k in range(2):
                    sp.wait_ge(s_put[k], 16 * i)
                    sp.dma_start(rows[k][:, :], w_t[:, bass.ds(i * (2 * CH) + k * CH, CH)]).then_inc(s_row[k], 16)
            sp.wait_ge(s_zero, 1)
            for fill in fills:
                sp.dma_start(fill, zeros[:, :]).then_inc(s_zeroed, 16)
            sp.wait_ge(s_zeroed, 16 * len(fills))

        @block.gpsimd
        def _(pool):
            nc.gpsimd.memset(ident[:, :], 0.0).then_inc(s_const, 1)
            nc.gpsimd.memset(off_diag[:, :], 1).then_inc(s_const, 1)
            nc.gpsimd.memset(head_of[:, :], 1.0).then_inc(s_const, 1)
            nc.gpsimd.iota(freq_i[:, :], [[1, D]], base=1, channel_multiplier=0).then_inc(s_const, 1)
            nc.gpsimd.memset(minus[:, :], MASK_VAL).then_inc(s_const, 1)
            pool.wait_ge(s_const, 5)
            nc.gpsimd.affine_select(out=ident[:, :], in_=ident[:, :], compare_op=ALU.not_equal, fill=1.0,
                                    base=0, pattern=[[-1, P]], channel_multiplier=1).then_inc(s_const, 1)
            nc.gpsimd.affine_select(out=off_diag[:, :], in_=off_diag[:, :], compare_op=ALU.not_equal, fill=0,
                                    base=0, pattern=[[-1, P]], channel_multiplier=1).then_inc(s_const, 1)
            nc.gpsimd.affine_select(out=head_of[:, :], in_=head_of[:, :], compare_op=ALU.is_ge, fill=0.0,
                                    base=0, pattern=[[1, HD]], channel_multiplier=-DH).then_inc(s_const, 1)
            pool.wait_ge(s_const, 8)
            nc.gpsimd.affine_select(out=head_of[:, :], in_=head_of[:, :], compare_op=ALU.is_ge, fill=0.0,
                                    base=DH - 1, pattern=[[-1, HD]], channel_multiplier=DH).then_inc(s_const, 1)
            nc.gpsimd.memset(zeros[:, :], 0.0).then_inc(s_zero, 1)

        @block.scalar
        def _(act):
            for n, (ps, hi) in enumerate(((ps_m, "M_hi"), (ps_n, "N_hi"))):
                act.wait_ge(s_M, n + 1)
                nc.scalar.activation(mats[hi][:, :], ps[:, :], ACT.Copy).then_inc(s_hi, 1)
            with act.Fori(0, chunks // 2) as i:
                for k in range(2):
                    act.wait_ge(s_angle, 2 * i + (k + 1))
                    nc.scalar.activation(sines[k][:, :], angle[k][:, :], ACT.Sin).then_inc(s_sine, 1)
                    act.wait_ge(s_done, 2 * i + (k + 1))
                    act.dma_start(t_t[:, bass.ds(i * (2 * CH) + k * CH, CH)], rows[k][:, :]).then_inc(s_put[k], 16)
            for k in range(2):
                act.wait_ge(s_put[k], 16 * (chunks // 2))

        @block.tensor
        def _(pe):
            pe.wait_ge(s_const, 9)
            pe.wait_ge(s_small, 112)
            for c in range(HC):
                nc.tensor.transpose(ps_t[0][:, c * P:(c + 1) * P], wq[:, c * P:(c + 1) * P], ident[:, :])
                nc.tensor.transpose(ps_t[1][:, c * P:(c + 1) * P], wkv[:, c * P:(c + 1) * P], ident[:, :])
                last = nc.tensor.transpose(ps_t[2][:, c * P:(c + 1) * P], wkv[:, HD + c * P:HD + (c + 1) * P], ident[:, :])
            last.then_inc(s_turn, 1)
            pe.wait_ge(s_coef, 1)
            for c in range(HC):
                nc.tensor.matmul(ps_c[:, c * H:(c + 1) * H], head_of[:, c * P:(c + 1) * P], spre[:, :], start=True, stop=True)
                nc.tensor.matmul(ps_c[:, 64 + c * H:64 + (c + 1) * H], head_of[:, c * P:(c + 1) * P], postT[:, :], start=True, stop=True)
            nc.tensor.matmul(ps_c[:, 128:128 + H], minus[:, :], pre[:, :], start=True, stop=True)
            nc.tensor.transpose(ps_c[:, 256:384], idx_f[:, :], ident[:, :]).then_inc(s_coefd, 1)
            for w, (lhs, ps) in enumerate(((wkT, ps_m), (wvT, ps_n))):
                for c in range(HC):
                    pe.wait_ge(s_mixed, w * HC + c + 1)
                    m = mixed[w * HC + c][:, :, :].rearrange("p g d -> p (g d)")
                    for half in range(2):
                        last = nc.tensor.matmul(ps[:, half * 512:(half + 1) * 512], lhs[:, c, :],
                                                m[:, half * 512:(half + 1) * 512], start=(c == 0), stop=(c == HC - 1))
                last.then_inc(s_M, 1)

        @block.vector
        def _(dve):
            link = Chain(dve, s_v)
            dve.wait_ge(s_small, 112)
            link.inc(nc.vector.tensor_copy(idx_f[:, :], idx_i[:, :]))
            nc.vector.tensor_scalar(spre[:, :], pre[:, :], sc[:, 0:1], None, ALU.mult).then_inc(s_coef, 1)
            dve.wait_ge(s_turn, 1)
            for n, dst in enumerate((wqT, wkT, wvT)):
                link.inc(nc.vector.tensor_copy(dst[:, :, :].rearrange("p c n -> p (c n)"), ps_t[n][:, :]))
            dve.wait_ge(s_coefd, 1)
            link.inc(nc.vector.tensor_copy(cpre[:, :, :].rearrange("p c h -> p (c h)"), ps_c[:, 0:HC * H]))
            link.inc(nc.vector.tensor_copy(cpost[:, :, :].rearrange("p c h -> p (c h)"), ps_c[:, 64:64 + HC * H]))
            link.inc(nc.vector.tensor_copy(diag[:, :], ps_c[:, 128:128 + H]))
            link(nc.vector.tensor_copy(ids[:, :], ps_c[:, 256:384]))
            for w, (src, co) in enumerate(((wqT, cpre), (wo, cpost))):
                for c in range(HC):
                    nc.vector.tensor_tensor(mixed[w * HC + c][:, :, :], src[:, c, :].unsqueeze(1).to_broadcast([P, H, D]),
                                            co[:, c, :].unsqueeze(2).to_broadcast([P, H, D]), ALU.mult).then_inc(s_mixed, 1)
            for k in range(2):
                link.inc(nc.vector.tensor_copy(masked[k][:, :].rearrange("p (g j) -> p g j", g=H),
                                               diag[:, :].unsqueeze(2).to_broadcast([P, H, N])))
            for n, (ps, m) in enumerate(((ps_m, "M"), (ps_n, "N"))):
                dve.wait_ge(s_hi, n + 1)
                link.inc(nc.vector.tensor_tensor(mats[m + "_lo"][:, :], ps[:, :], mats[m + "_hi"][:, :].bitcast(F32), ALU.subtract))
            dve.wait_ge(s_const, 4)
            dve.wait_ge(s_num, 32)
            link.inc(nc.vector.tensor_copy(freq[:, :], freq_i[:, :]))
            link(nc.vector.tensor_scalar(num_f[:, :], num_i[:, :], 0.001, None, ALU.mult))
            per = 14
            with dve.Fori(0, chunks // 2) as i:
                link.enter(i, 0, per)
                for k in range(2):
                    a = angle[k][:, :]
                    link.inc(nc.vector.tensor_copy(mask_c[k][:, :], isn[:, bass.ds(i * (2 * VC) + k * VC, VC)]))
                    link(nc.vector.tensor_copy(num_c[:, :], num_f[:, bass.ds(i * (2 * VC) + k * VC, VC)]))
                    link(nc.vector.tensor_tensor(a.rearrange("p (r d) -> p r d", r=VC),
                                                 freq[0:VP, :].unsqueeze(1).to_broadcast([VP, VC, D]),
                                                 num_c[:, :].unsqueeze(2).to_broadcast([VP, VC, D]), ALU.mult))
                    link(nc.vector.tensor_scalar(turns[:, :], a, INV_TWO_PI, ROUND, ALU.mult, ALU.add))
                    link(nc.vector.tensor_scalar(turns[:, :], turns[:, :], ROUND, None, ALU.subtract))
                    link(nc.vector.scalar_tensor_tensor(a, turns[:, :], -TWO_PI_HI, a, ALU.mult, ALU.add))
                    link(nc.vector.scalar_tensor_tensor(a, turns[:, :], -TWO_PI_LO, a, ALU.mult, ALU.add))
                    nc.vector.tensor_scalar(a, a, PI_BELOW, -PI_BELOW, ALU.min, ALU.max).then_inc(s_angle, 1)
                    dve.wait_ge(s_row[k], 16 * i + 16)
                    need_apart(dve, s_sine, 2 * i + (k + 1))
                    nc.vector.copy_predicated(rows[k][:, :].rearrange("p (r d) -> p r d", r=VC),
                                              mask_c[k][:, :].unsqueeze(2).to_broadcast([VP, VC, D]),
                                              sines[k][:, :].rearrange("p (r d) -> p r d", r=VC)).then_inc(s_done, 1)
                link.leave(chunks // 2)


def attention(nc, bout, Wr_sp, br_sp, Wr_fq, br_fq, table, sent, ident, h_sb, ids, slots, gates, norm2,
              mats, masked, off_diag):
    BODY, FIRST, LAST, LEAD, END = 16, 2, 7, 12, TILES + 21
    GROUPS, QUADS = TILES // 2, TILES // 4
    BATCH = 8
    LOGIT_COL, CUM_COL = D, D + BATCH * RE
    with ExitStack() as s:
        def sb(name, shape, dt=F32):
            return s.enter_context(nc.sbuf_tensor(name, shape, dt))

        def pb(name, cols):
            return s.enter_context(nc.psum_tensor(name, [P, cols], F32))

        def sem(name):
            return s.enter_context(nc.semaphore(name))

        got = [sb(f"got{k}", [P, D]) for k in range(8)]
        gi = [sb(f"gi{k}", [P, 4], I32) for k in range(2)]
        x1 = [sb(f"x1_{k}", [P, 2 * D]) for k in range(2)]
        xT_hi = sb("xT_hi", [P, 4, 2 * N], F32R)
        xT_lo = sb("xT_lo", [P, 4, 2 * N], F32R)
        w_hi = [sb(f"w_hi{k}", [P, 2, H, N], F32R) for k in range(2)]
        w_lo = [sb(f"w_lo{k}", [P, 2, H, N], F32R) for k in range(2)]
        nmax = [sb(f"nmax{k}", [P, H]) for k in range(2)]
        expd = [sb(f"expd{k}", [P, H * N]) for k in range(2)]
        total = [sb(f"total{k}", [P, H]) for k in range(4)]
        rtotal = [sb(f"rtotal{k}", [P, H]) for k in range(2)]
        prob = [sb(f"prob{k}", [P, H * N]) for k in range(2)]
        probT = [sb(f"probT{k}", [P, H * N]) for k in range(2)]
        u = [sb(f"u{k}", [P, H * D]) for k in range(2)]
        bout_b = sb("bout_b", [P, D])
        x2 = [sb(f"x2_{k}", [P, D]) for k in range(16)]
        x2T = sb("x2T", [P, 4 * N])
        stat = [sb(f"stat{k}", [P, 6]) for k in range(8)]
        mv1 = [sb(f"mv1_{k}", [P, 4, 2]) for k in range(2)]
        mv2 = [sb(f"mv2_{k}", [P, 4, 2]) for k in range(2)]
        var = sb("var", [P, 8])
        rstd = [sb(f"rstd{k}", [P, 8]) for k in range(2)]
        power = sb("power", [P, 8])
        wr = sb("wr", [P, RE])
        br_b = sb("br_b", [P, RE])
        tri = sb("tri", [P, P], BF16)
        ones = sb("ones", [P, P], BF16)
        rank = sb("rank", [P, E])
        rank_i = sb("rank_i", [P, E], I32)
        logits = sb("logits", [P, BATCH * RE])
        work = sb("work", [P, BATCH * RE])
        work2 = sb("work2", [P, BATCH * RE])
        expo = sb("expo", [P, BATCH * RE])
        chosen = sb("chosen", [P, (BATCH + 1) * RE], BF16)
        counts = sb("counts", [P, (BATCH + 1) * RE])
        carry = sb("carry", [P, RE])
        top = sb("top", [P, BATCH * BANKS])
        gate = sb("gate", [P, BATCH * BANKS])
        key = sb("key", [P, BATCH * BANKS])
        place = sb("place", [P, BATCH * BANKS])
        slot = sb("slot", [P, BATCH * BANKS])
        over = sb("over", [P, BATCH * BANKS])
        to_row = [sb(f"to_row{k}", [P, BATCH * BANKS], I32) for k in range(2)]
        ps_s = pb("ps_s", H * N)
        ps_ut = pb("ps_ut", H * D)
        ps_w = [pb(f"ps_w{k}", 512) for k in range(2)]
        ps_x = pb("ps_x", 512)
        ps_o = pb("ps_o", 512)
        names = ("scored", "copied", "maxed", "expd", "rtot", "normed", "turned", "turn_out", "u_made", "u_out",
                 "pv", "h1", "w_made", "w_hi", "w_lo", "x_made", "x_turned", "xhi", "xlo", "stat1", "stat2",
                 "rstd", "x2", "x2_turned", "x2T", "logit", "logit_out", "chosen", "cum", "cum_out", "routed",
                 "gate_in", "gate_exp", "resid", "const", "cload", "chain", "pchain")
        S = {n: sem("a_" + n) for n in names}
        s_got = [sem(f"a_got{k}") for k in range(8)]
        s_sent = [sem(f"a_sent{k}") for k in range(8)]
        block = s.enter_context(nc.Block())

        def live(i, k):
            return not isinstance(i, int) or 0 <= BODY * i + k < TILES

        def tile(i, k):
            return i * BODY + k

        def group(i, k):
            return i * (BODY // 2) + k // 2

        def quad(i, k):
            return i * (BODY // 4) + k // 4

        def batch(i, k):
            return i * (BODY // BATCH) + k // BATCH

        def landed(i, k):
            return (i * (BODY // 8) + k // 8 + 1) * 16

        @block.sync
        def _(sp):
            sp.dma_start(wr[:, 0:E], Wr_sp).then_inc(S["cload"], 16)
            sp.dma_start(wr[:, E:RE], Wr_fq).then_inc(S["cload"], 16)
            sp.dma_start(br_b[:, 0:E], br_sp.rearrange("(o e) -> o e", o=1).to_broadcast([P, E])).then_inc(S["cload"], 16)
            sp.dma_start(br_b[:, E:RE], br_fq.rearrange("(o e) -> o e", o=1).to_broadcast([P, E])).then_inc(S["cload"], 16)
            sp.dma_start(bout_b[:, :], bout.rearrange("(o e) -> o e", o=1).to_broadcast([P, D])).then_inc(S["cload"], 16)

        @block.gpsimd
        def _(pool):
            link = Chain(pool, S["pchain"])
            link.inc(nc.gpsimd.memset(power[:, :], -0.5))
            link.inc(nc.gpsimd.memset(ones[:, :], 1.0))
            link.inc(nc.gpsimd.memset(tri[:, :], 1.0))
            link.inc(nc.gpsimd.iota(rank_i[:, :], [[-1, E]], base=E, channel_multiplier=0))
            link.inc(nc.gpsimd.memset(carry[:, :], 0.0))
            link.inc(nc.gpsimd.memset(chosen[:, :], 0.0))
            for m in (*mv1, *mv2):
                link.inc(nc.gpsimd.memset(m[:, :, :], 1.0))
            link.wait()
            link(nc.gpsimd.affine_select(out=tri[:, :], in_=tri[:, :], compare_op=ALU.is_ge, fill=0.0,
                                         base=0, pattern=[[1, P]], channel_multiplier=-1))
            pool.wait_ge(S["cload"], 80)
            nc.gpsimd.memset(var[:, :], 1.0).then_inc(S["const"], 1)
            pool.wait_ge(S["const"], 1)

            def step(i, k):
                j = k % 4
                if live(i, k - 2):
                    need(pool, S["rtot"], tile(i, k - 1))
                    need(pool, S["turned"], tile(i, k - 3))
                    nc.gpsimd.tensor_tensor(prob[k % 2][:, :].rearrange("p (g j) -> p g j", g=H),
                                            expd[k % 2][:, :].rearrange("p (g j) -> p g j", g=H),
                                            rtotal[k % 2][:, :].unsqueeze(2).to_broadcast([P, H, N]),
                                            ALU.mult).then_inc(S["normed"], 1)
                if live(i, k + 10):
                    if (k + 10) % 4 == 0:
                        q = quad(i, k + 10)
                        if (not isinstance(i, int)) or q >= 2:
                            for b in range(4):
                                pool.wait_ge(s_got[(k + 10 + b) % 8], landed(i, k + 2 + b))
                        link(nc.gpsimd.tensor_copy(gi[((k + 10) // 4) % 2][:, :], ids[:, bass.ds(tile(i, k + 10), 4)]))
                    need(pool, S["x_made"], group(i, k + 2) + 1)
                    need_apart(pool, S["resid"], tile(i, k + 3))
                    nc.gpsimd.indirect_dma_start(
                        got[(k + 10) % 8][:, :], None, table,
                        bass.IndirectOffsetOnAxis(ap=gi[((k + 10) // 4) % 2][:, (k + 10) % 4:(k + 10) % 4 + 1], axis=0),
                    ).then_inc(s_got[(k + 10) % 8], 16)
                if live(i, k + 7):
                    pool.wait_ge(s_got[(k + 7) % 8], landed(i, k + 7))
                    nc.gpsimd.tensor_tensor(h_sb[:, bass.ds(tile(i, k + 7) * D, D)], got[(k + 7) % 8][:, :],
                                            bout_b[:, :], ALU.add).then_inc(S["resid"], 1)
                if j == 0 and (live(i, k + 4) or live(i, k - 8)):
                    if live(i, k + 4):
                        need(pool, S["stat1"], quad(i, k + 4) + 1)
                    if live(i, k - 8):
                        need(pool, S["stat2"], quad(i, k - 8) + 1)
                    need(pool, S["x_made"], group(i, k), GROUPS)
                    need(pool, S["x2"], group(i, k - 12), GROUPS)
                    if not isinstance(i, int):
                        pool.nop(nofuse=True)
                    m1, m2 = mv1[(k // 4 + 1) % 2], mv2[(k // 4) % 2]
                    link.inc(nc.gpsimd.tensor_scalar(var[:, 0:4], m1[:, :, 1], 1.0, EPS, ALU.mult, ALU.add))
                    link(nc.gpsimd.tensor_scalar(var[:, 4:8], m2[:, :, 1], 1.0, EPS, ALU.mult, ALU.add))
                    nc.gpsimd.tensor_tensor(rstd[(k // 4) % 2][:, :], var[:, :], power[:, :], ALU.pow).then_inc(S["rstd"], 1)
                if live(i, k - 21):
                    t = k - 21
                    need_apart(pool, S["routed"], batch(i, t) + 1)
                    for b in range(BANKS):
                        c = (t % BATCH) * BANKS + b
                        nc.gpsimd.indirect_dma_start(
                            sent[b], bass.IndirectOffsetOnAxis(ap=to_row[(t // BATCH) % 2][:, c:c + 1], axis=0),
                            x2[t % 16][:, :], None, bounds_check=ROWS - 1, oob_is_err=False,
                        ).then_inc(s_sent[t // 2 % 8], 16)

            pipelined(pool, step, BODY, FIRST, LAST, LEAD, END, link, PCHAIN)
            for k in range(8):
                pool.wait_ge(s_sent[k], TILES // 16 * 64)

        @block.tensor
        def _(pe):
            pe.wait_ge(S["const"], 1)

            def step(i, k):
                j = k % 4
                if j == 0 and live(i, k - 12):
                    need(pe, S["x2T"], quad(i, k - 12) + 1)
                    need(pe, S["h1"], tile(i, k - 4), TILES)
                    for b in range(4):
                        c = LOGIT_COL + ((k - 12) % BATCH + b) * RE
                        mm = nc.tensor.matmul(ps_o[:, c:c + RE], x2T[:, b * N:(b + 1) * N], wr[:, :], start=True, stop=True)
                    mm.then_inc(S["logit"], 1)
                if k % BATCH == 2 and live(i, k - 18):
                    need(pe, S["chosen"], batch(i, k - 18) + 1)
                    need(pe, S["h1"], tile(i, k - 4), TILES)
                    end = CUM_COL + (BATCH + 1) * RE
                    nc.tensor.matmul(ps_o[:, CUM_COL:end], tri[:, :], chosen[:, :], start=True, stop=False)
                    for d in range(1, BATCH + 1):
                        mm = nc.tensor.matmul(ps_o[:, CUM_COL + d * RE:end], ones[:, :], chosen[:, 0:(BATCH + 1 - d) * RE],
                                              start=False, stop=(d == BATCH))
                    mm.then_inc(S["cum"], 1)
                if live(i, k):
                    m, b = k // 2, k % 2
                    need(pe, S["copied"], tile(i, k))
                    need(pe, S["w_lo"], group(i, k) * 4 + 4)
                    cols = slice(b * N, (b + 1) * N)
                    hi, lo = xT_hi[:, m % 4, cols], xT_lo[:, m % 4, cols]
                    for n, (lhs, rhs) in enumerate(((hi, w_hi), (hi, w_lo), (lo, w_hi))):
                        r = rhs[m % 2][:, b, :, :].rearrange("p g j -> p (g j)")
                        for half in range(2):
                            mm = nc.tensor.matmul(ps_s[:, half * 512:(half + 1) * 512], lhs,
                                                  r[:, half * 512:(half + 1) * 512], start=(n == 0), stop=(n == 2))
                    mm.then_inc(S["scored"], 1)
                if live(i, k - 3):
                    need(pe, S["normed"], tile(i, k - 2))
                    need(pe, S["u_out"], tile(i, k - 3))
                    for g in range(H):
                        mm = nc.tensor.transpose(ps_ut[:, g * N:(g + 1) * N], prob[(k - 3) % 2][:, g * N:(g + 1) * N], ident[:, :])
                    mm.then_inc(S["turned"], 1)
                if k % 2 and live(i, k + 3):
                    m = group(i, k + 3)
                    need(pe, S["x_made"], m + 1)
                    need(pe, S["xlo"], m)
                    need(pe, S["x2T"], quad(i, k - 11) + 1, QUADS)
                    for b in range(2):
                        mm = nc.tensor.transpose(ps_x[:, b * N:(b + 1) * N], x1[((k + 3) // 2) % 2][:, b * D:(b + 1) * D], ident[:, :])
                    mm.then_inc(S["x_turned"], 1)
                if live(i, 2 * (k // 2 + 1)):
                    m = k // 2 + 1
                    need(pe, S["xlo"], group(i, 2 * m) + 1)
                    for q in (2 * (k % 2), 2 * (k % 2) + 1):
                        need(pe, S["w_lo"], group(i, 2 * m) * 4 + q - 1)
                        for g in (2 * q, 2 * q + 1):
                            o = ps_w[q % 2][:, (g % 2) * 256:(g % 2 + 1) * 256]
                            M_hi, M_lo = (mats[n][:, g * D:(g + 1) * D] for n in ("M_hi", "M_lo"))
                            nc.tensor.matmul(o, M_hi, xT_hi[:, m % 4, :], start=True, stop=False)
                            nc.tensor.matmul(o, M_lo, xT_hi[:, m % 4, :], start=False, stop=False)
                            mm = nc.tensor.matmul(o, M_hi, xT_lo[:, m % 4, :], start=False, stop=True)
                        mm.then_inc(S["w_made"], 1)
                if live(i, k - 4):
                    need(pe, S["turn_out"], tile(i, k - 3))
                    need(pe, S["u_out"], tile(i, k - 3))
                    need(pe, S["h1"], tile(i, k - 4))
                    if j == 0 and live(i, k - 12):
                        need(pe, S["logit_out"], quad(i, k - 12) + 1)
                    if k % BATCH == 2 and live(i, k - 18):
                        need(pe, S["cum_out"], batch(i, k - 18) + 1)
                    for g in range(H):
                        mm = nc.tensor.matmul(ps_o[:, 0:D], probT[k % 2][:, g * N:(g + 1) * N],
                                              u[k % 2][:, g * D:(g + 1) * D], start=(g == 0), stop=(g == H - 1))
                    mm.then_inc(S["pv"], 1)
                if live(i, k - 3):
                    m, b = (k - 3) // 2, (k - 3) % 2
                    need(pe, S["turn_out"], tile(i, k - 2))
                    cols = slice(b * N, (b + 1) * N)
                    hi, lo = xT_hi[:, m % 4, cols], xT_lo[:, m % 4, cols]
                    for n, (lhs, rhs) in enumerate(((hi, "N_hi"), (hi, "N_lo"), (lo, "N_hi"))):
                        for half in range(2):
                            mm = nc.tensor.matmul(ps_ut[:, half * 512:(half + 1) * 512], lhs,
                                                  mats[rhs][:, half * 512:(half + 1) * 512], start=(n == 0), stop=(n == 2))
                    mm.then_inc(S["u_made"], 1)
                if j == 2 and live(i, k - 10):
                    need(pe, S["x2"], group(i, k - 10) + 2)
                    need(pe, S["xlo"], group(i, k + 2) + 1, GROUPS)
                    for b in range(4):
                        mm = nc.tensor.transpose(ps_x[:, b * N:(b + 1) * N], x2[(k - 10 + b) % 16][:, :], ident[:, :])
                    mm.then_inc(S["x2_turned"], 1)

            pipelined(pe, step, BODY, FIRST, LAST, LEAD, END)

        @block.scalar
        def _(act):
            def step(i, k):
                j = k % 4

                def exps(heads):
                    for g in heads:
                        ins = nc.scalar.activation(expd[(k - 1) % 2][:, g * N:(g + 1) * N],
                                                   masked[(k - 1) % 2][:, g * N:(g + 1) * N], ACT.Exp,
                                                   bias=nmax[(k - 1) % 2][:, g:g + 1],
                                                   accum_out=total[(k - 1) % 4][:, g:g + 1])
                    return ins

                if live(i, k - 4):
                    need(act, S["u_made"], tile(i, k - 3))
                    need(act, S["pv"], tile(i, k - 5))
                    nc.scalar.activation(u[k % 2][:, :], ps_ut[:, :], ACT.Copy).then_inc(S["u_out"], 1)
                if j == 3 and live(i, k - 11):
                    q = quad(i, k - 11)
                    need(act, S["x2_turned"], q + 1)
                    need(act, S["logit"], q)
                    nc.scalar.activation(x2T[:, :], ps_x[:, :], ACT.Copy).then_inc(S["x2T"], 1)
                if live(i, k - 1):
                    need(act, S["maxed"], tile(i, k))
                    need(act, S["normed"], tile(i, k - 2))
                    exps(range(0, 3))
                if live(i, k - 3):
                    need(act, S["turned"], tile(i, k - 2))
                    need(act, S["pv"], tile(i, k - 4))
                    nc.scalar.activation(probT[(k - 3) % 2][:, :], ps_ut[:, :], ACT.Copy).then_inc(S["turn_out"], 1)
                if live(i, 2 * (k // 2 + 1)):
                    m = k // 2 + 1
                    for q in (2 * (k % 2), 2 * (k % 2) + 1):
                        need(act, S["w_made"], group(i, 2 * m) * 4 + q + 1)
                        need(act, S["scored"], tile(i, 2 * m) - 2)
                        nc.scalar.activation(w_hi[m % 2][:, :, 2 * q:2 * q + 2, :].rearrange("p b g j -> p g b j"),
                                             ps_w[q % 2][:, :].rearrange("p (g b j) -> p g b j", g=2, b=2),
                                             ACT.Copy).then_inc(S["w_hi"], 1)
                if k % 2 and live(i, k + 3):
                    m = group(i, k + 3)
                    need(act, S["x_turned"], m + 1)
                    need(act, S["u_made"], tile(i, k + 3) - 6)
                    nc.scalar.activation(xT_hi[:, ((k + 3) // 2) % 4, :], ps_x[:, 0:2 * N], ACT.Copy).then_inc(S["xhi"], 1)
                if live(i, k - 1):
                    exps(range(3, 8)).then_inc(S["expd"], 1)
                if k % BATCH == 1 and live(i, k - 17):
                    need(act, S["gate_in"], batch(i, k - 17) + 1)
                    nc.scalar.activation(expo[:, :], work[:, :], ACT.Exp).then_inc(S["gate_exp"], 1)

            pipelined(act, step, BODY, FIRST, LAST, LEAD, END)

        @block.vector
        def _(dve):
            link = Chain(dve, S["chain"])
            dve.wait_ge(S["const"], 1)
            link(nc.vector.tensor_copy(rank[:, :], rank_i[:, :]))

            def by_expert(t):
                return t[:, :].rearrange("p (n e) -> p n e", e=E)

            def over_experts(t):
                return t[:, :].unsqueeze(2).to_broadcast([P, BATCH * BANKS, E])

            def step(i, k):
                j = k % 4
                if live(i, k - 2):
                    need(dve, S["expd"], tile(i, k - 1))
                    need(dve, S["normed"], tile(i, k - 3))
                    nc.vector.reciprocal(rtotal[k % 2][:, :], total[(k - 2) % 4][:, :]).then_inc(S["rtot"], 1)
                if j == 0 and live(i, k - 12):
                    c = (k - 12) % BATCH * RE
                    need(dve, S["logit"], quad(i, k - 12) + 1)
                    nc.vector.tensor_tensor(logits[:, c:c + 4 * RE].rearrange("p (t e) -> p t e", t=4),
                                            ps_o[:, LOGIT_COL + c:LOGIT_COL + c + 4 * RE].rearrange("p (t e) -> p t e", t=4),
                                            br_b[:, :].unsqueeze(1).to_broadcast([P, 4, RE]), ALU.add).then_inc(S["logit_out"], 1)
                if k % BATCH == 2 and live(i, k - 18):
                    need(dve, S["cum"], batch(i, k - 18) + 1)
                    nc.vector.tensor_tensor(counts[:, :].rearrange("p (t e) -> p t e", e=RE),
                                            ps_o[:, CUM_COL:CUM_COL + (BATCH + 1) * RE].rearrange("p (t e) -> p t e", e=RE),
                                            carry[:, :].unsqueeze(1).to_broadcast([P, BATCH + 1, RE]), ALU.add).then_inc(S["cum_out"], 1)
                route = iter(router(i, k))
                if live(i, k):
                    need(dve, S["scored"], tile(i, k + 1))
                    need_apart(dve, S["expd"], tile(i, k - 1))
                    nc.vector.copy_predicated(masked[k % 2][:, :].rearrange("p (g j) -> p g j", g=H),
                                              off_diag[:, :].unsqueeze(1).to_broadcast([P, H, N]),
                                              ps_s[:, :].rearrange("p (g j) -> p g j", g=H)).then_inc(S["copied"], 1)
                next(route, None)
                if live(i, k):
                    need(dve, S["copied"], tile(i, k + 1))
                    nc.vector.tensor_reduce(nmax[k % 2][:, :], masked[k % 2][:, :].rearrange("p (g j) -> p g j", g=H),
                                            X_AXIS, ALU.max, negate=True).then_inc(S["maxed"], 1)
                next(route, None)
                if live(i, 2 * (k // 2 + 1)):
                    m = k // 2 + 1
                    for q in (2 * (k % 2), 2 * (k % 2) + 1):
                        need(dve, S["w_hi"], group(i, 2 * m) * 4 + q + 1)
                        dst, hi = (w[m % 2][:, :, 2 * q:2 * q + 2, :].rearrange("p b g j -> p g b j") for w in (w_lo, w_hi))
                        nc.vector.tensor_tensor(dst, ps_w[q % 2][:, :].rearrange("p (g b j) -> p g b j", g=2, b=2),
                                                hi.bitcast(F32), ALU.subtract).then_inc(S["w_lo"], 1)
                next(route, None)
                if j in (1, 2) and live(i, k - 8 - (j == 1)):
                    t0 = k - 8 - (j == 1)
                    if j == 1:
                        need(dve, S["rstd"], quad(i, k) + 2)
                    need(dve, s_sent[t0 // 2 % 8], i * 64 + t0 // 16 * 64)
                    for b in range(2):
                        t = t0 + b
                        a = ((t // 4) % 2, t % 4)
                        mean, rs = mv2[a[0]][:, a[1], 0:1], rstd[a[0]][:, 4 + a[1]:5 + a[1]]
                        ins = nc.vector.tensor_scalar(x2[t % 16][:, :], h_sb[:, bass.ds(tile(i, t) * D, D)], mean, rs,
                                                      ALU.subtract, ALU.mult)
                    ins.then_inc(S["x2"], 1)
                    if j == 2:
                        n2 = norm2[:, bass.ds(tile(i, k - 10) * 2, 8)].rearrange("p (t c) -> p t c", c=2)
                        a = ((k - 10) // 4) % 2
                        link.inc(nc.vector.tensor_copy(n2[:, :, 0], mv2[a][:, :, 0]))
                        link.inc(nc.vector.tensor_copy(n2[:, :, 1], rstd[a][:, 4:8]))
                if k % 2 == 0 and live(i, k + 4):
                    need(dve, S["rstd"], quad(i, k) + 2)
                    need(dve, S["x_turned"], group(i, k + 2))
                    for b in range(2):
                        t = k + 4 + b
                        a = ((t // 4) % 2, t % 4)
                        mean, rs = mv1[a[0]][:, a[1], 0:1], rstd[(t // 4 - 1) % 2][:, a[1]:a[1] + 1]
                        ins = nc.vector.tensor_scalar(x1[((k + 4) // 2) % 2][:, b * D:(b + 1) * D], got[t % 8][:, :], mean, rs,
                                                      ALU.subtract, ALU.mult)
                    ins.then_inc(S["x_made"], 1)
                if live(i, k + 8):
                    dve.wait_ge(s_got[k % 8], landed(i, k + 8))
                    link.inc(nc.vector.bn_stats(stat[j][:, :], got[k % 8][:, :]))
                if live(i, k - 4):
                    hk = h_sb[:, bass.ds(tile(i, k - 4) * D, D)]
                    need(dve, S["pv"], tile(i, k - 3))
                    need(dve, S["resid"], tile(i, k - 3))
                    nc.vector.tensor_tensor(hk, ps_o[:, 0:D], hk, ALU.add).then_inc(S["h1"], 1)
                if live(i, k + 8):
                    link.wait(apart=True)
                    ins = nc.vector.bn_aggr(mv1[((k + 8) // 4) % 2][:, k % 4, :], stat[j][:, :])
                    if j == 3:
                        ins.then_inc(S["stat1"], 1)
                    else:
                        link.inc(ins)
                if live(i, k - 4):
                    need_apart(dve, S["h1"], tile(i, k - 3))
                    link.inc(nc.vector.bn_stats(stat[4 + j][:, :], hk))
                if k % 2 and live(i, k + 3):
                    need(dve, S["xhi"], group(i, k + 3) + 1)
                    c = ((k + 3) // 2) % 4
                    nc.vector.tensor_tensor(xT_lo[:, c, :], ps_x[:, 0:2 * N], xT_hi[:, c, :].bitcast(F32), ALU.subtract).then_inc(S["xlo"], 1)
                if live(i, k - 4):
                    link.wait(apart=True)
                    ins = nc.vector.bn_aggr(mv2[((k - 4) // 4) % 2][:, k % 4, :], stat[4 + j][:, :])
                    if j == 3:
                        ins.then_inc(S["stat2"], 1)
                    else:
                        link.inc(ins)
                for _ in route:
                    pass

            def router(i, k):
                at = k % BATCH
                if not live(i, k - 16 - at):
                    return
                if at == 0:
                    need(dve, S["logit_out"], quad(i, k - 12) + 1)
                    link.inc(nc.vector.tensor_reduce(top[:, :], by_expert(logits), X_AXIS, ALU.max))
                    yield
                    link.wait()
                    link.inc(nc.vector.tensor_tensor(by_expert(work2), by_expert(logits), over_experts(top), ALU.is_equal))
                    nc.vector.tensor_tensor(by_expert(work), by_expert(logits), over_experts(top), ALU.subtract).then_inc(S["gate_in"], 1)
                    yield
                    link.wait()
                    link.inc(nc.vector.tensor_tensor(by_expert(work2), by_expert(work2),
                                                     rank[:, :].unsqueeze(1).to_broadcast([P, BATCH * BANKS, E]), ALU.mult))
                if at == 1:
                    link.wait()
                    link.inc(nc.vector.tensor_reduce(key[:, :], by_expert(work2), X_AXIS, ALU.max))
                    yield
                    link.wait()
                    nc.vector.tensor_tensor(by_expert(chosen)[:, 0:BATCH * BANKS, :], rank[:, :].unsqueeze(1).to_broadcast([P, BATCH * BANKS, E]),
                                            over_experts(key), ALU.is_equal).then_inc(S["chosen"], 1)
                if at == 2:
                    need(dve, S["cum_out"], batch(i, k - 18) + 1)
                    link.inc(nc.vector.tensor_tensor(work2[:, :], counts[:, 0:BATCH * RE], chosen[:, 0:BATCH * RE], ALU.mult))
                    link.inc(nc.vector.tensor_copy(carry[:, :], counts[:, BATCH * RE:(BATCH + 1) * RE]))
                    yield
                    link.wait()
                    link.inc(nc.vector.tensor_scalar(key[:, :], key[:, :], -float(CAP), float(ROWS - 1), ALU.mult, ALU.add))
                    link.inc(nc.vector.tensor_reduce(place[:, :], by_expert(work2), X_AXIS, ALU.add))
                    yield
                    need(dve, S["gate_exp"], batch(i, k - 18) + 1)
                    link.inc(nc.vector.tensor_reduce(gate[:, :], by_expert(expo), X_AXIS, ALU.add))
                if at == 3:
                    link.wait()
                    link.inc(nc.vector.reciprocal(gate[:, :], gate[:, :]))
                    link.inc(nc.vector.tensor_scalar(over[:, :], place[:, :], CAP + 0.5, float(DROPPED), ALU.is_gt, ALU.mult))
                    yield
                    link.wait()
                    link.inc(nc.vector.scalar_tensor_tensor(slot[:, :], place[:, :], float(CAP), key[:, :], ALU.min, ALU.add))
                    c = tile(i, k - 19) * BANKS
                    link.inc(nc.vector.scalar_tensor_tensor(gates[:, bass.ds(c, BATCH * BANKS)], place[:, :], CAP + 0.5, gate[:, :],
                                                            ALU.is_lt, ALU.mult))
                    yield
                    link.wait()
                    link.inc(nc.vector.tensor_copy(slots[:, bass.ds(c, BATCH * BANKS)], slot[:, :]))
                    nc.vector.tensor_tensor(to_row[((k - 19) // BATCH) % 2][:, :], slot[:, :], over[:, :], ALU.add).then_inc(S["routed"], 1)

            pipelined(dve, step, BODY, FIRST, LAST, LEAD, END, link, VCHAIN)
            link.wait()



def feed_forward(nc, which, W1, b1, W2, b2, bs2, sent, answered, ident, h_sb, slots, gates, norm2, acc, out):
    routed = which < 2
    name = ("sp", "fq", "sh")[which]
    G = 2 * P
    EACH = ROWS // E // G if routed else B * N // G
    GROUPS = EACH * E if routed else EACH
    BODY, FIRST, LAST = (2 * EACH, 1, GROUPS // (2 * EACH) - 1) if routed else (4, 1, GROUPS // 4 - 1)
    RING = EACH if routed else 2
    LOADS = 64
    with ExitStack() as s:
        def sb(n, shape, dt=F32):
            return s.enter_context(nc.sbuf_tensor(f"{name}_{n}", shape, dt))

        def sem(n):
            return s.enter_context(nc.semaphore(f"{name}_{n}"))

        w1 = [sb(f"w1_{k}", [P, FF]) for k in range(2)]
        w1_hi = [sb(f"w1_hi{k}", [P, FF], F32R) for k in range(2)]
        w1_lo = [sb(f"w1_lo{k}", [P, FF], F32R) for k in range(2)]
        w2 = [sb(f"w2_{k}", [P, FC, D]) for k in range(2)]
        b1_c = [sb(f"b1_{k}", [P, FC]) for k in range(2)]
        b2_b = [sb(f"b2_{k}", [P, D]) for k in range(2)]
        rows = [sb(f"rows{k}", [P, 2, D]) for k in range(RING)]
        xT_hi = [sb(f"xT_hi{k}", [P, G], F32R) for k in range(2)]
        xT_lo = [sb(f"xT_lo{k}", [P, G], F32R) for k in range(2)]
        hid = [sb(f"hid{k}", [P, FC, G]) for k in range(2)]
        res = [sb(f"res{k}", [P, 2, D]) for k in range(2)]
        back = [sb(f"back{k}", [P, D]) for k in range(8)] if which else []
        back_i = [sb(f"back_i{k}", [P, 8], I32) for k in range(4)]
        part = [sb(f"part{k}", [P, 2, D]) for k in range(2)]
        ps_x = [s.enter_context(nc.psum_tensor(f"{name}_ps_x{k}", [P, 512], F32)) for k in range(2)]
        ps_h = [s.enter_context(nc.psum_tensor(f"{name}_ps_h{k}", [P, FC, G], F32)) for k in range(2)]
        ps_o = [s.enter_context(nc.psum_tensor(f"{name}_ps_o{k}", [P, 512], F32)) for k in range(2)]
        S = {n: sem(n) for n in ("w_hi", "w_lo", "rows", "turned", "xhi", "xlo", "up", "gelu", "down", "part",
                                 "out", "added", "index")}
        s_w = [sem(f"w{k}") for k in range(2)]
        s_in = [sem(f"in{k}") for k in range(RING)] if routed else []
        s_put = [sem(f"put{k}") for k in range(2)]
        s_back = [sem(f"back{k}") for k in range(8)] if which else []
        block = s.enter_context(nc.Block())

        def live(i, k):
            return not isinstance(i, int) or 0 <= BODY * i + k < GROUPS

        def group(i, k):
            return i * BODY + k

        def expert(i, k):
            return i * 2 + k // EACH if routed else 0

        def opens(k):
            return k % EACH == 0

        def side(w):
            return (w // EACH) % 2 if routed else 0

        def gathered(k):
            per = BODY * 2 if which == 2 else BODY * TILES // GROUPS
            return range(k * per // BODY, (k + 1) * per // BODY)

        def tile(i, t):
            return i * (BODY * TILES // GROUPS) + t

        def round_of(i, t, ring):
            return i * (BODY * TILES // GROUPS // ring) + t // ring

        def dram_rows(t, i, k):
            return t[bass.ds(group(i, k) * G, G), :].rearrange("(s p) d -> p s d", p=P)

        @block.sync
        def _(sp):
            if which == 0:
                sp.dma_start(part[0][:, 0, :], bs2.rearrange("(o d) -> o d", o=1).to_broadcast([P, D])).then_inc(S["index"], 16)

            def step(i, k):
                a = k + 4
                if opens(a) and live(i, a):
                    e, c = expert(i, a), side(a)
                    need(sp, S["w_lo"], e - 1)
                    need_apart(sp, S["down"], group(i, a) - EACH)
                    need_apart(sp, S["out"], group(i, a) - EACH)
                    src = [t[bass.ds(e, 1)] for t in (W1, b1, W2, b2)] if routed else [W1, b1, W2, b2]
                    if routed:
                        src = [src[0].rearrange("o d f -> (o d) f"), src[1].rearrange("o (c p) -> p (o c)", p=P),
                               src[2].rearrange("o (c p) d -> p (o c) d", p=P), src[3].to_broadcast([P, D])]
                    else:
                        src = [src[0], src[1].rearrange("(c p) -> p c", p=P), src[2].rearrange("(c p) d -> p c d", p=P),
                               src[3].rearrange("(o d) -> o d", o=1).to_broadcast([P, D])]
                    for dst, one in zip((w1[c][:, :], b1_c[c][:, :], w2[c][:, :, :], b2_b[c][:, :]), src):
                        sp.dma_start(dst, one, allow_slow_non_contiguous=True).then_inc(s_w[c], 16)
                if routed and live(i, k + 4):
                    need(sp, S["turned"], group(i, k + 4) - RING + 1)
                    sp.dma_start(rows[(k + 4) % RING][:, :, :],
                                 dram_rows(sent[which], i, k + 4)).then_inc(s_in[(k + 4) % RING], 16)
                if live(i, k - 1):
                    need(sp, S["out"], group(i, k))
                    dst = dram_rows(answered[which], i, k - 1) if routed else dram_rows(out, i, k - 1)
                    sp.dma_start(dst, res[(k - 1) % 2][:, :, :]).then_inc(s_put[(k - 1) % 2], 16)

            pipelined(sp, step, BODY, FIRST, LAST, 4, GROUPS + 2)
            for k in range(2):
                sp.wait_ge(s_put[k], 16 * GROUPS // 2)

        @block.tensor
        def _(pe):
            def step(i, k):
                if live(i, k + 1):
                    c = (k + 1) % 2
                    if routed:
                        pe.wait_ge(s_in[(k + 1) % RING], (i * (BODY // RING) + (k + 1) // RING + 1) * 16)
                    else:
                        need(pe, S["rows"], group(i, k + 1) + 1)
                    need(pe, S["xlo"], group(i, k))
                    for b in range(2):
                        mm = nc.tensor.transpose(ps_x[c][:, b * P:(b + 1) * P], rows[(k + 1) % RING][:, b, :], ident[:, :])
                    mm.then_inc(S["turned"], 1)
                if live(i, k):
                    c, w = k % 2, side(k)
                    need(pe, S["xlo"], group(i, k) + 1)
                    need(pe, S["w_lo"], expert(i, k) + 1)
                    need(pe, S["gelu"], group(i, k) - 1)
                    for f in range(FC):
                        hi, lo = w1_hi[w][:, f * P:(f + 1) * P], w1_lo[w][:, f * P:(f + 1) * P]
                        nc.tensor.matmul(ps_h[c][:, f, :], hi, xT_hi[c][:, :], start=True, stop=False)
                        nc.tensor.matmul(ps_h[c][:, f, :], lo, xT_hi[c][:, :], start=False, stop=False)
                        mm = nc.tensor.matmul(ps_h[c][:, f, :], hi, xT_lo[c][:, :], start=False, stop=True)
                    mm.then_inc(S["up"], 1)
                if live(i, k - 1):
                    c, w = (k - 1) % 2, side(k - 1)
                    need(pe, S["gelu"], group(i, k))
                    need(pe, S["out"], group(i, k) - 2)
                    for b in range(2):
                        for f in range(FC):
                            mm = nc.tensor.matmul(ps_o[c][:, b * D:(b + 1) * D], hid[c][:, f, b * P:(b + 1) * P],
                                                  w2[w][:, f, :], start=(f == 0), stop=(f == FC - 1))
                    mm.then_inc(S["down"], 1)

            pipelined(pe, step, BODY, FIRST, LAST, 4, GROUPS + 2)

        @block.scalar
        def _(act):
            def step(i, k):
                if live(i, k + 1):
                    c = (k + 1) % 2
                    need(act, S["turned"], group(i, k) + 2)
                    need(act, S["up"], group(i, k))
                    nc.scalar.activation(xT_hi[c][:, :], ps_x[c][:, 0:G], ACT.Copy).then_inc(S["xhi"], 1)
                if live(i, k):
                    c = k % 2
                    need(act, S["up"], group(i, k) + 1)
                    need(act, S["down"], group(i, k) - 1)
                    for f in range(FC):
                        ins = nc.scalar.activation(hid[c][:, f, :], ps_h[c][:, f, :], ACT.Gelu, bias=b1_c[side(k)][:, f:f + 1])
                    ins.then_inc(S["gelu"], 1)

            pipelined(act, step, BODY, FIRST, LAST, 4, GROUPS + 2)

        @block.vector
        def _(dve):
            def step(i, k):
                a = k + 2
                if opens(a) and live(i, a):
                    c = side(a)
                    e = expert(i, a)
                    dve.wait_ge(s_w[c], (i + a // EACH // 2 + 1) * LOADS if routed else LOADS)
                    need(dve, S["up"], group(i, a) - EACH)
                    nc.vector.tensor_copy(w1_hi[c][:, :], w1[c][:, :]).then_inc(S["w_hi"], 1)
                    dve.wait_ge(S["w_hi"], e + 1)
                    nc.vector.tensor_tensor(w1_lo[c][:, :], w1[c][:, :], w1_hi[c][:, :].bitcast(F32), ALU.subtract).then_inc(S["w_lo"], 1)
                if not routed and live(i, k + 2):
                    need(dve, S["turned"], group(i, k) + 1)
                    for b in range(2):
                        t = tile(i, 2 * (k + 2) + b)
                        ins = nc.vector.tensor_scalar(rows[k % 2][:, b, :], h_sb[:, bass.ds(t * D, D)],
                                                      norm2[:, bass.ds(t * 2, 1)], norm2[:, bass.ds(t * 2 + 1, 1)],
                                                      ALU.subtract, ALU.mult)
                    ins.then_inc(S["rows"], 1)
                if live(i, k + 1):
                    c = (k + 1) % 2
                    need(dve, S["xhi"], group(i, k) + 2)
                    nc.vector.tensor_tensor(xT_lo[c][:, :], ps_x[c][:, 0:G], xT_hi[c][:, :].bitcast(F32), ALU.subtract).then_inc(S["xlo"], 1)
                if which == 1 and live(i, k - 1):
                    for t in gathered(k - 1):
                        n = tile(i, t)
                        dve.wait_ge(s_back[t % 8], (round_of(i, t, 8) + 1) * 16)
                        a = acc[:, bass.ds(n * D, D)]
                        nc.vector.scalar_tensor_tensor(a, back[t % 8][:, :], gates[:, bass.ds(n * 2, 1)], a,
                                                       ALU.mult, ALU.add).then_inc(S["added"], 1)
                if live(i, k - 1):
                    c = (k - 1) % 2
                    if which == 2:
                        need(dve, S["out"], group(i, k) - 2)
                        for b in range(2):
                            t = 2 * (k - 1) + b
                            n = tile(i, t)
                            dve.wait_ge(s_back[t % 8], (round_of(i, t, 8) + 1) * 16)
                            ins = nc.vector.scalar_tensor_tensor(part[c][:, b, :], back[t % 8][:, :], gates[:, bass.ds(n * 2 + 1, 1)],
                                                                 acc[:, bass.ds(n * D, D)], ALU.mult, ALU.add)
                        ins.then_inc(S["part"], 1)
                    need(dve, S["down"], group(i, k))
                    need(dve, s_put[c], (i * (BODY // 2) + (k - 1) // 2) * 16)
                    if which == 2:
                        need(dve, S["part"], group(i, k))
                        plus = part[c][:, :, :]
                    else:
                        plus = b2_b[side(k - 1)][:, :].unsqueeze(1).to_broadcast([P, 2, D])
                    nc.vector.tensor_tensor(res[c][:, :, :], ps_o[c][:, 0:G].rearrange("p (b d) -> p b d", b=2), plus,
                                            ALU.add).then_inc(S["out"], 1)

            pipelined(dve, step, BODY, FIRST, LAST, 4, GROUPS + 2)

        @block.gpsimd
        def _(pool):
            if which == 0:
                pool.wait_ge(S["index"], 16)
                per = TILES // 16
                with pool.Fori(0, 16) as i:
                    at = bass.ds(i * (per * D), per * D)
                    nc.gpsimd.tensor_tensor(acc[:, at].rearrange("p (t d) -> p t d", t=per),
                                            h_sb[:, at].rearrange("p (t d) -> p t d", t=per),
                                            part[0][:, 0, :].unsqueeze(1).to_broadcast([P, per, D]), ALU.add).then_inc(S["added"], 1)
                pool.wait_ge(S["added"], 16)
                return
            bank = which - 1

            def step(i, k):
                a = k + (2 if which == 2 else 0)
                if not live(i, a):
                    return
                ts = gathered(a)
                c = a % (4 if which == 2 else 2)
                if which == 2:
                    need(pool, S["part"], group(i, a) - 3)
                else:
                    need(pool, S["added"], tile(i, gathered(k - 1)[0]))
                nc.gpsimd.tensor_copy(back_i[c][:, 0:2 * len(ts)], slots[:, bass.ds(tile(i, ts[0]) * 2, 2 * len(ts))]).then_inc(S["index"], 1)
                need_apart(pool, S["index"], group(i, a) + 1)
                for n, t in enumerate(ts):
                    if which == 1:
                        need_apart(pool, S["added"], tile(i, t) - 7)
                    nc.gpsimd.indirect_dma_start(back[t % 8][:, :], None, answered[bank],
                                                 bass.IndirectOffsetOnAxis(ap=back_i[c][:, 2 * n + bank:2 * n + bank + 1], axis=0)
                                                 ).then_inc(s_back[t % 8], 16)

            pipelined(pool, step, BODY, FIRST, LAST, 4, GROUPS + 2)



PCHAIN = 12
VCHAIN = 92

_INS = ["x", "L0_tok_weight", "L0_tok_num_value", "L0_tok_is_num", "L0_attn_Wq", "L0_attn_Wkv", "L0_attn_scale",
        "L0_attn_mix_pre", "L0_attn_mix_post", "L0_attn_Wout", "L0_attn_bout", "L0_ffn_Wr_sp", "L0_ffn_br_sp",
        "L0_ffn_Wr_fq", "L0_ffn_br_fq", "L0_ffn_Ws1", "L0_ffn_bs1", "L0_ffn_Ws2", "L0_ffn_bs2", "L0_ffn_W1_sp",
        "L0_ffn_b1_sp", "L0_ffn_W2_sp", "L0_ffn_b2_sp", "L0_ffn_W1_fq", "L0_ffn_b1_fq", "L0_ffn_W2_fq", "L0_ffn_b2_fq"]


def kernel(**inputs):
    import numpy as np
    import concourse.bacc as bacc
    from concourse.bass_utils import run_bass_kernel_spmd

    nc = bacc.Bacc("TRN2", target_bir_lowering=False, num_devices=1)
    arrays, args = {}, []
    for name in _INS:
        a = np.ascontiguousarray(inputs[name])
        arrays[f"in_{name}"] = a
        args.append(nc.dram_tensor(f"in_{name}", a.shape, mybir.dt.from_np(a.dtype), kind="ExternalInput").ap())
    out = nc.dram_tensor("out_0", (B, N, D), F32, kind="ExternalOutput").ap()
    build(nc, *args, out)
    r = run_bass_kernel_spmd(nc, [arrays], core_ids=[0])
    return r.results[0]["out_0"]
```

```python
from contextlib import ExitStack

import concourse.bass as bass
from concourse import mybir

F32 = mybir.dt.float32
F32R = mybir.dt.float32r
BF16 = mybir.dt.bfloat16
I32 = mybir.dt.int32
U8 = mybir.dt.uint8
ALU = mybir.AluOpType
ACT = mybir.ActivationFunctionType
X_AXIS = mybir.AxisListType.X

P = 128
VOCAB, D = 12500, 128
B, N = 128, 128
TILES = B * N // P
H, DH = 8, 64
HD = H * DH
HC = HD // P
E, FF = 8, 512
FC = FF // P
CAP = 1280
ROWS = E * CAP
BANKS = 2
RE = BANKS * E
EPS = 1e-5
MASK_VAL = -1e-9
TWO_PI_HI = 6.28125
TWO_PI_LO = 0.0019353071795864769
INV_TWO_PI = 0.15915494309189535
ROUND = 12582912.0
PI_BELOW = 3.1415925
HEAD = 8
ZERO_ROWS = 10
FILLS = ROWS // P // ZERO_ROWS
DROPPED = 1 << 20
GROUP = 2 * P
EACH = CAP // GROUP
RING = EACH
BATCH = 8
LATE = TILES - 2 * BATCH

VP = 125
VR = VOCAB // VP
VC = 10


def need(eng, sem, count, most=None):
    if isinstance(count, int):
        if most is not None:
            count = min(count, most)
        if count <= 0:
            return
    eng.wait_ge(sem, count)


def need_apart(eng, sem, count):
    need(eng, sem, count)
    if not isinstance(count, int):
        eng.nop(nofuse=True)


class Chain:

    def __init__(self, eng, sem):
        self.eng, self.sem, self.n, self.at = eng, sem, 0, None

    def inc(self, ins):
        self.n += 1
        ins.then_inc(self.sem, 1)

    def wait(self, apart=False):
        if self.at is None:
            self.eng.wait_ge(self.sem, self.n)
        else:
            i, first, per, before = self.at
            self.eng.wait_ge(self.sem, i * per + (self.n - first * per))
            if apart:
                self.eng.nop(nofuse=True)

    def __call__(self, ins):
        self.inc(ins)
        self.wait()

    def enter(self, i, first, per):
        self.at = (i, first, per, self.n)

    def leave(self, rounds):
        _, _, per, before = self.at
        assert self.n - before == per, (self.n - before, per)
        self.n = before + per * rounds
        self.at = None


def pipelined(eng, step, body, first, last, lead, end, chain=None, per=0):
    for t in range(-lead, first * body):
        step(0, t)
    with eng.Fori(first, last) as i:
        if chain:
            chain.enter(i, first, per)
        for k in range(body):
            step(i, k)
        if chain:
            chain.leave(last - first)
    for t in range(last * body, end):
        step(0, t)


def build(nc, x, weight, num_value, is_num, Wq, Wkv, scale, mix_pre, mix_post, Wout, bout,
          Wr_sp, br_sp, Wr_fq, br_fq, Ws1, bs1, Ws2, bs2,
          W1_sp, b1_sp, W2_sp, b2_sp, W1_fq, b1_fq, W2_fq, b2_fq, out):
    table = nc.dram_tensor("table", (VOCAB, D), F32).ap()
    sent = [nc.dram_tensor(f"sent_{b}", (ROWS, D), F32).ap() for b in ("sp", "fq")]
    answered = [nc.dram_tensor(f"answered_{b}", (ROWS, D), F32).ap() for b in ("sp", "fq")]
    with ExitStack() as whole:
        def keep(name, shape, dt=F32):
            return whole.enter_context(nc.sbuf_tensor(name, shape, dt))

        ident = keep("ident", [P, P])
        h_sb = keep("h_sb", [P, TILES * D])
        ids = keep("ids", [P, B], I32)
        slots = keep("slots", [P, TILES * BANKS], I32)
        gates = keep("gates", [P, TILES * BANKS])
        x2 = [keep(f"x2_{k}", [P, D]) for k in range(16)]
        to_row = [keep(f"to_row{k}", [P, BATCH * BANKS], I32) for k in range(2)]
        norm2 = keep("norm2", [P, TILES * 2])
        banks = ((W1_sp, b1_sp, W2_sp, b2_sp), (W1_fq, b1_fq, W2_fq, b2_fq), (Ws1, bs1, Ws2, bs2))
        first = ExpertSlot(keep, 0)
        first.loaded, first.s_hi, first.s_lo = (whole.enter_context(nc.semaphore(n)) for n in ("w_loaded", "w_hi", "w_lo"))
        with ExitStack() as s:
            zeros = s.enter_context(nc.sbuf_tensor("zeros", [P, ZERO_ROWS * D], F32))
            s_zeroed = s.enter_context(nc.semaphore("s_zeroed"))
            C = RouterConstants(lambda n, shape, dt=F32: s.enter_context(nc.sbuf_tensor(n, shape, dt)))
            mats = {n: s.enter_context(nc.sbuf_tensor(n, [P, H * D], F32R))
                    for n in ("M_hi", "M_lo", "N_hi", "N_lo")}
            masked = [s.enter_context(nc.sbuf_tensor(f"masked{k}", [P, H * N], F32)) for k in range(2)]
            off_diag = s.enter_context(nc.sbuf_tensor("off_diag", [P, N], I32))
            setup(nc, x, weight, num_value, is_num, Wq, Wkv, scale, mix_pre, mix_post, Wout,
                  bout, Wr_sp, br_sp, Wr_fq, br_fq, table, sent, ident, ids, mats, masked, off_diag, h_sb, zeros, C)
            attention(nc, banks[0], banks[2], first, C, table, sent, ident, h_sb, ids, slots,
                      gates, norm2, x2, to_row, mats, masked, off_diag, zeros, s_zeroed)
        acc = keep("acc", [P, TILES * D])
        rows = [keep(f"rows{k}", [P, 2, D]) for k in range(RING)]
        s_in = [whole.enter_context(nc.semaphore(f"in{k}")) for k in range(RING)]
        for which in range(3):
            feed_forward(nc, which, banks, first, bs2, sent, x2, to_row, answered, ident, h_sb, slots, gates, norm2, acc,
                         rows, s_in, out.rearrange("b n d -> (b n) d"))


class RouterConstants:

    def __init__(self, sb):
        self.power, self.var = sb("power", [P, 8]), sb("var", [P, 8])
        self.wr, self.br_b, self.bout_b = sb("wr", [P, RE]), sb("br_b", [P, RE]), sb("bout_b", [P, D])
        self.tri = sb("tri", [P, P], BF16)
        self.ones = sb("ones", [P, P], BF16)
        self.rank, self.rank_i = sb("rank", [P, E]), sb("rank_i", [P, E], I32)
        self.chosen = sb("chosen", [P, (BATCH + 1) * RE], BF16)
        self.carry = sb("carry", [P, RE])
        self.mv1 = [sb(f"mv1_{k}", [P, 4, 2]) for k in range(2)]
        self.mv2 = [sb(f"mv2_{k}", [P, 4, 2]) for k in range(2)]


class ExpertSlot:

    def __init__(self, sb, k):
        self.w1, self.w2 = sb(f"w1_{k}", [P, FF]), sb(f"w2_{k}", [P, FC, D])
        self.w1_hi, self.w1_lo = sb(f"w1_hi{k}", [P, FF], F32R), sb(f"w1_lo{k}", [P, FF], F32R)
        self.b1_c, self.b2_b = sb(f"b1_{k}", [P, FC]), sb(f"b2_{k}", [P, D])


def load_expert(sp, weights, e, slot, sem):
    W1, b1, W2, b2 = weights
    if len(W1.shape) == 3:
        W1, b1, W2, b2 = (t[bass.ds(e, 1)] for t in weights)
        src = (W1.rearrange("o d f -> (o d) f"), b1.rearrange("o (c p) -> p (o c)", p=P),
               W2.rearrange("o (c p) d -> p (o c) d", p=P), b2.to_broadcast([P, D]))
    else:
        src = (W1, b1.rearrange("(c p) -> p c", p=P), W2.rearrange("(c p) d -> p c d", p=P),
               b2.rearrange("(o d) -> o d", o=1).to_broadcast([P, D]))
    for dst, one in zip((slot.w1[:, :], slot.b1_c[:, :], slot.w2[:, :, :], slot.b2_b[:, :]), src):
        sp.dma_start(dst, one, allow_slow_non_contiguous=True).then_inc(sem, 16)


def split_expert(nc, dve, slot, s_hi, s_lo, count):
    nc.vector.tensor_copy(slot.w1_hi[:, :], slot.w1[:, :]).then_inc(s_hi, 1)
    dve.wait_ge(s_hi, count)
    nc.vector.tensor_tensor(slot.w1_lo[:, :], slot.w1[:, :], slot.w1_hi[:, :].bitcast(F32), ALU.subtract).then_inc(s_lo, 1)


def setup(nc, x, weight, num_value, is_num, Wq, Wkv, scale, mix_pre, mix_post, Wout,
          bout, Wr_sp, br_sp, Wr_fq, br_fq, table, sent, ident, ids, mats, masked, off_diag, h_sb, zeros, C):
    CH = VC * D
    CHUNKS = VR // VC
    with ExitStack() as s:
        def sb(name, shape, dt=F32):
            return s.enter_context(nc.sbuf_tensor(name, shape, dt))

        def sem(name):
            return s.enter_context(nc.semaphore(name))

        freq_i = sb("freq_i", [P, D], I32)
        freq = sb("freq", [P, D])
        num_i = sb("num_i", [VP, VR], I32)
        num_f = sb("num_f", [VP, VR])
        part = sb("part", [VP, 4, VR])
        isn = sb("isn", [VP, VR], U8)
        mask = sb("mask", [VP, VR], I32)
        angle = [sb(f"angle{k}", [VP, CH]) for k in range(3)]
        turns = [sb(f"turns{k}", [VP, CH]) for k in range(2)]
        sines = [sb(f"sines{k}", [VP, CH]) for k in range(2)]
        wq = sb("wq", [P, HD])
        wkv = sb("wkv", [P, 2 * HD])
        wkT = sb("wkT", [P, HC, P])
        wvT = sb("wvT", [P, HC, P])
        mix_src = sb("mix_src", [P, 2 * HC, P])
        mix_co = sb("mix_co", [P, 2 * HC, H])
        mixed = sb("mixed", [P, 2 * HC, H * D])
        pre = sb("pre", [H, H])
        spre = sb("spre", [H, H])
        sc = sb("sc", [H, 1])
        postT = sb("postT", [H, H])
        head_of = sb("head_of", [H, HD])
        minus = sb("minus", [H, P])
        diag = sb("diag", [P, H])
        idx_i = sb("idx_i", [P, N], I32)
        idx_f = sb("idx_f", [P, N])
        ps_t = [s.enter_context(nc.psum_tensor(f"ps_t{k}", [P, 512], F32)) for k in range(3)]
        ps_m = s.enter_context(nc.psum_tensor("ps_m", [P, H * D], F32))
        ps_n = s.enter_context(nc.psum_tensor("ps_n", [P, H * D], F32))
        ps_c = s.enter_context(nc.psum_tensor("ps_c", [P, 512], F32))
        s_num, s_small, s_put = sem("s_num"), sem("s_small"), sem("s_put")
        s_row = [sem(f"s_row{k}") for k in range(2)]
        s_const, s_freq, s_angle, s_reduced, s_clamped = (sem("s_const"), sem("s_freq"), sem("s_angle"), sem("s_reduced"),
                                                          sem("s_clamped"))
        s_sine, s_done, s_turn, s_mixed, s_M, s_hi = (sem("s_sine"), sem("s_done"), sem("s_turn"), sem("s_mixed"),
                                                      sem("s_M"), sem("s_hi"))
        s_coef, s_coefd, s_v, s_a = sem("s_coef"), sem("s_coefd"), sem("s_v"), sem("s_a")
        s_p, s_turned, s_rank, s_consts = sem("s_p"), sem("s_turned"), sem("s_rank"), sem("s_consts")
        w_t = weight.rearrange("(p r) d -> p (r d)", p=VP)
        t_t = table.rearrange("(p r) d -> p (r d)", p=VP)
        block = s.enter_context(nc.Block())

        def chunk(c):
            return slice(c * CH, (c + 1) * CH)

        @block.sync
        def _(sp):
            sp.dma_start(num_i[:, :], num_value.rearrange("(p r) -> p r", p=VP)).then_inc(s_num, 16)
            sp.dma_start(isn[:, :], is_num.rearrange("(p r) -> p r", p=VP)).then_inc(s_num, 16)
            for dst, src in ((idx_i[:, :], x), (wq[:, :], Wq), (wkv[:, :], Wkv),
                             (mix_src[:, HC:2 * HC, :], Wout.rearrange("(c p) n -> p c n", p=P)),
                             (pre[:, :], mix_pre), (postT[:, :], mix_post.rearrange("h g -> g h")),
                             (sc[:, :], scale.rearrange("(h o) -> h o", o=1))):
                sp.dma_start(dst, src, allow_slow_non_contiguous=True).then_inc(s_small, 16)
            for c in range(CHUNKS):
                need(sp, s_row[c % 2], 16 * (c // 2))
                sp.dma_start(h_sb[0:VP, chunk(c)], w_t[:, chunk(c)]).then_inc(s_row[c % 2], 16)
            for dst, src in ((C.wr[:, 0:E], Wr_sp), (C.wr[:, E:RE], Wr_fq),
                             (C.br_b[:, 0:E], br_sp.rearrange("(o e) -> o e", o=1).to_broadcast([P, E])),
                             (C.br_b[:, E:RE], br_fq.rearrange("(o e) -> o e", o=1).to_broadcast([P, E])),
                             (C.bout_b[:, :], bout.rearrange("(o e) -> o e", o=1).to_broadcast([P, D]))):
                sp.dma_start(dst, src).then_inc(s_consts, 16)
            sp.wait_ge(s_consts, 80)

        @block.gpsimd
        def _(pool):
            nc.gpsimd.iota(freq_i[:, :], [[1, D]], base=1, channel_multiplier=0).then_inc(s_freq, 1)
            nc.gpsimd.memset(ident[:, :], 0.0).then_inc(s_const, 1)
            nc.gpsimd.memset(off_diag[:, :], 1).then_inc(s_const, 1)
            nc.gpsimd.memset(head_of[:, :], 1.0).then_inc(s_const, 1)
            nc.gpsimd.memset(minus[:, :], MASK_VAL).then_inc(s_const, 1)
            pool.wait_ge(s_const, 4)
            nc.gpsimd.affine_select(out=ident[:, :], in_=ident[:, :], compare_op=ALU.not_equal, fill=1.0,
                                    base=0, pattern=[[-1, P]], channel_multiplier=1).then_inc(s_const, 1)
            nc.gpsimd.affine_select(out=off_diag[:, :], in_=off_diag[:, :], compare_op=ALU.not_equal, fill=0,
                                    base=0, pattern=[[-1, P]], channel_multiplier=1).then_inc(s_const, 1)
            nc.gpsimd.affine_select(out=head_of[:, :], in_=head_of[:, :], compare_op=ALU.is_ge, fill=0.0,
                                    base=0, pattern=[[1, HD]], channel_multiplier=-DH).then_inc(s_const, 1)
            pool.wait_ge(s_const, 7)
            nc.gpsimd.affine_select(out=head_of[:, :], in_=head_of[:, :], compare_op=ALU.is_ge, fill=0.0,
                                    base=DH - 1, pattern=[[-1, HD]], channel_multiplier=DH).then_inc(s_const, 1)

            link = Chain(pool, s_p)

            def make_angle(c):
                a, t = angle[c % 3][:, :], turns[c % 2][:, :]
                nc.gpsimd.tensor_tensor(a.rearrange("p (r d) -> p r d", r=VC),
                                        freq[0:VP, :].unsqueeze(1).to_broadcast([VP, VC, D]),
                                        num_f[:, c * VC:(c + 1) * VC].unsqueeze(2).to_broadcast([VP, VC, D]),
                                        ALU.mult).then_inc(s_angle, 1)
                need(pool, s_reduced, c - 1)
                pool.wait_ge(s_angle, c + 1)
                link(nc.gpsimd.tensor_scalar(t, a, INV_TWO_PI, ROUND, ALU.mult, ALU.add))
                nc.gpsimd.tensor_scalar(t, t, 1.0, -ROUND, ALU.mult, ALU.add).then_inc(s_turned, 1)

            pool.wait_ge(s_freq, 3)
            for c in range(CHUNKS):
                need(pool, s_sine, c - 2)
                make_angle(c)
                if c == 1:
                    link(nc.gpsimd.memset(zeros[:, :], 0.0))
            for t, value in ((C.power, -0.5), (C.ones, 1.0), (C.tri, 1.0), (C.carry, 0.0), (C.chosen, 0.0), (C.var, 1.0)):
                link.inc(nc.gpsimd.memset(t[:, :], value))
            for m in (*C.mv1, *C.mv2):
                link.inc(nc.gpsimd.memset(m[:, :, :], 1.0))
            link.wait()
            nc.gpsimd.iota(C.rank_i[:, :], [[-1, E]], base=E, channel_multiplier=0).then_inc(s_rank, 1)
            link(nc.gpsimd.affine_select(out=C.tri[:, :], in_=C.tri[:, :], compare_op=ALU.is_ge, fill=0.0,
                                         base=0, pattern=[[1, P]], channel_multiplier=-1))

        @block.scalar
        def _(act):
            link = Chain(act, s_a)
            act.wait_ge(s_turn, 1)
            link.inc(nc.scalar.activation(mix_src[:, 0:HC, :].rearrange("p c n -> p (c n)"), ps_t[0][:, :], ACT.Copy))
            link.inc(nc.scalar.activation(wkT[:, :, :].rearrange("p c n -> p (c n)"), ps_t[1][:, :], ACT.Copy))
            link.inc(nc.scalar.activation(wvT[:, :, :].rearrange("p c n -> p (c n)"), ps_t[2][:, :], ACT.Copy))
            act.wait_ge(s_coefd, 1)
            link(nc.scalar.activation(mix_co[:, :, :].rearrange("p c h -> p (c h)"), ps_c[:, 0:2 * HC * H], ACT.Copy))
            for c in range(CHUNKS):
                if c < 2 * HC:
                    for g in range(H):
                        ins = nc.scalar.activation(mixed[:, c, g * D:(g + 1) * D], mix_src[:, c, :], ACT.Copy,
                                                   scale=mix_co[:, c, g:g + 1])
                    ins.then_inc(s_mixed, 1)
                act.wait_ge(s_clamped, c + 1)
                need(act, s_done, c - 1)
                nc.scalar.activation(sines[c % 2][:, :], angle[c % 3][:, :], ACT.Sin).then_inc(s_sine, 1)
                if c:
                    act.wait_ge(s_done, c)
                    act.dma_start(t_t[:, chunk(c - 1)], h_sb[0:VP, chunk(c - 1)]).then_inc(s_put, 16)
                if c in (HC + 1, CHUNKS - 1):
                    w = int(c == CHUNKS - 1)
                    act.wait_ge(s_M, w + 1)
                    nc.scalar.activation(mats["MN"[w] + "_hi"][:, :], (ps_m, ps_n)[w][:, :], ACT.Copy).then_inc(s_hi, 1)
            act.wait_ge(s_done, CHUNKS)
            act.dma_start(t_t[:, chunk(CHUNKS - 1)], h_sb[0:VP, chunk(CHUNKS - 1)]).then_inc(s_put, 16)
            act.wait_ge(s_put, 16 * CHUNKS)

        @block.tensor
        def _(pe):
            pe.wait_ge(s_const, 8)
            pe.wait_ge(s_small, 112)
            for c in range(HC):
                nc.tensor.transpose(ps_t[0][:, c * P:(c + 1) * P], wq[:, c * P:(c + 1) * P], ident[:, :])
                nc.tensor.transpose(ps_t[1][:, c * P:(c + 1) * P], wkv[:, c * P:(c + 1) * P], ident[:, :])
                last = nc.tensor.transpose(ps_t[2][:, c * P:(c + 1) * P], wkv[:, HD + c * P:HD + (c + 1) * P], ident[:, :])
            last.then_inc(s_turn, 1)
            pe.wait_ge(s_coef, 1)
            for c in range(HC):
                head = head_of[:, c * P:(c + 1) * P]
                nc.tensor.matmul(ps_c[:, c * H:(c + 1) * H], head, spre[:, :], start=True, stop=True)
                nc.tensor.matmul(ps_c[:, (HC + c) * H:(HC + c + 1) * H], head, postT[:, :], start=True, stop=True)
            nc.tensor.matmul(ps_c[:, 128:128 + H], minus[:, :], pre[:, :], start=True, stop=True)
            nc.tensor.transpose(ps_c[:, 256:384], idx_f[:, :], ident[:, :]).then_inc(s_coefd, 1)
            for w, (lhs, ps) in enumerate(((wkT, ps_m), (wvT, ps_n))):
                for c in range(HC):
                    pe.wait_ge(s_mixed, w * HC + c + 1)
                    for half in range(2):
                        cols = slice(half * 512, (half + 1) * 512)
                        last = nc.tensor.matmul(ps[:, cols], lhs[:, c, :], mixed[:, w * HC + c, cols],
                                                start=(c == 0), stop=(c == HC - 1))
                last.then_inc(s_M, 1)

        @block.vector
        def _(dve):
            link = Chain(dve, s_v)
            dve.wait_ge(s_freq, 1)
            nc.vector.tensor_copy(freq[:, :], freq_i[:, :]).then_inc(s_freq, 1)
            dve.wait_ge(s_num, 32)
            value, q, hi, lo = (part[:, n, :] for n in range(4))
            link(nc.vector.tensor_copy(value, num_i[:, :]))
            link(nc.vector.tensor_scalar(q, value, 0.001, None, ALU.mult))
            link(nc.vector.tensor_scalar(hi, q, 4097.0, None, ALU.mult))
            link(nc.vector.tensor_tensor(lo, hi, q, ALU.subtract))
            link(nc.vector.tensor_tensor(hi, hi, lo, ALU.subtract))
            link(nc.vector.tensor_tensor(lo, q, hi, ALU.subtract))
            link(nc.vector.scalar_tensor_tensor(hi, hi, -1000.0, value, ALU.mult, ALU.add))
            link(nc.vector.scalar_tensor_tensor(lo, lo, -1000.0, hi, ALU.mult, ALU.add))
            nc.vector.scalar_tensor_tensor(num_f[:, :], lo, 0.001, q, ALU.mult, ALU.add).then_inc(s_freq, 1)
            link.inc(nc.vector.tensor_copy(mask[:, :], isn[:, :]))
            dve.wait_ge(s_small, 112)
            link.inc(nc.vector.tensor_copy(idx_f[:, :], idx_i[:, :]))
            link.wait()
            nc.vector.tensor_scalar(spre[:, :], pre[:, :], sc[:, 0:1], None, ALU.mult).then_inc(s_coef, 1)

            def put_sines(c):
                dve.wait_ge(s_row[c % 2], 16 * (c // 2 + 1))
                dve.wait_ge(s_sine, c + 1)
                nc.vector.copy_predicated(h_sb[0:VP, chunk(c)].rearrange("p (r d) -> p r d", r=VC),
                                          mask[:, c * VC:(c + 1) * VC].unsqueeze(2).to_broadcast([VP, VC, D]),
                                          sines[c % 2][:, :].rearrange("p (r d) -> p r d", r=VC)).then_inc(s_done, 1)

            for c in range(CHUNKS):
                a, t = angle[c % 3][:, :], turns[c % 2][:, :]
                dve.wait_ge(s_turned, c + 1)
                link(nc.vector.scalar_tensor_tensor(a, t, -TWO_PI_HI, a, ALU.mult, ALU.add))
                nc.vector.scalar_tensor_tensor(a, t, -TWO_PI_LO, a, ALU.mult, ALU.add).then_inc(s_reduced, 1)
                dve.wait_ge(s_reduced, c + 1)
                nc.vector.tensor_scalar(a, a, PI_BELOW, -PI_BELOW, ALU.min, ALU.max).then_inc(s_clamped, 1)
                if c:
                    put_sines(c - 1)
                if c == 1:
                    dve.wait_ge(s_coefd, 1)
                    link.inc(nc.vector.tensor_copy(ids[:, :], ps_c[:, 256:384]))
                    link(nc.vector.tensor_copy(diag[:, :], ps_c[:, 128:128 + H]))
                    for k in range(2):
                        link.inc(nc.vector.tensor_copy(masked[k][:, :].rearrange("p (g j) -> p g j", g=H),
                                                       diag[:, :].unsqueeze(2).to_broadcast([P, H, N])))
            put_sines(CHUNKS - 1)
            dve.wait_ge(s_hi, 2)
            for ps, m in ((ps_m, "M"), (ps_n, "N")):
                link.inc(nc.vector.tensor_tensor(mats[m + "_lo"][:, :], ps[:, :], mats[m + "_hi"][:, :].bitcast(F32), ALU.subtract))
            dve.wait_ge(s_rank, 1)
            link(nc.vector.tensor_copy(C.rank[:, :], C.rank_i[:, :]))


def send(nc, sent, x2, to_row, t, b, sem):
    c = (t % BATCH) * BANKS + b
    nc.gpsimd.indirect_dma_start(
        sent[b], bass.IndirectOffsetOnAxis(ap=to_row[(t // BATCH) % 2][:, c:c + 1], axis=0),
        x2[t % 16][:, :], None, bounds_check=ROWS - 1, oob_is_err=False).then_inc(sem, 16)


def attention(nc, bank, shared, first, C, table, sent, ident, h_sb, ids, slots, gates, norm2,
              x2, to_row, mats, masked, off_diag, zeros, s_zeroed):
    BODY, FIRST, LAST, LEAD, END = 16, 2, 7, 12, TILES + 20
    GROUPS, QUADS = TILES // 2, TILES // 4
    LOGIT_COL, CUM_COL = D, D + BATCH * RE
    with ExitStack() as s:
        def sb(name, shape, dt=F32):
            return s.enter_context(nc.sbuf_tensor(name, shape, dt))

        def pb(name, cols):
            return s.enter_context(nc.psum_tensor(name, [P, cols], F32))

        def sem(name):
            return s.enter_context(nc.semaphore(name))

        chosen, carry, rank, mv1, mv2, var = C.chosen, C.carry, C.rank, C.mv1, C.mv2, C.var
        got = [sb(f"got{k}", [P, D]) for k in range(8)]
        gi = [sb(f"gi{k}", [P, 4], I32) for k in range(2)]
        x1 = [sb(f"x1_{k}", [P, 2 * D]) for k in range(2)]
        xT_hi = sb("xT_hi", [P, 4, 2 * N], F32R)
        xT_lo = sb("xT_lo", [P, 4, 2 * N], F32R)
        w_hi = [sb(f"w_hi{k}", [P, 2, H, N], F32R) for k in range(2)]
        w_lo = [sb(f"w_lo{k}", [P, 2, H, N], F32R) for k in range(2)]
        nmax = [sb(f"nmax{k}", [P, H]) for k in range(2)]
        expd = [sb(f"expd{k}", [P, H * N]) for k in range(2)]
        total = [sb(f"total{k}", [P, H]) for k in range(4)]
        rtotal = [sb(f"rtotal{k}", [P, H]) for k in range(2)]
        prob = [sb(f"prob{k}", [P, H * N]) for k in range(2)]
        probT = [sb(f"probT{k}", [P, H * N]) for k in range(2)]
        u = [sb(f"u{k}", [P, H * D]) for k in range(2)]
        x2T = sb("x2T", [P, 4 * N])
        stat = [sb(f"stat{k}", [P, 6]) for k in range(8)]
        rstd = [sb(f"rstd{k}", [P, 8]) for k in range(2)]
        logits = sb("logits", [P, BATCH * RE])
        work = sb("work", [P, BATCH * RE])
        work2 = sb("work2", [P, BATCH * RE])
        expo = sb("expo", [P, BATCH * RE])
        counts = sb("counts", [P, (BATCH + 1) * RE])
        top = sb("top", [P, BATCH * BANKS])
        gate = sb("gate", [P, BATCH * BANKS])
        key = sb("key", [P, BATCH * BANKS])
        place = sb("place", [P, BATCH * BANKS])
        slot = sb("slot", [P, BATCH * BANKS])
        over = sb("over", [P, BATCH * BANKS])
        ps_s = pb("ps_s", H * N)
        ps_ut = pb("ps_ut", H * D)
        ps_w = [pb(f"ps_w{k}", 512) for k in range(2)]
        ps_x = pb("ps_x", 512)
        ps_o = pb("ps_o", 512)
        ws1, ws2, bs1_c = sb("ws1", [P, FF]), sb("ws2", [P, FC, D]), sb("bs1_c", [P, FC])
        ws1_hi, ws1_lo = w_hi[0][:, 0, 0:FC, :], w_lo[0][:, 0, 0:FC, :]
        AFTER = {132: (0,), 133: (1,), 134: (2,), 135: (3,), 136: (4,), 139: range(5, HEAD + 2)}
        names = ("head_w", "head_hi", "head_made", "head_turned", "head_xhi", "head_xlo", "head_up", "head_gelu",
                 "head_down", "head_out", "scored", "copied", "maxed", "expd", "rtot", "normed", "turned", "turn_out", "u_made", "u_out",
                 "pv", "h1", "w_made", "w_hi", "w_lo", "x_made", "x_turned", "xhi", "xlo", "stat1", "stat2",
                 "rstd", "x2", "x2_turned", "x2T", "logit", "logit_out", "chosen", "cum", "cum_out", "routed",
                 "gate_in", "gate_exp", "resid", "chain", "pchain")
        S = {n: sem("a_" + n) for n in names}
        s_got = [sem(f"a_got{k}") for k in range(8)]
        s_sent = [sem(f"a_sent{k}") for k in range(8)]
        block = s.enter_context(nc.Block())

        def live(i, k):
            return not isinstance(i, int) or 0 <= BODY * i + k < TILES

        def tile(i, k):
            return i * BODY + k

        def group(i, k):
            return i * (BODY // 2) + k // 2

        def head_stages(i, k):
            return AFTER.get(k, ()) if isinstance(i, int) else ()

        def hidden(t, f):
            return t[:, f * GROUP:(f + 1) * GROUP]

        def quad(i, k):
            return i * (BODY // 4) + k // 4

        def batch(i, k):
            return i * (BODY // BATCH) + k // BATCH

        def landed(i, k):
            return (i * (BODY // 8) + k // 8 + 1) * 16

        @block.sync
        def _(sp):
            load_expert(sp, bank, 0, first, first.loaded)
            W1, b1, W2, _ = shared
            for dst, src in ((ws1[:, :], W1), (ws2[:, :, :], W2.rearrange("(c p) d -> p c d", p=P)),
                             (bs1_c[:, :], b1.rearrange("(c p) -> p c", p=P))):
                sp.dma_start(dst, src, allow_slow_non_contiguous=True).then_inc(S["head_w"], 16)
            for b in range(BANKS):
                z_t = sent[b].rearrange("(p n r) d -> n p (r d)", p=P, r=ZERO_ROWS)
                for n in range(FILLS):
                    sp.wait_ge(S["scored"], b * FILLS + n + 1)
                    sp.dma_start(z_t[n], zeros[:, :]).then_inc(s_zeroed, 16)

        @block.gpsimd
        def _(pool):
            link = Chain(pool, S["pchain"])
            def step(i, k):
                j = k % 4
                if live(i, k - 2):
                    need(pool, S["rtot"], tile(i, k - 1))
                    need(pool, S["turned"], tile(i, k - 3))
                    nc.gpsimd.tensor_tensor(prob[k % 2][:, :].rearrange("p (g j) -> p g j", g=H),
                                            expd[k % 2][:, :].rearrange("p (g j) -> p g j", g=H),
                                            rtotal[k % 2][:, :].unsqueeze(2).to_broadcast([P, H, N]),
                                            ALU.mult).then_inc(S["normed"], 1)
                if live(i, k + 10):
                    if (k + 10) % 4 == 0:
                        q = quad(i, k + 10)
                        if (not isinstance(i, int)) or q >= 2:
                            for b in range(4):
                                pool.wait_ge(s_got[(k + 10 + b) % 8], landed(i, k + 2 + b))
                        link(nc.gpsimd.tensor_copy(gi[((k + 10) // 4) % 2][:, :], ids[:, bass.ds(tile(i, k + 10), 4)]))
                    need(pool, S["x_made"], group(i, k + 2) + 1)
                    need_apart(pool, S["resid"], tile(i, k + 3))
                    nc.gpsimd.indirect_dma_start(
                        got[(k + 10) % 8][:, :], None, table,
                        bass.IndirectOffsetOnAxis(ap=gi[((k + 10) // 4) % 2][:, (k + 10) % 4:(k + 10) % 4 + 1], axis=0),
                    ).then_inc(s_got[(k + 10) % 8], 16)
                if live(i, k + 7):
                    pool.wait_ge(s_got[(k + 7) % 8], landed(i, k + 7))
                    nc.gpsimd.tensor_tensor(h_sb[:, bass.ds(tile(i, k + 7) * D, D)], got[(k + 7) % 8][:, :],
                                            C.bout_b[:, :], ALU.add).then_inc(S["resid"], 1)
                if j == 0 and (live(i, k + 4) or live(i, k - 8)):
                    if live(i, k + 4):
                        need(pool, S["stat1"], quad(i, k + 4) + 1)
                    if live(i, k - 8):
                        need(pool, S["stat2"], quad(i, k - 8) + 1)
                    need(pool, S["x_made"], group(i, k), GROUPS)
                    need(pool, S["x2"], group(i, k - 12), GROUPS)
                    if not isinstance(i, int):
                        pool.nop(nofuse=True)
                    m1, m2 = mv1[(k // 4 + 1) % 2], mv2[(k // 4) % 2]
                    link.inc(nc.gpsimd.tensor_scalar(var[:, 0:4], m1[:, :, 1], 1.0, EPS, ALU.mult, ALU.add))
                    link(nc.gpsimd.tensor_scalar(var[:, 4:8], m2[:, :, 1], 1.0, EPS, ALU.mult, ALU.add))
                    nc.gpsimd.tensor_tensor(rstd[(k // 4) % 2][:, :], var[:, :], C.power[:, :], ALU.pow).then_inc(S["rstd"], 1)
                if live(i, k - 20):
                    t = k - 20
                    if isinstance(i, int) and t == 0:
                        pool.wait_ge(s_zeroed, 16 * BANKS * FILLS)
                    need_apart(pool, S["routed"], batch(i, t) + 1)
                    late = isinstance(i, int) and tile(i, t) >= LATE
                    for b in range(1 if late else BANKS):
                        send(nc, sent, x2, to_row, t, b, s_sent[t // 2 % 8])

            pipelined(pool, step, BODY, FIRST, LAST, LEAD, END, link, PCHAIN)
            for k in range(8):
                pool.wait_ge(s_sent[k], TILES // 16 * 64 - 32)

        @block.tensor
        def _(pe):
            def step(i, k):
                j = k % 4
                if j == 0 and live(i, k - 12):
                    need(pe, S["x2T"], quad(i, k - 12) + 1)
                    need(pe, S["h1"], tile(i, k - 4), TILES)
                    for b in range(4):
                        c = LOGIT_COL + ((k - 12) % BATCH + b) * RE
                        mm = nc.tensor.matmul(ps_o[:, c:c + RE], x2T[:, b * N:(b + 1) * N], C.wr[:, :], start=True, stop=True)
                    mm.then_inc(S["logit"], 1)
                if k % BATCH == 2 and live(i, k - 18):
                    need(pe, S["chosen"], batch(i, k - 18) + 1)
                    need(pe, S["h1"], tile(i, k - 4), TILES)
                    end = CUM_COL + (BATCH + 1) * RE
                    nc.tensor.matmul(ps_o[:, CUM_COL:end], C.tri[:, :], chosen[:, :], start=True, stop=False)
                    for d in range(1, BATCH + 1):
                        mm = nc.tensor.matmul(ps_o[:, CUM_COL + d * RE:end], C.ones[:, :], chosen[:, 0:(BATCH + 1 - d) * RE],
                                              start=False, stop=(d == BATCH))
                    mm.then_inc(S["cum"], 1)
                if live(i, k):
                    m, b = k // 2, k % 2
                    need(pe, S["copied"], tile(i, k))
                    need(pe, S["w_lo"], group(i, k) * 4 + 4)
                    cols = slice(b * N, (b + 1) * N)
                    hi, lo = xT_hi[:, m % 4, cols], xT_lo[:, m % 4, cols]
                    for n, (lhs, rhs) in enumerate(((hi, w_hi), (hi, w_lo), (lo, w_hi))):
                        r = rhs[m % 2][:, b, :, :].rearrange("p g j -> p (g j)")
                        for half in range(2):
                            mm = nc.tensor.matmul(ps_s[:, half * 512:(half + 1) * 512], lhs,
                                                  r[:, half * 512:(half + 1) * 512], start=(n == 0), stop=(n == 2))
                    mm.then_inc(S["scored"], 1)
                if live(i, k - 3):
                    need(pe, S["normed"], tile(i, k - 2))
                    need(pe, S["u_out"], tile(i, k - 3))
                    for g in range(H):
                        mm = nc.tensor.transpose(ps_ut[:, g * N:(g + 1) * N], prob[(k - 3) % 2][:, g * N:(g + 1) * N], ident[:, :])
                    mm.then_inc(S["turned"], 1)
                if k % 2 and live(i, k + 3):
                    m = group(i, k + 3)
                    need(pe, S["x_made"], m + 1)
                    need(pe, S["xlo"], m)
                    need(pe, S["x2T"], quad(i, k - 11) + 1, QUADS)
                    for b in range(2):
                        mm = nc.tensor.transpose(ps_x[:, b * N:(b + 1) * N], x1[((k + 3) // 2) % 2][:, b * D:(b + 1) * D], ident[:, :])
                    mm.then_inc(S["x_turned"], 1)
                if live(i, 2 * (k // 2 + 1)):
                    m = k // 2 + 1
                    need(pe, S["xlo"], group(i, 2 * m) + 1)
                    for q in (2 * (k % 2), 2 * (k % 2) + 1):
                        need(pe, S["w_lo"], group(i, 2 * m) * 4 + q - 1)
                        for g in (2 * q, 2 * q + 1):
                            o = ps_w[q % 2][:, (g % 2) * 256:(g % 2 + 1) * 256]
                            M_hi, M_lo = (mats[n][:, g * D:(g + 1) * D] for n in ("M_hi", "M_lo"))
                            nc.tensor.matmul(o, M_hi, xT_hi[:, m % 4, :], start=True, stop=False)
                            nc.tensor.matmul(o, M_lo, xT_hi[:, m % 4, :], start=False, stop=False)
                            mm = nc.tensor.matmul(o, M_hi, xT_lo[:, m % 4, :], start=False, stop=True)
                        mm.then_inc(S["w_made"], 1)
                if live(i, k - 4):
                    need(pe, S["turn_out"], tile(i, k - 3))
                    need(pe, S["u_out"], tile(i, k - 3))
                    need(pe, S["h1"], tile(i, k - 4))
                    if j == 0 and live(i, k - 12):
                        need(pe, S["logit_out"], quad(i, k - 12) + 1)
                    if k % BATCH == 2 and live(i, k - 18):
                        need(pe, S["cum_out"], batch(i, k - 18) + 1)
                    for g in range(H):
                        mm = nc.tensor.matmul(ps_o[:, 0:D], probT[k % 2][:, g * N:(g + 1) * N],
                                              u[k % 2][:, g * D:(g + 1) * D], start=(g == 0), stop=(g == H - 1))
                    mm.then_inc(S["pv"], 1)
                if live(i, k - 3):
                    m, b = (k - 3) // 2, (k - 3) % 2
                    need(pe, S["turn_out"], tile(i, k - 2))
                    cols = slice(b * N, (b + 1) * N)
                    hi, lo = xT_hi[:, m % 4, cols], xT_lo[:, m % 4, cols]
                    for n, (lhs, rhs) in enumerate(((hi, "N_hi"), (hi, "N_lo"), (lo, "N_hi"))):
                        for half in range(2):
                            mm = nc.tensor.matmul(ps_ut[:, half * 512:(half + 1) * 512], lhs,
                                                  mats[rhs][:, half * 512:(half + 1) * 512], start=(n == 0), stop=(n == 2))
                    mm.then_inc(S["u_made"], 1)
                if j == 2 and live(i, k - 10):
                    need(pe, S["x2"], group(i, k - 10) + 2)
                    need(pe, S["xlo"], group(i, k + 2) + 1, GROUPS)
                    for b in range(4):
                        mm = nc.tensor.transpose(ps_x[:, b * N:(b + 1) * N], x2[(k - 10 + b) % 16][:, :], ident[:, :])
                    mm.then_inc(S["x2_turned"], 1)
                for n in head_stages(i, k):
                    if n < HEAD:
                        pe.wait_ge(S["head_made"], n + 1)
                        need(pe, S["head_xlo"], n - 1)
                        need(pe, S["u_out"], TILES)
                        for b in range(2):
                            c = (n % 2) * 512 + b * P
                            mm = nc.tensor.transpose(ps_ut[:, c:c + P], x1[n % 2][:, b * D:(b + 1) * D], ident[:, :])
                        mm.then_inc(S["head_turned"], 1)
                    if 0 <= n - 1 < HEAD:
                        m = n - 1
                        pe.wait_ge(S["head_xlo"], m + 1)
                        pe.wait_ge(S["copied"], TILES)
                        need(pe, S["head_gelu"], m)
                        for f in range(FC):
                            h = hidden(ps_s, f)
                            nc.tensor.matmul(h, ws1_hi[:, f, :], xT_hi[:, m % 4, :], start=True, stop=False)
                            nc.tensor.matmul(h, ws1_lo[:, f, :], xT_hi[:, m % 4, :], start=False, stop=False)
                            mm = nc.tensor.matmul(h, ws1_hi[:, f, :], xT_lo[:, m % 4, :], start=False, stop=True)
                        mm.then_inc(S["head_up"], 1)
                    if 0 <= n - 2 < HEAD:
                        m = n - 2
                        pe.wait_ge(S["head_gelu"], m + 1)
                        need(pe, S["head_out"], m - 1)
                        for b in range(2):
                            for f in range(FC):
                                mm = nc.tensor.matmul(ps_w[m % 2][:, b * D:(b + 1) * D], hidden(expd[m % 2], f)[:, b * P:(b + 1) * P],
                                                      ws2[:, f, :], start=(f == 0), stop=(f == FC - 1))
                        mm.then_inc(S["head_down"], 1)

            pipelined(pe, step, BODY, FIRST, LAST, LEAD, END)

        @block.scalar
        def _(act):
            def step(i, k):
                j = k % 4

                def exps(heads):
                    for g in heads:
                        ins = nc.scalar.activation(expd[(k - 1) % 2][:, g * N:(g + 1) * N],
                                                   masked[(k - 1) % 2][:, g * N:(g + 1) * N], ACT.Exp,
                                                   bias=nmax[(k - 1) % 2][:, g:g + 1],
                                                   accum_out=total[(k - 1) % 4][:, g:g + 1])
                    return ins

                if live(i, k - 4):
                    need(act, S["u_made"], tile(i, k - 3))
                    need(act, S["pv"], tile(i, k - 5))
                    nc.scalar.activation(u[k % 2][:, :], ps_ut[:, :], ACT.Copy).then_inc(S["u_out"], 1)
                if j == 3 and live(i, k - 11):
                    q = quad(i, k - 11)
                    need(act, S["x2_turned"], q + 1)
                    need(act, S["logit"], q)
                    nc.scalar.activation(x2T[:, :], ps_x[:, :], ACT.Copy).then_inc(S["x2T"], 1)
                if live(i, k - 1):
                    need(act, S["maxed"], tile(i, k))
                    need(act, S["normed"], tile(i, k - 2))
                    exps(range(0, 3))
                if live(i, k - 3):
                    need(act, S["turned"], tile(i, k - 2))
                    need(act, S["pv"], tile(i, k - 4))
                    nc.scalar.activation(probT[(k - 3) % 2][:, :], ps_ut[:, :], ACT.Copy).then_inc(S["turn_out"], 1)
                if live(i, 2 * (k // 2 + 1)):
                    m = k // 2 + 1
                    for q in (2 * (k % 2), 2 * (k % 2) + 1):
                        need(act, S["w_made"], group(i, 2 * m) * 4 + q + 1)
                        need(act, S["scored"], tile(i, 2 * m) - 2)
                        nc.scalar.activation(w_hi[m % 2][:, :, 2 * q:2 * q + 2, :].rearrange("p b g j -> p g b j"),
                                             ps_w[q % 2][:, :].rearrange("p (g b j) -> p g b j", g=2, b=2),
                                             ACT.Copy).then_inc(S["w_hi"], 1)
                if k % 2 and live(i, k + 3):
                    m = group(i, k + 3)
                    need(act, S["x_turned"], m + 1)
                    need(act, S["u_made"], tile(i, k + 3) - 6)
                    nc.scalar.activation(xT_hi[:, ((k + 3) // 2) % 4, :], ps_x[:, 0:2 * N], ACT.Copy).then_inc(S["xhi"], 1)
                if live(i, k - 1):
                    exps(range(3, 8)).then_inc(S["expd"], 1)
                if k % BATCH == 1 and live(i, k - 17):
                    need(act, S["gate_in"], batch(i, k - 17) + 1)
                    nc.scalar.activation(expo[:, :], work[:, :], ACT.Exp).then_inc(S["gate_exp"], 1)
                for n in head_stages(i, k):
                    if n < HEAD:
                        act.wait_ge(S["head_turned"], n + 1)
                        need(act, S["head_up"], n - 3)
                        nc.scalar.activation(xT_hi[:, n % 4, :], ps_ut[:, (n % 2) * 512:(n % 2) * 512 + GROUP],
                                             ACT.Copy).then_inc(S["head_xhi"], 1)
                    if 0 <= n - 1 < HEAD:
                        m = n - 1
                        act.wait_ge(S["head_up"], m + 1)
                        act.wait_ge(S["normed"], TILES)
                        need(act, S["head_down"], m - 1)
                        for f in range(FC):
                            ins = nc.scalar.activation(hidden(expd[m % 2], f), hidden(ps_s, f), ACT.Gelu, bias=bs1_c[:, f:f + 1])
                        ins.then_inc(S["head_gelu"], 1)

            pipelined(act, step, BODY, FIRST, LAST, LEAD, END)

        @block.vector
        def _(dve):
            link = Chain(dve, S["chain"])

            def by_expert(t):
                return t[:, :].rearrange("p (n e) -> p n e", e=E)

            def over_experts(t):
                return t[:, :].unsqueeze(2).to_broadcast([P, BATCH * BANKS, E])

            def step(i, k):
                j = k % 4
                if live(i, k - 2):
                    need(dve, S["expd"], tile(i, k - 1))
                    need(dve, S["normed"], tile(i, k - 3))
                    nc.vector.reciprocal(rtotal[k % 2][:, :], total[(k - 2) % 4][:, :]).then_inc(S["rtot"], 1)
                if j == 0 and live(i, k - 12):
                    c = (k - 12) % BATCH * RE
                    need(dve, S["logit"], quad(i, k - 12) + 1)
                    nc.vector.tensor_tensor(logits[:, c:c + 4 * RE].rearrange("p (t e) -> p t e", t=4),
                                            ps_o[:, LOGIT_COL + c:LOGIT_COL + c + 4 * RE].rearrange("p (t e) -> p t e", t=4),
                                            C.br_b[:, :].unsqueeze(1).to_broadcast([P, 4, RE]), ALU.add).then_inc(S["logit_out"], 1)
                if k % BATCH == 2 and live(i, k - 18):
                    need(dve, S["cum"], batch(i, k - 18) + 1)
                    nc.vector.tensor_tensor(counts[:, :].rearrange("p (t e) -> p t e", e=RE),
                                            ps_o[:, CUM_COL:CUM_COL + (BATCH + 1) * RE].rearrange("p (t e) -> p t e", e=RE),
                                            carry[:, :].unsqueeze(1).to_broadcast([P, BATCH + 1, RE]), ALU.add).then_inc(S["cum_out"], 1)
                route = iter(router(i, k))
                if live(i, k):
                    need(dve, S["scored"], tile(i, k + 1))
                    need_apart(dve, S["expd"], tile(i, k - 1))
                    nc.vector.copy_predicated(masked[k % 2][:, :].rearrange("p (g j) -> p g j", g=H),
                                              off_diag[:, :].unsqueeze(1).to_broadcast([P, H, N]),
                                              ps_s[:, :].rearrange("p (g j) -> p g j", g=H)).then_inc(S["copied"], 1)
                next(route, None)
                if live(i, k):
                    need(dve, S["copied"], tile(i, k + 1))
                    nc.vector.tensor_reduce(nmax[k % 2][:, :], masked[k % 2][:, :].rearrange("p (g j) -> p g j", g=H),
                                            X_AXIS, ALU.max, negate=True).then_inc(S["maxed"], 1)
                next(route, None)
                if live(i, 2 * (k // 2 + 1)):
                    m = k // 2 + 1
                    for q in (2 * (k % 2), 2 * (k % 2) + 1):
                        need(dve, S["w_hi"], group(i, 2 * m) * 4 + q + 1)
                        dst, hi = (w[m % 2][:, :, 2 * q:2 * q + 2, :].rearrange("p b g j -> p g b j") for w in (w_lo, w_hi))
                        nc.vector.tensor_tensor(dst, ps_w[q % 2][:, :].rearrange("p (g b j) -> p g b j", g=2, b=2),
                                                hi.bitcast(F32), ALU.subtract).then_inc(S["w_lo"], 1)
                next(route, None)
                if j in (1, 2) and live(i, k - 8 - (j == 1)):
                    t0 = k - 8 - (j == 1)
                    if j == 1:
                        need(dve, S["rstd"], quad(i, k) + 2)
                    need(dve, s_sent[t0 // 2 % 8], i * 64 + t0 // 16 * 64)
                    for b in range(2):
                        t = t0 + b
                        a = ((t // 4) % 2, t % 4)
                        mean, rs = mv2[a[0]][:, a[1], 0:1], rstd[a[0]][:, 4 + a[1]:5 + a[1]]
                        ins = nc.vector.tensor_scalar(x2[t % 16][:, :], h_sb[:, bass.ds(tile(i, t) * D, D)], mean, rs,
                                                      ALU.subtract, ALU.mult)
                    ins.then_inc(S["x2"], 1)
                    if j == 2:
                        n2 = norm2[:, bass.ds(tile(i, k - 10) * 2, 8)].rearrange("p (t c) -> p t c", c=2)
                        a = ((k - 10) // 4) % 2
                        link.inc(nc.vector.tensor_copy(n2[:, :, 0], mv2[a][:, :, 0]))
                        link.inc(nc.vector.tensor_copy(n2[:, :, 1], rstd[a][:, 4:8]))
                if k % 2 == 0 and live(i, k + 4):
                    need(dve, S["rstd"], quad(i, k) + 2)
                    need(dve, S["x_turned"], group(i, k + 2))
                    for b in range(2):
                        t = k + 4 + b
                        a = ((t // 4) % 2, t % 4)
                        mean, rs = mv1[a[0]][:, a[1], 0:1], rstd[(t // 4 - 1) % 2][:, a[1]:a[1] + 1]
                        ins = nc.vector.tensor_scalar(x1[((k + 4) // 2) % 2][:, b * D:(b + 1) * D], got[t % 8][:, :], mean, rs,
                                                      ALU.subtract, ALU.mult)
                    ins.then_inc(S["x_made"], 1)
                if live(i, k + 8):
                    dve.wait_ge(s_got[k % 8], landed(i, k + 8))
                    link.inc(nc.vector.bn_stats(stat[j][:, :], got[k % 8][:, :]))
                if live(i, k - 4):
                    hk = h_sb[:, bass.ds(tile(i, k - 4) * D, D)]
                    need(dve, S["pv"], tile(i, k - 3))
                    need(dve, S["resid"], tile(i, k - 3))
                    nc.vector.tensor_tensor(hk, ps_o[:, 0:D], hk, ALU.add).then_inc(S["h1"], 1)
                if live(i, k + 8):
                    link.wait(apart=True)
                    ins = nc.vector.bn_aggr(mv1[((k + 8) // 4) % 2][:, k % 4, :], stat[j][:, :])
                    if j == 3:
                        ins.then_inc(S["stat1"], 1)
                    else:
                        link.inc(ins)
                if live(i, k - 4):
                    need_apart(dve, S["h1"], tile(i, k - 3))
                    link.inc(nc.vector.bn_stats(stat[4 + j][:, :], hk))
                if k % 2 and live(i, k + 3):
                    need(dve, S["xhi"], group(i, k + 3) + 1)
                    c = ((k + 3) // 2) % 4
                    nc.vector.tensor_tensor(xT_lo[:, c, :], ps_x[:, 0:2 * N], xT_hi[:, c, :].bitcast(F32), ALU.subtract).then_inc(S["xlo"], 1)
                if live(i, k - 4):
                    link.wait(apart=True)
                    ins = nc.vector.bn_aggr(mv2[((k - 4) // 4) % 2][:, k % 4, :], stat[4 + j][:, :])
                    if j == 3:
                        ins.then_inc(S["stat2"], 1)
                    else:
                        link.inc(ins)
                for _ in route:
                    pass

                def head_norm(n):
                    need(dve, S["head_turned"], n - 1)
                    for b in range(2):
                        t = 2 * n + b
                        ins = nc.vector.tensor_scalar(x1[n % 2][:, b * D:(b + 1) * D], h_sb[:, t * D:(t + 1) * D],
                                                      norm2[:, 2 * t:2 * t + 1], norm2[:, 2 * t + 1:2 * t + 2],
                                                      ALU.subtract, ALU.mult)
                    ins.then_inc(S["head_made"], 1)

                if isinstance(i, int) and k == TILES:
                    dve.wait_ge(first.loaded, 64)
                    split_expert(nc, dve, first, first.s_hi, first.s_lo, 1)
                for n in head_stages(i, k):
                    if n == 0:
                        dve.wait_ge(S["scored"], TILES)
                        dve.wait_ge(S["head_w"], 48)
                        w = ws1[:, :].rearrange("p (f c) -> p f c", f=FC)
                        nc.vector.tensor_copy(ws1_hi, w).then_inc(S["head_hi"], 1)
                        head_norm(0)
                        dve.wait_ge(S["head_hi"], 1)
                        link.inc(nc.vector.tensor_tensor(ws1_lo, w, ws1_hi.bitcast(F32), ALU.subtract))
                    if n + 1 < HEAD:
                        head_norm(n + 1)
                    if n < HEAD:
                        dve.wait_ge(S["head_xhi"], n + 1)
                        nc.vector.tensor_tensor(xT_lo[:, n % 4, :], ps_ut[:, (n % 2) * 512:(n % 2) * 512 + GROUP],
                                                xT_hi[:, n % 4, :].bitcast(F32), ALU.subtract).then_inc(S["head_xlo"], 1)
                    if 0 <= n - 2 < HEAD:
                        m = n - 2
                        h = h_sb[:, m * GROUP:(m + 1) * GROUP]
                        dve.wait_ge(S["head_down"], m + 1)
                        nc.vector.tensor_tensor(h, ps_w[m % 2][:, 0:GROUP], h, ALU.add).then_inc(S["head_out"], 1)

            def router(i, k):
                at = k % BATCH
                if not live(i, k - 16 - at):
                    return
                if at == 0:
                    need(dve, S["logit_out"], quad(i, k - 12) + 1)
                    link.inc(nc.vector.tensor_reduce(top[:, :], by_expert(logits), X_AXIS, ALU.max))
                    yield
                    link.wait()
                    link.inc(nc.vector.tensor_tensor(by_expert(work2), by_expert(logits), over_experts(top), ALU.is_equal))
                    nc.vector.tensor_tensor(by_expert(work), by_expert(logits), over_experts(top), ALU.subtract).then_inc(S["gate_in"], 1)
                    yield
                    link.wait()
                    link.inc(nc.vector.tensor_tensor(by_expert(work2), by_expert(work2),
                                                     rank[:, :].unsqueeze(1).to_broadcast([P, BATCH * BANKS, E]), ALU.mult))
                if at == 1:
                    link.wait()
                    link.inc(nc.vector.tensor_reduce(key[:, :], by_expert(work2), X_AXIS, ALU.max))
                    yield
                    link.wait()
                    nc.vector.tensor_tensor(by_expert(chosen)[:, 0:BATCH * BANKS, :], rank[:, :].unsqueeze(1).to_broadcast([P, BATCH * BANKS, E]),
                                            over_experts(key), ALU.is_equal).then_inc(S["chosen"], 1)
                if at == 2:
                    need(dve, S["cum_out"], batch(i, k - 18) + 1)
                    link.inc(nc.vector.tensor_tensor(work2[:, :], counts[:, 0:BATCH * RE], chosen[:, 0:BATCH * RE], ALU.mult))
                    link.inc(nc.vector.tensor_copy(carry[:, :], counts[:, BATCH * RE:(BATCH + 1) * RE]))
                    yield
                    link.wait()
                    link.inc(nc.vector.tensor_scalar(key[:, :], key[:, :], -float(CAP), float(ROWS - 1), ALU.mult, ALU.add))
                    link.inc(nc.vector.tensor_reduce(place[:, :], by_expert(work2), X_AXIS, ALU.add))
                    yield
                    need(dve, S["gate_exp"], batch(i, k - 18) + 1)
                    link.inc(nc.vector.tensor_reduce(gate[:, :], by_expert(expo), X_AXIS, ALU.add))
                if at == 3:
                    link.wait()
                    link.inc(nc.vector.reciprocal(gate[:, :], gate[:, :]))
                    link.inc(nc.vector.tensor_scalar(over[:, :], place[:, :], CAP + 0.5, float(DROPPED), ALU.is_gt, ALU.mult))
                    yield
                    link.wait()
                    link.inc(nc.vector.scalar_tensor_tensor(slot[:, :], place[:, :], float(CAP), key[:, :], ALU.min, ALU.add))
                    c = tile(i, k - 19) * BANKS
                    link.inc(nc.vector.scalar_tensor_tensor(gates[:, bass.ds(c, BATCH * BANKS)], place[:, :], CAP + 0.5, gate[:, :],
                                                            ALU.is_lt, ALU.mult))
                    yield
                    link.wait()
                    link.inc(nc.vector.tensor_copy(slots[:, bass.ds(c, BATCH * BANKS)], slot[:, :]))
                    nc.vector.tensor_tensor(to_row[((k - 19) // BATCH) % 2][:, :], slot[:, :], over[:, :], ALU.add).then_inc(S["routed"], 1)

            pipelined(dve, step, BODY, FIRST, LAST, LEAD, END, link, VCHAIN)
            link.wait()



def feed_forward(nc, which, banks, first, bs2, sent, x2, to_row, answered, ident, h_sb, slots, gates, norm2, acc,
                 rows, s_in, out):
    routed = which < 2
    name = ("sp", "fq", "sh")[which]
    G = GROUP
    GROUPS = EACH * E if routed else B * N // G - HEAD
    BODY, FIRST, LAST = (2 * EACH, 1, GROUPS // (2 * EACH) - 1) if routed else (4, 1, GROUPS // 4 - 1)
    PER = BODY * TILES // GROUPS if routed else 2 * BODY
    LOADS = 64
    BEFORE = which * E
    INDICES = 4 if which == 2 else 2
    with ExitStack() as s:
        def sb(n, shape, dt=F32):
            return s.enter_context(nc.sbuf_tensor(f"{name}_{n}", shape, dt))

        def sem(n):
            return s.enter_context(nc.semaphore(f"{name}_{n}"))

        slot = [first, ExpertSlot(sb, 1) if routed else None]
        xT_hi = [sb(f"xT_hi{k}", [P, G], F32R) for k in range(2)]
        xT_lo = [sb(f"xT_lo{k}", [P, G], F32R) for k in range(2)]
        hid = [sb(f"hid{k}", [P, FC, G]) for k in range(2)]
        res = [sb(f"res{k}", [P, 2, D]) for k in range(2)]
        back = [sb(f"back{k}", [P, D]) for k in range(8)] if which else []
        back_i = [sb(f"back_i{k}", [P, 8], I32) for k in range(INDICES)]
        part = [sb(f"part{k}", [P, 2, D]) for k in range(2)]
        ps_x = [s.enter_context(nc.psum_tensor(f"{name}_ps_x{k}", [P, 512], F32)) for k in range(2)]
        ps_h = [s.enter_context(nc.psum_tensor(f"{name}_ps_h{k}", [P, FC, G], F32)) for k in range(2)]
        ps_o = [s.enter_context(nc.psum_tensor(f"{name}_ps_o{k}", [P, 512], F32)) for k in range(2)]
        S = {n: sem(n) for n in ("turned", "xhi", "xlo", "up", "gelu", "down", "out")}
        S.update({n: sem(n) for n in (("index", "added", "late"), ("index", "added"), ("index", "rows", "part"))[which]})
        S["w_hi"], S["w_lo"] = first.s_hi, first.s_lo
        s_w = [first.loaded, sem("loaded") if routed else None]
        s_put = [sem(f"put{k}") for k in range(2)]
        s_back = [sem(f"back{k}") for k in range(8)] if which else []
        if which == 2:
            one_i, one_back, one_out = sb("one_i", [P, 1], I32), sb("one_back", [P, D]), sb("one_out", [P, D])
            for n in ("one_index", "one_back", "one_out", "one_put"):
                S[n] = sem(n)
        block = s.enter_context(nc.Block())

        def live(i, k):
            return not isinstance(i, int) or 0 <= BODY * i + k < GROUPS

        def group(i, k):
            return i * BODY + k

        def expert(i, k):
            return i * 2 + k // EACH if routed else 0

        def opens(k):
            return k % EACH == 0

        def side(w):
            return (w // EACH) % 2 if routed else 0

        def opening(i, a):
            return routed and opens(a) and (not isinstance(i, int) or 0 < BODY * i + a <= GROUPS)

        def loads(i, a):
            return (i + a // (2 * EACH) + 1 + (which * E // 2 if side(a) == 0 else 0)) * LOADS

        def gathered(k):
            return range(k * PER // BODY, (k + 1) * PER // BODY)

        def tile(i, t):
            return i * PER + t + (0 if routed else 2 * HEAD)

        def round_of(i, t, ring):
            return i * (PER // ring) + t // ring

        def head_tile(i, k):
            if which < 2:
                return None
            if isinstance(i, int) and k in (-3, -1, 1):
                return (2 * HEAD - 2, 2 * HEAD - 1, 0)[(k + 3) // 2], (k + 3) // 2
            if k % 4 != 1 or not live(i, k):
                return None
            return i + k // 4, i + k // 4 + 2

        def dram_rows(t, i, k):
            return t[bass.ds((group(i, k) + (0 if routed else HEAD)) * G, G), :].rearrange("(s p) d -> p s d", p=P)

        @block.sync
        def _(sp):
            if which == 0:
                sp.dma_start(part[0][:, 0, :], bs2.rearrange("(o d) -> o d", o=1).to_broadcast([P, D])).then_inc(S["index"], 16)

            def step(i, k):
                a = k + 4
                if opening(i, a):
                    need(sp, S["w_lo"], expert(i, a) - 1 + BEFORE)
                    need_apart(sp, S["down"], group(i, a) - EACH)
                    need_apart(sp, S["out"], group(i, a) - EACH)
                    if isinstance(i, int) and group(i, a) == GROUPS:
                        load_expert(sp, banks[which + 1], 0, slot[0], s_w[0])
                    else:
                        load_expert(sp, banks[which], expert(i, a), slot[side(a)], s_w[side(a)])
                if routed and live(i, a) and not (which == 1 and isinstance(i, int) and group(i, a) < 4):
                    need(sp, S["turned"], group(i, a) - RING + 1)
                    sp.dma_start(rows[a % RING][:, :, :], dram_rows(sent[which], i, a)).then_inc(s_in[a % RING], 16)
                if which == 0 and isinstance(i, int) and 0 <= group(i, a) - GROUPS < 4:
                    sp.wait_ge(S["turned"], group(i, a) - RING + 1)
                    sp.wait_ge(S["late"], 16 * (TILES - LATE))
                    sp.dma_start(rows[a % RING][:, :, :], dram_rows(sent[1], i, a - GROUPS)).then_inc(s_in[a % RING], 16)
                if live(i, k - 1):
                    need(sp, S["out"], group(i, k))
                    dst = dram_rows(answered[which], i, k - 1) if routed else dram_rows(out, i, k - 1)
                    sp.dma_start(dst, res[(k - 1) % 2][:, :, :]).then_inc(s_put[(k - 1) % 2], 16)
                if head_tile(i, k - 3):
                    t, n = head_tile(i, k - 3)
                    need(sp, S["one_out"], n + 1)
                    sp.dma_start(out[bass.ds(t * P, P), :], one_out[:, :]).then_inc(S["one_put"], 16)

            pipelined(sp, step, BODY, FIRST, LAST, 4, GROUPS + 2)
            for k in range(2):
                sp.wait_ge(s_put[k], 16 * GROUPS // 2)
            if which == 2:
                sp.wait_ge(S["one_put"], 16 * 2 * HEAD)

        @block.tensor
        def _(pe):
            def step(i, k):
                if live(i, k + 1):
                    c = (k + 1) % 2
                    if routed:
                        pe.wait_ge(s_in[(k + 1) % RING], (i * (BODY // RING) + (k + 1) // RING + 1 + which * GROUPS // RING) * 16)
                    else:
                        need(pe, S["rows"], group(i, k + 1) + 1)
                    need(pe, S["xlo"], group(i, k))
                    for b in range(2):
                        mm = nc.tensor.transpose(ps_x[c][:, b * P:(b + 1) * P], rows[(k + 1) % (RING if routed else 2)][:, b, :], ident[:, :])
                    mm.then_inc(S["turned"], 1)
                if live(i, k):
                    c, w = k % 2, side(k)
                    need(pe, S["xlo"], group(i, k) + 1)
                    need(pe, S["w_lo"], expert(i, k) + 1 + BEFORE)
                    need(pe, S["gelu"], group(i, k) - 1)
                    for f in range(FC):
                        hi, lo = slot[w].w1_hi[:, f * P:(f + 1) * P], slot[w].w1_lo[:, f * P:(f + 1) * P]
                        nc.tensor.matmul(ps_h[c][:, f, :], hi, xT_hi[c][:, :], start=True, stop=False)
                        nc.tensor.matmul(ps_h[c][:, f, :], lo, xT_hi[c][:, :], start=False, stop=False)
                        mm = nc.tensor.matmul(ps_h[c][:, f, :], hi, xT_lo[c][:, :], start=False, stop=True)
                    mm.then_inc(S["up"], 1)
                if live(i, k - 1):
                    c, w = (k - 1) % 2, side(k - 1)
                    need(pe, S["gelu"], group(i, k))
                    need(pe, S["out"], group(i, k) - 2)
                    for b in range(2):
                        for f in range(FC):
                            mm = nc.tensor.matmul(ps_o[c][:, b * D:(b + 1) * D], hid[c][:, f, b * P:(b + 1) * P],
                                                  slot[w].w2[:, f, :], start=(f == 0), stop=(f == FC - 1))
                    mm.then_inc(S["down"], 1)

            pipelined(pe, step, BODY, FIRST, LAST, 4, GROUPS + 2)

        @block.scalar
        def _(act):
            def step(i, k):
                if live(i, k + 1):
                    c = (k + 1) % 2
                    need(act, S["turned"], group(i, k) + 2)
                    need(act, S["up"], group(i, k))
                    nc.scalar.activation(xT_hi[c][:, :], ps_x[c][:, 0:G], ACT.Copy).then_inc(S["xhi"], 1)
                if live(i, k):
                    c = k % 2
                    need(act, S["up"], group(i, k) + 1)
                    need(act, S["down"], group(i, k) - 1)
                    for f in range(FC):
                        ins = nc.scalar.activation(hid[c][:, f, :], ps_h[c][:, f, :], ACT.Gelu, bias=slot[side(k)].b1_c[:, f:f + 1])
                    ins.then_inc(S["gelu"], 1)

            pipelined(act, step, BODY, FIRST, LAST, 4, GROUPS + 2)

        @block.vector
        def _(dve):
            def step(i, k):
                a = k + 2
                if opening(i, a):
                    dve.wait_ge(s_w[side(a)], loads(i, a))
                    need(dve, S["up"], group(i, a) - EACH)
                    split_expert(nc, dve, slot[side(a)], S["w_hi"], S["w_lo"], expert(i, a) + 1 + BEFORE)
                if not routed and live(i, k + 2):
                    need(dve, S["turned"], group(i, k) + 1)
                    for b in range(2):
                        t = tile(i, 2 * (k + 2) + b)
                        ins = nc.vector.tensor_scalar(rows[k % 2][:, b, :], h_sb[:, bass.ds(t * D, D)],
                                                      norm2[:, bass.ds(t * 2, 1)], norm2[:, bass.ds(t * 2 + 1, 1)],
                                                      ALU.subtract, ALU.mult)
                    ins.then_inc(S["rows"], 1)
                if live(i, k + 1):
                    c = (k + 1) % 2
                    need(dve, S["xhi"], group(i, k) + 2)
                    nc.vector.tensor_tensor(xT_lo[c][:, :], ps_x[c][:, 0:G], xT_hi[c][:, :].bitcast(F32), ALU.subtract).then_inc(S["xlo"], 1)
                if which == 1 and live(i, k - 1):
                    for t in gathered(k - 1):
                        n = tile(i, t)
                        dve.wait_ge(s_back[t % 8], (round_of(i, t, 8) + 1) * 16)
                        a = acc[:, bass.ds(n * D, D)]
                        nc.vector.scalar_tensor_tensor(a, back[t % 8][:, :], gates[:, bass.ds(n * 2, 1)], a,
                                                       ALU.mult, ALU.add).then_inc(S["added"], 1)
                if live(i, k - 1):
                    c = (k - 1) % 2
                    if which == 2:
                        need(dve, S["out"], group(i, k) - 2)
                        for b in range(2):
                            t = 2 * (k - 1) + b
                            n = tile(i, t)
                            dve.wait_ge(s_back[t % 8], (round_of(i, t, 8) + 1) * 16)
                            ins = nc.vector.scalar_tensor_tensor(part[c][:, b, :], back[t % 8][:, :], gates[:, bass.ds(n * 2 + 1, 1)],
                                                                 acc[:, bass.ds(n * D, D)], ALU.mult, ALU.add)
                        ins.then_inc(S["part"], 1)
                    need(dve, S["down"], group(i, k))
                    need(dve, s_put[c], (i * (BODY // 2) + (k - 1) // 2) * 16)
                    if which == 2:
                        need(dve, S["part"], group(i, k))
                        plus = part[c][:, :, :]
                    else:
                        plus = slot[side(k - 1)].b2_b[:, :].unsqueeze(1).to_broadcast([P, 2, D])
                    nc.vector.tensor_tensor(res[c][:, :, :], ps_o[c][:, 0:G].rearrange("p (b d) -> p b d", b=2), plus,
                                            ALU.add).then_inc(S["out"], 1)

                if head_tile(i, k - 2):
                    t, n = head_tile(i, k - 2)
                    dve.wait_ge(S["one_back"], (n + 1) * 16)
                    need(dve, S["one_put"], n * 16)
                    nc.vector.scalar_tensor_tensor(one_out[:, :], one_back[:, :], gates[:, bass.ds(t * 2 + 1, 1)],
                                                   acc[:, bass.ds(t * D, D)], ALU.mult, ALU.add).then_inc(S["one_out"], 1)
                if head_tile(i, k):
                    t, n = head_tile(i, k)
                    need(dve, S["one_out"], n)
                    nc.vector.tensor_copy(one_i[:, :], slots[:, bass.ds(t * 2 + 1, 1)]).then_inc(S["one_index"], 1)
                a = k + (3 if which == 2 else 1)
                if which and live(i, a):
                    ts = gathered(a)
                    nc.vector.tensor_copy(back_i[a % INDICES][:, 0:2 * len(ts)],
                                          slots[:, bass.ds(tile(i, ts[0]) * 2, 2 * len(ts))]).then_inc(S["index"], 1)

            pipelined(dve, step, BODY, FIRST, LAST, 4, GROUPS + 2)

        @block.gpsimd
        def _(pool):
            if which == 0:
                pool.wait_ge(S["index"], 16)
                per = TILES // 16
                with pool.Fori(0, 16) as i:
                    at = bass.ds(i * (per * D), per * D)
                    nc.gpsimd.tensor_tensor(acc[:, at].rearrange("p (t d) -> p t d", t=per),
                                            h_sb[:, at].rearrange("p (t d) -> p t d", t=per),
                                            part[0][:, 0, :].unsqueeze(1).to_broadcast([P, per, D]), ALU.add).then_inc(S["added"], 1)
                for t in range(LATE, TILES):
                    send(nc, sent, x2, to_row, t, 1, S["late"])
                pool.wait_ge(S["added"], 16)
                pool.wait_ge(S["late"], 16 * (TILES - LATE))
                return
            bank = which - 1

            def step(i, k):
                if head_tile(i, k):
                    _, n = head_tile(i, k)
                    need_apart(pool, S["one_index"], n + 1)
                    nc.gpsimd.indirect_dma_start(one_back[:, :], None, answered[bank],
                                                 bass.IndirectOffsetOnAxis(ap=one_i[:, 0:1], axis=0)).then_inc(S["one_back"], 16)
                a = k + (2 if which == 2 else 0)
                if not live(i, a):
                    return
                ts = gathered(a)
                c = a % INDICES
                need_apart(pool, S["index"], group(i, a) + 1)
                for n, t in enumerate(ts):
                    nc.gpsimd.indirect_dma_start(back[t % 8][:, :], None, answered[bank],
                                                 bass.IndirectOffsetOnAxis(ap=back_i[c][:, 2 * n + bank:2 * n + bank + 1], axis=0)
                                                 ).then_inc(s_back[t % 8], 16)

            pipelined(pool, step, BODY, FIRST, LAST, 4, GROUPS + 2)



PCHAIN = 12
VCHAIN = 92

_INS = ["x", "L0_tok_weight", "L0_tok_num_value", "L0_tok_is_num", "L0_attn_Wq", "L0_attn_Wkv", "L0_attn_scale",
        "L0_attn_mix_pre", "L0_attn_mix_post", "L0_attn_Wout", "L0_attn_bout", "L0_ffn_Wr_sp", "L0_ffn_br_sp",
        "L0_ffn_Wr_fq", "L0_ffn_br_fq", "L0_ffn_Ws1", "L0_ffn_bs1", "L0_ffn_Ws2", "L0_ffn_bs2", "L0_ffn_W1_sp",
        "L0_ffn_b1_sp", "L0_ffn_W2_sp", "L0_ffn_b2_sp", "L0_ffn_W1_fq", "L0_ffn_b1_fq", "L0_ffn_W2_fq", "L0_ffn_b2_fq"]


def kernel(**inputs):
    import numpy as np
    import concourse.bacc as bacc
    from concourse.bass_utils import run_bass_kernel_spmd

    nc = bacc.Bacc("TRN2", target_bir_lowering=False, num_devices=1)
    arrays, args = {}, []
    for name in _INS:
        a = np.ascontiguousarray(inputs[name])
        arrays[f"in_{name}"] = a
        args.append(nc.dram_tensor(f"in_{name}", a.shape, mybir.dt.from_np(a.dtype), kind="ExternalInput").ap())
    out = nc.dram_tensor("out_0", (B, N, D), F32, kind="ExternalOutput").ap()
    build(nc, *args, out)
    r = run_bass_kernel_spmd(nc, [arrays], core_ids=[0])
    return r.results[0]["out_0"]
```
